# Optimizing a Trainium2 kernel written in Bass

```python
import numpy as np
import jax
import jax.numpy as jnp

def _softmax(x, axis=-1):
    return jax.nn.softmax(x, axis=axis)

def _gelu(x):
    return jax.nn.gelu(x, approximate=True)

def _silu(x):
    return jax.nn.silu(x)

def _sigmoid(x):
    return jax.nn.sigmoid(x)

def _layernorm(x, axis=-1, eps=1e-05):
    m = jnp.mean(x, axis=axis, keepdims=True)
    v = jnp.var(x, axis=axis, keepdims=True)
    return (x - m) / jnp.sqrt(v + eps)

def _scatter_add(tgt, idx, src, axis=0):
    return tgt.at[idx].add(src)

def _segment_sum(src, seg, n):
    return jax.ops.segment_sum(src, seg, n)
kernel_name = 'mk_gnn_preln_d4_gnn_r32_f04e7c'

def setup_inputs(seed: int=0):
    np.random.seed(seed)
    _w = jnp.asarray

    def _rec_inputs():
        import jax
        import jax.numpy as jnp
        _gk = jax.random.key(seed)
        x = -0.0003713 + 1 * jax.random.normal(jax.random.fold_in(_gk, 1), (3125, 256), jnp.float32)
        src = jax.random.randint(jax.random.fold_in(_gk, 2), (50000,), 0, 3125, jnp.int32)
        dst = jax.random.randint(jax.random.fold_in(_gk, 3), (50000,), 0, 3125, jnp.int32)
        _o = jnp.argsort(dst, stable=True)
        src = src[_o]
        dst = dst[_o]
        edge_attr_64 = -9.77346e-05 + 0.999888 * jax.random.normal(jax.random.fold_in(_gk, 12), (50000, 64), jnp.float32)
        edge_type_8 = jax.random.randint(jax.random.fold_in(_gk, 14), (50000,), 0, 8, jnp.int32)
        edge_weight = jax.random.uniform(jax.random.fold_in(_gk, 15), (50000,), jnp.float32, 0.0, 1)
        return (x, src, dst, edge_attr_64, edge_type_8, edge_weight)
    x, src, dst, edge_attr_64, edge_type_8, edge_weight = _rec_inputs()

    def _L0_gnn_setup():
        import jax, jax.numpy as jnp
        import numpy as np
        N_NODES = 50000
        N_EDGES = 25000
        IN_FEAT = 256
        OUT_FEAT = 256
        NUM_RELS = 8
        ALPHA = 0.5
        key = jax.random.key(seed)
        k1, k2, k3, k4, k5, k6 = jax.random.split(key, 6)
        x = jax.random.normal(k1, (N_NODES, IN_FEAT), dtype=jnp.float32)
        edge_index = jax.random.randint(k2, (2, N_EDGES), 0, N_NODES, dtype=jnp.int64)
        edge_type = jax.random.randint(k3, (N_EDGES,), 0, NUM_RELS, dtype=jnp.int64)
        gain = float(np.sqrt(2.0))
        lim_w = gain * float(np.sqrt(6.0 / (IN_FEAT + OUT_FEAT)))
        weight = jax.random.uniform(k4, (NUM_RELS, IN_FEAT, OUT_FEAT), dtype=jnp.float32, minval=-lim_w, maxval=lim_w)
        loop_weight = jax.random.uniform(k5, (IN_FEAT, OUT_FEAT), dtype=jnp.float32, minval=-lim_w, maxval=lim_w)
        h_bias = jnp.zeros((OUT_FEAT,), dtype=jnp.float32)
        return {'edge_index': edge_index, 'x': x, 'edge_type': edge_type, 'weight': weight, 'h_bias': h_bias, 'loop_weight': loop_weight}
    _L0_gnn_all = _L0_gnn_setup()
    _L0_gnn_in = {k: v for k, v in _L0_gnn_all.items() if k in ('weight', 'h_bias', 'loop_weight')}
    del _L0_gnn_all

    def _L1_gnn_setup():
        import jax, jax.numpy as jnp
        import numpy as np
        N_NODES = 10000
        N_EDGES = 10000
        IN_F, HID_F, OUT_F = (256, 512, 256)

        def _glorot(key, shape):
            lim = np.sqrt(6.0 / (shape[0] + shape[1]))
            return jax.random.uniform(key, shape, jnp.float32, -lim, lim)

        def _sage_mean(h, src, dst, n, deg, W_self, W_neigh, b):
            msum = jax.ops.segment_sum(h[src], dst, num_segments=n)
            h_neigh = msum / jnp.clip(deg, 1.0)[:, None]
            return h @ W_self + h_neigh @ W_neigh + b

        def _sage_pool(h, src, dst, n, deg, W_pool, b_pool, W_self, W_neigh, b):
            hp = jax.nn.relu(h @ W_pool + b_pool)
            hmax = jax.ops.segment_max(hp[src], dst, num_segments=n)
            hmax = jnp.where(deg[:, None] > 0, hmax, 0.0)
            return h @ W_self + hmax @ W_neigh + b

        def _sage_gcn(h, src, dst, n, deg, W_neigh, b):
            msum = jax.ops.segment_sum(h[src], dst, num_segments=n)
            h_neigh = (msum + h) / (deg + 1.0)[:, None]
            return h_neigh @ W_neigh + b
        key = jax.random.key(seed)
        ks = jax.random.split(key, 16)
        inp = {'features': jax.random.normal(ks[0], (N_NODES, IN_F), jnp.float32), 'edge_src': jax.random.randint(ks[1], (N_EDGES,), 0, N_NODES, jnp.int32), 'edge_dst': jax.random.randint(ks[2], (N_EDGES,), 0, N_NODES, jnp.int32), 'W1_self': _glorot(ks[3], (IN_F, HID_F)), 'W1_neigh': _glorot(ks[4], (IN_F, HID_F)), 'b1': jnp.zeros((HID_F,), jnp.float32), 'W2_pool': _glorot(ks[5], (HID_F, HID_F)), 'b2_pool': jnp.zeros((HID_F,), jnp.float32), 'W2_self': _glorot(ks[6], (HID_F, HID_F)), 'W2_neigh': _glorot(ks[7], (HID_F, HID_F)), 'b2': jnp.zeros((HID_F,), jnp.float32), 'W3_neigh': _glorot(ks[8], (HID_F, HID_F)), 'b3': jnp.zeros((HID_F,), jnp.float32), 'W4_self': _glorot(ks[9], (HID_F, HID_F)), 'W4_neigh': _glorot(ks[10], (HID_F, HID_F)), 'b4': jnp.zeros((HID_F,), jnp.float32), 'W_fc': _glorot(ks[11], (HID_F, OUT_F)), 'b_fc': jnp.zeros((OUT_F,), jnp.float32)}
        return inp
    _L1_gnn_all = _L1_gnn_setup()
    _L1_gnn_in = {k: v for k, v in _L1_gnn_all.items() if k in ('W1_self', 'W1_neigh', 'b1', 'W2_pool', 'b2_pool', 'W2_self', 'W2_neigh', 'b2', 'W3_neigh', 'b3', 'W4_self', 'W4_neigh', 'b4', 'W_fc', 'b_fc')}
    del _L1_gnn_all

    def _L2_gnn_setup():
        import jax, jax.numpy as jnp
        import numpy as np
        N_NODES = 3125
        N_EDGES = 100000
        D_IN = 256
        D_OUT = 256
        key = jax.random.key(seed)
        k1, k2, k3, k4, k5 = jax.random.split(key, 5)
        inputs = jax.random.normal(k1, (N_NODES, D_IN), dtype=jnp.float32)
        init_range = np.sqrt(6.0 / (D_IN + D_OUT)).astype(np.float32)
        weight = jax.random.uniform(k2, (D_IN, D_OUT), dtype=jnp.float32, minval=-init_range, maxval=init_range)
        edge_src = jax.random.randint(k3, (N_EDGES,), 0, N_NODES, dtype=jnp.int32)
        edge_dst = jax.random.randint(k4, (N_EDGES,), 0, N_NODES, dtype=jnp.int32)
        edge_vals = jax.random.uniform(k5, (N_EDGES,), dtype=jnp.float32)
        return {'inputs': inputs, 'weight': weight, 'edge_src': edge_src, 'edge_dst': edge_dst, 'edge_vals': edge_vals}
    _L2_gnn_all = _L2_gnn_setup()
    _L2_gnn_in = {k: v for k, v in _L2_gnn_all.items() if k in ('weight',)}
    del _L2_gnn_all

    def _L3_gnn_setup():
        import jax, jax.numpy as jnp
        import numpy as np
        N_NODES = 50000
        key = jax.random.key(seed)
        k1, k2, k3, k4, k5 = jax.random.split(key, 5)
        N, E, F_IN, F_E, F_OUT = (N_NODES, 25000, 256, 64, 256)
        feat = jax.random.normal(k1, (N, F_IN), dtype=jnp.float32)
        edge_feat = jax.random.normal(k2, (E, F_E), dtype=jnp.float32)
        limit = float(np.sqrt(6.0 / (F_IN + F_E + F_OUT)))
        weight = jax.random.uniform(k3, (F_IN + F_E, F_OUT), minval=-limit, maxval=limit, dtype=jnp.float32)
        bias = jnp.zeros((F_OUT,), dtype=jnp.float32)
        src = jax.random.randint(k4, (E,), 0, N, dtype=jnp.int32)
        dst = jax.random.randint(k5, (E,), 0, N, dtype=jnp.int32)
        return {'feat': feat, 'edge_feat': edge_feat, 'weight': weight, 'bias': bias, 'src': src, 'dst': dst}
    _L3_gnn_all = _L3_gnn_setup()
    _L3_gnn_in = {k: v for k, v in _L3_gnn_all.items() if k in ('weight', 'bias')}
    del _L3_gnn_all
    return {'x': x, 'src': src, 'dst': dst, 'edge_attr_64': edge_attr_64, 'edge_type_8': edge_type_8, 'edge_weight': edge_weight, 'L0_gnn_weight': _L0_gnn_in['weight'], 'L0_gnn_h_bias': _L0_gnn_in['h_bias'], 'L0_gnn_loop_weight': _L0_gnn_in['loop_weight'], 'L1_gnn_W1_self': _L1_gnn_in['W1_self'], 'L1_gnn_W1_neigh': _L1_gnn_in['W1_neigh'], 'L1_gnn_b1': _L1_gnn_in['b1'], 'L1_gnn_W2_pool': _L1_gnn_in['W2_pool'], 'L1_gnn_b2_pool': _L1_gnn_in['b2_pool'], 'L1_gnn_W2_self': _L1_gnn_in['W2_self'], 'L1_gnn_W2_neigh': _L1_gnn_in['W2_neigh'], 'L1_gnn_b2': _L1_gnn_in['b2'], 'L1_gnn_W3_neigh': _L1_gnn_in['W3_neigh'], 'L1_gnn_b3': _L1_gnn_in['b3'], 'L1_gnn_W4_self': _L1_gnn_in['W4_self'], 'L1_gnn_W4_neigh': _L1_gnn_in['W4_neigh'], 'L1_gnn_b4': _L1_gnn_in['b4'], 'L1_gnn_W_fc': _L1_gnn_in['W_fc'], 'L1_gnn_b_fc': _L1_gnn_in['b_fc'], 'L2_gnn_weight': _L2_gnn_in['weight'], 'L3_gnn_weight': _L3_gnn_in['weight'], 'L3_gnn_bias': _L3_gnn_in['bias']}

def reference(x, src, dst, edge_attr_64, edge_type_8, edge_weight, L0_gnn_weight, L0_gnn_h_bias, L0_gnn_loop_weight, L1_gnn_W1_self, L1_gnn_W1_neigh, L1_gnn_b1, L1_gnn_W2_pool, L1_gnn_b2_pool, L1_gnn_W2_self, L1_gnn_W2_neigh, L1_gnn_b2, L1_gnn_W3_neigh, L1_gnn_b3, L1_gnn_W4_self, L1_gnn_W4_neigh, L1_gnn_b4, L1_gnn_W_fc, L1_gnn_b_fc, L2_gnn_weight, L3_gnn_weight, L3_gnn_bias):
    import jax
    import jax.numpy as jnp

    def _L0_gnn_ref(edge_index, x, edge_type, weight, h_bias, loop_weight):
        import jax, jax.numpy as jnp
        import numpy as np
        N_NODES = 50000
        N_EDGES = 25000
        IN_FEAT = 256
        OUT_FEAT = 256
        NUM_RELS = 8
        ALPHA = 0.5
        num_nodes = x.shape[0]
        src, dst = (edge_index[0], edge_index[1])
        hx = jnp.einsum('ni,rio->rno', x, weight)
        msg = hx[edge_type, src]
        agg = jax.ops.segment_sum(msg, dst, num_segments=num_nodes)
        node_repr = agg * jnp.asarray(ALPHA, x.dtype) ** 0.5
        node_repr = node_repr + h_bias
        loop_message = x @ loop_weight
        node_repr = node_repr + loop_message * jnp.asarray(1.0 - ALPHA, x.dtype) ** 0.5
        return node_repr

    def _L1_gnn_ref(features, edge_src, edge_dst, W1_self, W1_neigh, b1, W2_pool, b2_pool, W2_self, W2_neigh, b2, W3_neigh, b3, W4_self, W4_neigh, b4, W_fc, b_fc):
        import jax, jax.numpy as jnp
        import numpy as np
        N_NODES = 10000
        N_EDGES = 10000
        IN_F, HID_F, OUT_F = (256, 512, 256)

        def _glorot(key, shape):
            lim = np.sqrt(6.0 / (shape[0] + shape[1]))
            return jax.random.uniform(key, shape, jnp.float32, -lim, lim)

        def _sage_mean(h, src, dst, n, deg, W_self, W_neigh, b):
            msum = jax.ops.segment_sum(h[src], dst, num_segments=n)
            h_neigh = msum / jnp.clip(deg, 1.0)[:, None]
            return h @ W_self + h_neigh @ W_neigh + b

        def _sage_pool(h, src, dst, n, deg, W_pool, b_pool, W_self, W_neigh, b):
            hp = jax.nn.relu(h @ W_pool + b_pool)
            hmax = jax.ops.segment_max(hp[src], dst, num_segments=n)
            hmax = jnp.where(deg[:, None] > 0, hmax, 0.0)
            return h @ W_self + hmax @ W_neigh + b

        def _sage_gcn(h, src, dst, n, deg, W_neigh, b):
            msum = jax.ops.segment_sum(h[src], dst, num_segments=n)
            h_neigh = (msum + h) / (deg + 1.0)[:, None]
            return h_neigh @ W_neigh + b
        n = features.shape[0]
        deg = jax.ops.segment_sum(jnp.ones(edge_dst.shape[0], features.dtype), edge_dst, num_segments=n)
        h = _sage_mean(features, edge_src, edge_dst, n, deg, W1_self, W1_neigh, b1)
        h = _sage_pool(h, edge_src, edge_dst, n, deg, W2_pool, b2_pool, W2_self, W2_neigh, b2)
        h = _sage_gcn(h, edge_src, edge_dst, n, deg, W3_neigh, b3)
        h = _sage_mean(h, edge_src, edge_dst, n, deg, W4_self, W4_neigh, b4)
        return h @ W_fc + b_fc

    def _L2_gnn_ref(inputs, weight, edge_src, edge_dst, edge_vals):
        import jax, jax.numpy as jnp
        import numpy as np
        N_NODES = 3125
        N_EDGES = 100000
        D_IN = 256
        D_OUT = 256
        x = inputs @ weight
        msgs = edge_vals[:, None] * x[edge_src]
        out = jax.ops.segment_sum(msgs, edge_dst, num_segments=inputs.shape[0])
        return jax.nn.relu(out)

    def _L3_gnn_ref(feat, edge_feat, weight, bias, src, dst):
        import jax, jax.numpy as jnp
        import numpy as np
        N_NODES = 50000
        N, F_IN = feat.shape
        ones = jnp.ones(src.shape[0], dtype=jnp.float32)
        out_deg = jax.ops.segment_sum(ones, src, num_segments=N)
        norm_out = jnp.maximum(out_deg, 1.0) ** (-0.5)
        feat_n = feat * norm_out[:, None]
        agg_h = jax.ops.segment_sum(feat_n[src], dst, num_segments=N)
        agg_e = jax.ops.segment_sum(edge_feat, dst, num_segments=N)
        rst = jnp.concatenate([agg_h, agg_e], axis=1) @ weight
        in_deg = jax.ops.segment_sum(ones, dst, num_segments=N)
        norm_in = jnp.maximum(in_deg, 1.0) ** (-0.5)
        rst = rst * norm_in[:, None] + bias
        return jax.nn.relu(rst)
    edge_index = jnp.stack([src, dst])
    h = jnp.maximum(_layernorm(x, axis=-1), 0.0)
    x = x + _L0_gnn_ref(edge_index, h, edge_type_8, L0_gnn_weight, L0_gnn_h_bias, L0_gnn_loop_weight)
    h = jnp.maximum(_layernorm(x, axis=-1), 0.0)
    x = x + _L1_gnn_ref(h, src, dst, L1_gnn_W1_self, L1_gnn_W1_neigh, L1_gnn_b1, L1_gnn_W2_pool, L1_gnn_b2_pool, L1_gnn_W2_self, L1_gnn_W2_neigh, L1_gnn_b2, L1_gnn_W3_neigh, L1_gnn_b3, L1_gnn_W4_self, L1_gnn_W4_neigh, L1_gnn_b4, L1_gnn_W_fc, L1_gnn_b_fc)
    h = jnp.maximum(_layernorm(x, axis=-1), 0.0)
    x = x + _L2_gnn_ref(h, L2_gnn_weight, src, dst, edge_weight)
    h = jnp.maximum(_layernorm(x, axis=-1), 0.0)
    x = x + _L3_gnn_ref(h, edge_attr_64, L3_gnn_weight, L3_gnn_bias, src, dst)
    return x

_drawn_inputs = setup_inputs


def setup_inputs(seed=0):
    import zlib

    import numpy as np

    out = dict(_drawn_inputs(seed))
    spreads = {'L0_gnn_h_bias': (0.0, 0.36),
     'L1_gnn_b1': (0.0, 0.1),
     'L1_gnn_b2_pool': (0.0, 0.1),
     'L1_gnn_b2': (0.0, 0.1),
     'L1_gnn_b3': (0.0, 0.1),
     'L1_gnn_b4': (0.0, 0.307),
     'L1_gnn_b_fc': (0.0, 0.304),
     'L3_gnn_bias': (0.0, 0.649)}
    factors = {}
    for name, (base, spread) in spreads.items():
        noise = np.random.default_rng([zlib.crc32(name.encode()), seed]).standard_normal(out[name].shape)
        drawn = base * np.exp(spread * noise) if base else spread * noise
        out[name] = jnp.asarray(drawn.astype(out[name].dtype))
    for name, factor in factors.items():
        out[name] = (out[name] * factor).astype(out[name].dtype)
    return out
```

```python
from contextlib import ExitStack

import numpy as np

import concourse.bass as bass
from concourse import mybir

F32 = mybir.dt.float32
BF16 = mybir.dt.bfloat16
I32 = mybir.dt.int32
ALU = mybir.AluOpType
ACT = mybir.ActivationFunctionType

P = 128
UN = 5


def build_gnn(nc, x_in, src_in, dst_in, attr_in, type_in, weight_in,
              w0_in, b0_in, loop_in,
              w1s_in, w1n_in, b1_in, wp_in, bp_in, w2s_in, w2n_in, b2_in, w3_in, b3_in,
              w4s_in, w4n_in, b4_in, wfc_in, bfc_in, wl2_in, wl3_in, bl3_in, out):
    N, D = x_in.shape
    (E,) = src_in.shape
    R = w0_in.shape[0]
    HID = w1s_in.shape[1]
    DE = attr_in.shape[1]
    T = 5 * (-(-N // (P * 5)))
    NP = T * P
    TI = T // UN
    CAP = 41
    SPW = 32
    GB = 8
    ROUNDS = 2 * GB * (-(-(CAP + E // P) // (2 * GB)))
    RI = ROUNDS // (2 * GB)
    RC = ROUNDS + CAP
    EP = max(p for p in range(1, P + 1) if E % p == 0)
    EC = E // EP
    HC = 40
    HS = EC // HC
    assert EC % HC == 0 and HS % 2 == 0
    ZROW = NP
    REC = 3 * SPW + 3
    SPILLS = T + -(-E // SPW)
    KD, KH = D // P, HID // P
    EPS = 1e-5
    HALF = float(np.float32(0.5) ** np.float32(0.5))
    SLOTS2 = [u % 2 for u in range(UN)]
    USES = [3, 2]

    with ExitStack() as ctx:
        def sb(name, shape, dt=F32):
            return ctx.enter_context(nc.sbuf_tensor(name, shape, dt))

        def sem(name):
            return ctx.enter_context(nc.semaphore(name))

        def sems(prefix, names):
            return {n: sem(f"{prefix}_{n}") for n in names.split()}

        def dram(name, shape, dt=F32):
            return nc.dram_tensor(name, shape, dt)

        edge_rec = dram("edge_rec", [(E + CAP) * 3], I32)
        key_dram = dram("key_dram", [NP])
        node_rec = dram("node_rec", [NP, 4], I32)
        table0 = dram("table0", [NP + 1, R * D])
        table_h = dram("table_h", [NP + 1, D])
        table_hp = dram("table_hp", [NP + 1, HID])
        table_y = dram("table_y", [NP + 1, HID])
        table_g = dram("table_g", [NP + 1, D])
        table_2 = dram("table_2", [NP + 1, D])
        table_3 = dram("table_3", [NP + 1, D])
        spill = dram("spill", [SPILLS, P, REC], I32)

        x = sb("x", [P, T, D])
        acc = sb("acc", [P, T * HID])
        H = sb("H", [P, T, HID])
        G = sb("G", [P, GB, HID])
        attr_sum = sb("attr_sum", [P, T, DE])
        idx = sb("idx", [P, 2, RC], I32)
        wt = sb("wt", [P, RC])
        round_tile = sb("round_tile", [1, RC], I32)
        wreg = sb("wreg", [P, 3 * KH * HID])
        tile_in = sb("tile_in", [P, 2, HID])
        tile_T = sb("tile_T", [P, 2, HID])
        stats = sb("stats", [P, T, 6])
        mv = sb("mv", [P, T, 2])
        std = sb("std", [P, T])
        rstd = sb("rstd", [P, T])
        nmr = sb("nmr", [P, T])
        recs = sb("recs", [P, T, 4], I32)
        node_of = sb("node_of", [P, T], I32)
        xrow = sb("xrow", [P, T], I32)
        degf = sb("degf", [P, T])
        startf = sb("startf", [P, T])
        outdeg = sb("outdeg", [P, T])
        win_at = sb("win_at", [P, T], I32)
        attr_at = sb("attr_at", [P, T], I32)
        attr_lo = sb("attr_lo", [P, T])
        attr_hi = sb("attr_hi", [P, T])
        attr_atf = sb("attr_atf", [P, T])
        pool_at = sb("pool_at", [P, UN], I32)
        pool_at2 = sb("pool_at2", [P, UN], I32)
        ones_row = sb("ones_row", [1, P])
        rdeg = sb("rdeg", [P, T])
        rdeg1 = sb("rdeg1", [P, T])
        norm_in = sb("norm_in", [P, T])
        norm_out = sb("norm_out", [P, T])
        normtmp = sb("normtmp", [P, 2, T])
        slot_idx = sb("slot_idx", [P, 2, GB], I32)
        iota_i = sb("iota_i", [P, P], I32)
        iota_f = sb("iota_f", [P, P])
        part_i = sb("part_i", [P, 1], I32)
        part_f = sb("part_f", [P, 1])
        ident = sb("ident", [P, P])
        small = sb("small", [1, 8, T])
        small_i = sb("small_i", [1, 4, T + 1], I32)
        biasA = sb("biasA", [P, HID])
        biasB = sb("biasB", [P, HID])
        biasC = sb("biasC", [P, HID])
        mask = sb("mask", [P, 2, CAP])
        tmpw = sb("tmpw", [P, 2, CAP])
        sp_win = sb("sp_win", [P, 3 * SPW], I32)
        sp_rec = sb("sp_rec", [P, REC], I32)
        sp_run = sb("sp_run", [P, 2])
        sp_at = sb("sp_at", [P, 1], I32)
        sp_idx = sb("sp_idx", [P, 1], I32)
        sp_m = sb("sp_m", [P, 2, SPW])
        sp_f = sb("sp_f", [P, 4])
        sp_tile = sb("sp_tile", [P, T])
        sp_sum = sb("sp_sum", [P, DE])

        ps_T = [ctx.enter_context(nc.psum_tensor(f"ps_T{i}", [P, HID], F32)) for i in range(2)]
        ps_o = [ctx.enter_context(nc.psum_tensor(f"ps_o{i}", [P, HID], F32)) for i in range(5)]
        ps_m = ctx.enter_context(nc.psum_tensor("ps_m", [P, HID], F32))

        acc512 = acc[:, :].rearrange("p (t f) -> p t f", t=T)
        acc256 = acc[:, 0:T * D].rearrange("p (t f) -> p t f", t=T)
        Hflat = H[:, :, :].rearrange("p t f -> p (t f)")
        stage = G[:, :, :].rearrange("p b f -> p (b f)").rearrange("p (s f) -> p s f", s=2)
        w0 = wreg[:, 0:KD * R * D].rearrange("p (k n) -> p k n", k=KD)
        loopw = wreg[:, KD * R * D:KD * (R + 1) * D].rearrange("p (k n) -> p k n", k=KD)
        fold = [wreg[:, i * KH * HID:(i + 1) * KH * HID].rearrange("p (k n) -> p k n", k=KH) for i in range(3)]
        w_hp, w_y, w_v = fold
        wl2 = wreg[:, 0:KD * D].rearrange("p (k n) -> p k n", k=KD)
        wl3 = wreg[:, KD * D:KD * D + 3 * D].rearrange("p (k n) -> p k n", k=3)
        edge_i = acc[0:EP, 0:8 * EC].bitcast(I32).rearrange("p (a c) -> p a c", a=8)
        edge_b = acc[0:EP, 8 * EC:10 * EC].bitcast(BF16).rearrange("p (a c) -> p a c", a=4)
        edge3 = acc[0:EP, 10 * EC:13 * EC]
        lo_hot = Hflat[0:EP, 0:HC * P].bitcast(BF16).rearrange("p (s c n) -> p s c n", s=2, n=P)
        hi_hot = Hflat[0:EP, HC * P:HC * P + HC * T].bitcast(BF16).rearrange("p (s c n) -> p s c n", s=2, n=T)
        iota_b = Hflat[:, 6400:6464].bitcast(BF16)
        zero_b = Hflat[:, 6464:6528].bitcast(BF16)
        hist = Hflat[0:T, 6528:7552].rearrange("p (a c) -> p a c", c=P)
        upper = Hflat[0:T, 7552:7552 + T]
        tot = Hflat[0:T, 7600:7602]
        node_rec_s = Hflat[:, 7700:7700 + 4 * T].bitcast(I32).rearrange("p (t c) -> p t c", c=4)
        cols = Hflat[:, 7850:7850 + 4 * T].rearrange("p (a t) -> p a t", a=4)
        i_tmp = Hflat[:, 8100:8100 + T].bitcast(I32)
        pos_f = Hflat[:, 8000:8000 + T]
        pos_i = Hflat[:, 8050:8050 + T].bitcast(I32)
        zeros = Hflat[:, 8192:8192 + R * D]
        key_row = acc[:, 13 * EC:13 * EC + NP]
        cmp_out = acc[:, 13 * EC + NP:13 * EC + 2 * NP]
        win = acc[:, T * HID - UN * 3 * CAP:T * HID].bitcast(I32).rearrange("p (s c) -> p s c", s=UN)
        attr_win = [Hflat[:, i * CAP * DE:(i + 1) * CAP * DE] for i in range(2)]
        sp_attr = Hflat[:, 0:SPW * DE]
        f_wfc = Hflat[:, 0:KH * D].rearrange("p (k n) -> p k n", k=KH)

        def fold_buf(i):
            a = KH * D + i * KH * HID
            return Hflat[:, a:a + KH * HID].rearrange("p (k n) -> p k n", k=KH)

        f_left, f_leftT, f_F, f_M, f_S = [fold_buf(i) for i in range(5)]
        f_row = Hflat[0:1, KH * D + 5 * KH * HID:KH * D + 5 * KH * HID + 2 * HID].rearrange("p (a n) -> p a n", a=2)
        f_bias = tile_in[:, :, :].rearrange("p s f -> p (s f)").rearrange("p (a k n) -> p a k n", a=2, k=KH)
        f_bcol = stats[:, 0:4, 0:4]

        ld = sems("ld", "edges w0 zero tail rec keys nodes l2 l3")
        pr = sems("pr", "const hot hist sums carry key turned cols pos placed nodes norm x flat at")
        win_in = [sem(f"win_in{u}") for u in range(UN)]
        spb = sems("spb", "dve window stored")
        ea = sems("ea", "at in0 in1 sum dve load window done")
        fo = sems("fo", "turned lhs done out left right bias bcol")
        sent = "out at sent0 sent1"
        made = "in turned lhs mm"
        L = {"t0": sems("t0", f"{made} {sent} kept"), "tm": sems("tm", f"{sent} kept"),
             "thp": sems("thp", f"{made} {sent}"), "ty": sems("ty", f"{made} out"),
             "tv": sems("tv", f"{made} {sent} kept"), "tg": sems("tg", sent),
             "t2": sems("t2", f"{made} {sent}"), "t3": sems("t3", sent), "ro": sems("ro", f"{made} {sent}")}
        gather_in = [sem(f"gather_in{u}") for u in range(GB)]
        rows_in = [sem(f"rows_in{h}") for h in range(2)]
        acc_done = sem("acc_done")
        SPL = [sems(f"spl{n}", "dve load row") for n in range(7)]
        dve_chain = sem("dve_chain")
        act_chain = sem("act_chain")
        ln_var = sem("ln_var")
        ln_std = sem("ln_std")
        ln_ready = sem("ln_ready")
        passed = sem("passed")
        PER_PASS = GB + ROUNDS
        MARKS = 20
        mark = sb("mark", [1, MARKS])
        HOT0 = 3
        SPB_AT, SPB_PER = 2, 13
        EA_AT, EA_PER = 2, 9
        FOLD = [(w4s_in, [(f_wfc, f_F, 0, D)]),
                (w4n_in, [(f_wfc, f_F, D, D)]),
                (w3_in, [(f_F, f_M, 0, HID)]),
                (w2n_in, [(f_M, w_v, 0, HID)]),
                (w2s_in, [(f_M, f_S, 0, HID)]),
                (w1s_in, [(f_S, w_y, 0, HID), (f_F, w_hp, 0, HID)]),
                (w1n_in, [(f_S, w_y[:, KD:KH, :], 0, HID), (f_F, w_hp[:, KD:KH, :], 0, HID)])]
        FOLD_BIAS = {1: ((2, 3), [biasA]), 4: ((0, 1), [biasC, biasB])}
        FOLDED = sum(v.shape[0] // P * len(outs) for v, outs in FOLD) + 3

        class Chain:

            def __init__(self, eng, s):
                self.eng, self.sem, self.base, self.n = eng, s, 0, 0

            def __call__(self, ins):
                ins.then_inc(self.sem, 1)
                self.n += 1

            def sync(self):
                self.eng.wait_ge(self.sem, self.base + self.n)

            def link(self, ins):
                self(ins)
                self.sync()

        def w(eng, s, v):
            if not isinstance(v, int) or v > 0:
                eng.wait_ge(s, v)

        def apart(eng):
            eng.nop(nofuse=True)

        def loop(eng, n, body, chain=None):
            start = chain.n if chain else 0
            body(0)
            per = chain.n - start if chain else 0
            with eng.Fori(1, n) as i:
                if chain:
                    chain.base, chain.n = i * per + start, 0
                body(i)
            if chain:
                chain.base, chain.n = 0, start + n * per

        def lag(u):
            return 1 if u == 0 else 2

        def slot_uses(i, u):
            return i * USES[u % 2] + u // 2

        block = ctx.enter_context(nc.Block())

        @block.sync
        def _(sp):
            for a, v in enumerate((dst_in, src_in, type_in)):
                sp.dma_start(edge_i[:, a, :], v.rearrange("(p c) -> p c", p=EP)).then_inc(ld["edges"], 16)
            sp.dma_start(edge_i[:, 3, :].bitcast(F32), weight_in.rearrange("(p c) -> p c", p=EP))\
                .then_inc(ld["edges"], 16)
            for r in range(R):
                sp.dma_start(w0[:, :, r * D:(r + 1) * D], w0_in[r].rearrange("(k p) n -> p k n", p=P))\
                    .then_inc(ld["w0"], 16)
            sp.dma_start(loopw, loop_in.rearrange("(k p) n -> p k n", p=P)).then_inc(ld["w0"], 16)
            sp.dma_start(biasA[:, 0:D], b0_in.rearrange("(a n) -> a n", a=1).to_broadcast([P, D]))\
                .then_inc(ld["w0"], 16)
            sp.wait_ge(pr["const"], 8)
            for table, width in ((table0, R * D), (table_h, D), (table_hp, HID), (table_y, HID),
                                 (table_g, D), (table_2, D), (table_3, D)):
                sp.dma_start(table[NP:NP + 1, :], zeros[0:1, 0:width]).then_inc(ld["zero"], 16)
            sp.dma_start(edge_rec[3 * E:3 * (E + CAP)].rearrange("(a n) -> a n", a=1),
                         zeros[0:1, 0:3 * CAP].bitcast(I32)).then_inc(ld["tail"], 16)
            sp.wait_ge(pr["hot"], 3)
            sp.dma_start(edge_rec[0:3 * E].rearrange("(p c) -> p c", p=EP), edge3.bitcast(I32)).then_inc(ld["rec"], 16)
            sp.wait_ge(pr["key"], 1)
            sp.dma_start(key_dram[:].rearrange("(h l) -> h l", l=P), hist[:, 4, :]).then_inc(ld["keys"], 16)
            sp.wait_ge(ld["keys"], 16)
            sp.dma_start(key_row, key_dram[:].rearrange("(a n) -> a n", a=1).to_broadcast([P, NP]))\
                .then_inc(ld["keys"], 16)
            sp.wait_ge(pr["placed"], 16 * T)
            sp.dma_start(recs[:, :, :], node_rec[:, :].rearrange("(t p) c -> p t c", p=P)).then_inc(ld["nodes"], 16)

            def row_numbers(n):
                kind = 1 if n == 0 else 0

                def body(i):
                    for h in range(2):
                        w(sp, acc_done, n * PER_PASS + i * 2 * GB + h * GB)
                        sp.dma_start(slot_idx[:, h, :], idx[:, kind, bass.ds(i * 2 * GB + h * GB, GB)])\
                            .then_inc(rows_in[h], 16)
                loop(sp, RI, body)

            sp.wait_ge(pr["flat"], 1)
            for n in range(7):
                row_numbers(n)
                if n == 2:
                    sp.wait_ge(L["ty"]["mm"], T)
                    sp.dma_start(wl2[:, :, :], wl2_in.rearrange("(k p) n -> p k n", p=P)).then_inc(ld["l2"], 16)
                    sp.dma_start(wl3[:, 0:KD, :], wl3_in[0:D, :].rearrange("(k p) n -> p k n", p=P)).then_inc(ld["l3"], 16)
                    sp.dma_start(wl3[0:DE, KD, :], wl3_in[D:D + DE, :]).then_inc(ld["l3"], 16)
                    sp.dma_start(biasC[:, 0:D], bl3_in.rearrange("(a n) -> a n", a=1).to_broadcast([P, D]))\
                        .then_inc(ld["l3"], 16)

        @block.gpsimd
        def _(po):
            po.iota(iota_i[:, :], pattern=[[1, P]], base=0, channel_multiplier=0).then_inc(pr["const"], 1)
            po.iota(part_i[:, :], pattern=[[0, 1]], base=0, channel_multiplier=1).then_inc(pr["const"], 1)
            po.memset(ident[:, :], 0.0).then_inc(pr["const"], 1)
            po.memset(zeros, 0.0).then_inc(pr["const"], 1)
            po.memset(ones_row[:, :], 1.0).then_inc(pr["const"], 1)
            po.memset(upper, 1.0).then_inc(pr["const"], 1)
            po.wait_ge(pr["const"], 6)
            po.affine_select(out=ident[:, :], in_=ident[:, :], compare_op=ALU.not_equal, fill=1.0,
                             base=0, pattern=[[-1, P]], channel_multiplier=1).then_inc(pr["const"], 1)
            po.affine_select(out=upper, in_=upper, compare_op=ALU.is_gt, fill=0.0,
                             base=0, pattern=[[1, T]], channel_multiplier=-1).then_inc(pr["const"], 1)
            po.wait_ge(pr["pos"], 1)
            for t in range(T):
                po.indirect_dma_start(out=node_rec[:, :], out_offset=bass.IndirectOffsetOnAxis(ap=pos_i[:, t:t + 1], axis=0),
                                      in_=node_rec_s[:, t, :], in_offset=None).then_inc(pr["placed"], 16)
            po.wait_ge(pr["nodes"], 1)
            for t in range(T):
                po.indirect_dma_start(out=x[:, t, :], out_offset=None, in_=x_in,
                                      in_offset=bass.IndirectOffsetOnAxis(ap=xrow[:, t:t + 1], axis=0))\
                    .then_inc(pr["x"], 16)
            po.wait_ge(ld["rec"], 16)
            po.wait_ge(ld["tail"], 16)
            po.wait_ge(ld["zero"], 16 * 7)
            rec_row = edge_rec[:].rearrange("(a n) -> a n", a=1)
            attr_row = attr_in.rearrange("(a n) c -> a (n c)", a=1)

            def windows(i):
                for u in range(UN):
                    if u == 0:
                        w(po, pr["flat"], 0 if isinstance(i, int) else i)
                        po.tensor_copy(pool_at[:, :], win_at[:, bass.ds(i * UN, UN)]).then_inc(pr["at"], 1)
                        po.wait_ge(pr["at"], i + 1)
                    apart(po)
                    po.indirect_dma_start(out=win[:, u, :], out_offset=None, in_=rec_row,
                                          in_offset=bass.IndirectOffsetOnAxis(ap=pool_at[:, u:u + 1], axis=1))\
                        .then_inc(win_in[u], 16)
            loop(po, TI, windows)
            po.wait_ge(pr["flat"], TI)

            with po.Fori(0, T) as t:
                n = po.value_load(small_i[0:1, 1, bass.ds(t, 1)], min_val=0, max_val=SPILLS)
                first = po.value_load(small_i[0:1, 2, bass.ds(t, 1)], min_val=0, max_val=SPILLS)
                with po.If(n):
                    with po.Fori(0, n) as j:
                        q = nc.s_assert_within(po.snap(first + j), 0, SPILLS - 1, skip_runtime_bounds_check_because="the windows counted by this program are below their bound")
                        po.wait_ge(spb["dve"], 1 + SPB_PER * q + SPB_AT)
                        apart(po)
                        po.indirect_dma_start(out=sp_win[:, :], out_offset=None, in_=rec_row,
                                              in_offset=bass.IndirectOffsetOnAxis(ap=sp_at[:, :], axis=1))\
                            .then_inc(spb["window"], 16)
                        po.wait_ge(spb["dve"], 1 + SPB_PER * q + SPB_PER)
                        po.dma_start(spill[bass.ds(q, 1), :, :].rearrange("q p c -> p (q c)"), sp_rec[:, :])\
                            .then_inc(spb["stored"], 16)
                        po.wait_ge(spb["stored"], q * 16 + 16)
            q_total = po.value_load(small_i[0:1, 3, 0:1], min_val=0, max_val=SPILLS)

            def scatter(ph, table, width, **bound):
                S = L[ph]

                def body(i):
                    for u in range(UN):
                        s = u % 2
                        if u == 0:
                            w(po, S["sent0"], 48 * i)
                            w(po, S["sent1"], 32 * i)
                            po.tensor_copy(pool_at[:, :], node_of[:, bass.ds(i * UN, UN)]).then_inc(S["at"], 1)
                            po.wait_ge(S["at"], i + 1)
                        po.wait_ge(S["out"], i * UN + u + 1)
                        apart(po)
                        po.indirect_dma_start(out=table, out_offset=bass.IndirectOffsetOnAxis(ap=pool_at[:, u:u + 1], axis=0),
                                              in_=stage[:, s, 0:width], in_offset=None, **bound).then_inc(S[f"sent{s}"], 16)
                loop(po, TI, body)
                po.wait_ge(S["sent0"], 48 * TI)
                po.wait_ge(S["sent1"], 32 * TI)

            def gathers(n, table, width):
                def body(i):
                    for h in range(2):
                        po.wait_ge(rows_in[h], (n * RI + i + 1) * 16)
                        for u in range(GB):
                            po.wait_ge(acc_done, n * PER_PASS + i * 2 * GB + h * GB + u + 1)
                            apart(po)
                            po.indirect_dma_start(out=G[:, u, 0:width], out_offset=None, in_=table,
                                                  in_offset=bass.IndirectOffsetOnAxis(ap=slot_idx[:, h, u:u + 1], axis=0))\
                                .then_inc(gather_in[u], 16)
                loop(po, RI, body)
                S = SPL[n]
                with po.If(q_total):
                    with po.Fori(0, q_total) as q:
                        po.wait_ge(S["dve"], q * (2 * SPW) + 1)
                        po.dma_start(sp_rec[:, :], spill[bass.ds(q, 1), :, :].rearrange("q p c -> p (q c)"))\
                            .then_inc(S["load"], 16)
                        with po.Fori(0, SPW) as j:
                            po.wait_ge(S["dve"], (q * SPW + j) * 2 + 2)
                            apart(po)
                            po.indirect_dma_start(out=G[:, 0, 0:width], out_offset=None, in_=table,
                                                  in_offset=bass.IndirectOffsetOnAxis(ap=sp_idx[:, :], axis=0))\
                                .then_inc(S["row"], 16)

            S = L["t0"]

            def table0_and_attributes(i):
                for u in range(UN):
                    s = u % 2
                    if u == 0:
                        w(po, S["sent0"], 48 * i)
                        w(po, S["sent1"], 32 * i)
                        w(po, ea["sum"], i * UN)
                        po.tensor_copy(pool_at[:, :], node_of[:, bass.ds(i * UN, UN)]).then_inc(S["at"], 1)
                        po.tensor_copy(pool_at2[:, :], attr_at[:, bass.ds(i * UN, UN)]).then_inc(S["at"], 1)
                        po.wait_ge(S["at"], i * 2 + 2)
                    w(po, ea["sum"], i * UN + u + 1 - lag(u))
                    apart(po)
                    po.indirect_dma_start(out=attr_win[s], out_offset=None, in_=attr_row,
                                          in_offset=bass.IndirectOffsetOnAxis(ap=pool_at2[:, u:u + 1], axis=1))\
                        .then_inc(ea[f"in{s}"], 16)
                    po.wait_ge(S["out"], (i * UN + u + 1) * 4)
                    apart(po)
                    po.indirect_dma_start(out=table0[:, :], out_offset=bass.IndirectOffsetOnAxis(ap=pool_at[:, u:u + 1], axis=0),
                                          in_=stage[:, s, :], in_offset=None).then_inc(S[f"sent{s}"], 16)
            loop(po, TI, table0_and_attributes)
            with po.If(q_total):
                with po.Fori(0, q_total) as q:
                    po.wait_ge(ea["dve"], q * EA_PER + 1)
                    po.dma_start(sp_rec[:, :], spill[bass.ds(q, 1), :, :].rearrange("q p c -> p (q c)"))\
                        .then_inc(ea["load"], 16)
                    po.wait_ge(ea["dve"], q * EA_PER + 1 + EA_AT)
                    apart(po)
                    po.indirect_dma_start(out=sp_attr, out_offset=None, in_=attr_row,
                                          in_offset=bass.IndirectOffsetOnAxis(ap=sp_at[:, :], axis=1))\
                        .then_inc(ea["window"], 16)
            po.wait_ge(S["sent0"], 48 * TI)
            po.wait_ge(S["sent1"], 32 * TI)
            gathers(0, table0[:, :].rearrange("n (r f) -> (n r) f", r=R), D)
            for ph, n, table, width in (("tm", 1, table_h, D), ("thp", 2, table_hp, HID), ("tv", 3, table_y, HID),
                                        ("tg", 4, table_g, D), ("t2", 5, table_2, D), ("t3", 6, table_3, D)):
                scatter(ph, table[:, :], width)
                gathers(n, table[:, :], width)
            scatter("ro", out, D, bounds_check=N - 1, oob_is_err=False)

        @block.scalar
        def _(act):
            ch = Chain(act, act_chain)

            def roots(n):
                act.wait_ge(ln_var, n + 1)
                act.activation(std[:, :], std[:, :], ACT.Sqrt).then_inc(ln_std, 1)

            def tile_turned(S, T_, s):
                act.wait_ge(S["turned"], T_ + 1)
                act.activation(tile_T[:, s, :], ps_T[s][:, :], ACT.Copy).then_inc(S["lhs"], 1)

            act.wait_ge(pr["norm"], 1)
            act.activation(normtmp[:, :, :], normtmp[:, :, :], ACT.Sqrt).then_inc(pr["norm"], 1)
            roots(0)
            S = L["t0"]
            act.wait_ge(ln_ready, 1)

            def table0_tiles(i):
                for u in range(UN):
                    T_, s = i * UN + u, u % 2
                    w(act, S["turned"], T_ + 1 - lag(u))
                    apart(act)
                    act.activation(tile_in[:, s, 0:D], x[:, T_, :], ACT.Relu, bias=nmr[:, bass.ds(T_, 1)],
                                   scale=rstd[:, bass.ds(T_, 1)]).then_inc(S["in"], 1)
                    w(act, S["mm"], (T_ + 1 - lag(u)) * 5)
                    act.wait_ge(S["turned"], T_ + 1)
                    act.activation(tile_T[:, s, 0:D], ps_T[s][:, 0:D], ACT.Copy).then_inc(S["lhs"], 1)
                    w(act, S[f"sent{s}"], slot_uses(i, u) * 16)
                    for c in range(4):
                        act.wait_ge(S["mm"], T_ * 5 + c + 1)
                        act.activation(stage[:, s, c * HID:(c + 1) * HID], ps_o[c][:, :], ACT.Copy).then_inc(S["out"], 1)
            loop(act, TI, table0_tiles)

            act.wait_ge(ea["done"], 1)
            act.wait_ge(S["mm"], 5 * T)
            act.wait_ge(ld["zero"], 16 * 7)
            act.dma_start(f_wfc, wfc_in.rearrange("(k p) n -> p k n", p=P)).then_inc(fo["right"], 16)
            for a, v in enumerate((b1_in, b2_in, b3_in, b4_in)):
                act.dma_start(f_bcol[:, a, :], v.rearrange("(k p) -> p k", p=P), allow_slow_non_contiguous=True).then_inc(fo["bias"], 16)
            act.dma_start(f_row[0:1, 0, 0:D], bfc_in.rearrange("(a n) -> a n", a=1)).then_inc(fo["bias"], 16)
            act.dma_start(f_row[0:1, 1, :], bp_in.rearrange("(a n) -> a n", a=1)).then_inc(fo["bias"], 16)
            turned, done = 0, 0
            for n, (v, outs) in enumerate(FOLD):
                rows = v.shape[0]
                if n:
                    act.wait_ge(fo["turned"], turned)
                act.dma_start(f_left[:, 0:rows // P, :], v.rearrange("(m p) k -> p m k", p=P)).then_inc(fo["left"], 16)
                for k in range(KH):
                    act.wait_ge(fo["turned"], turned + 1)
                    if n and k == 0:
                        act.wait_ge(fo["done"], done)
                    act.activation(f_leftT[:, k, 0:rows], ps_T[k % 2][:, 0:rows], ACT.Copy).then_inc(fo["lhs"], 1)
                    turned += 1
                for (_, dest, lo, width) in outs:
                    for m in range(rows // P):
                        done += 1
                        act.wait_ge(fo["done"], done)
                        act.activation(dest[:, m, lo:lo + width], ps_o[m][:, 0:width], ACT.Copy).then_inc(fo["out"], 1)
                if n in FOLD_BIAS:
                    pair, dests = FOLD_BIAS[n]
                    if n == 4:
                        act.wait_ge(fo["turned"], turned)
                    act.wait_ge(fo["bias"], 16 * 6)
                    for a, b in enumerate(pair):
                        for k in range(KH):
                            act.activation(f_bias[:, a, k, :], f_bcol[:, b, k:k + 1].to_broadcast([P, P]), ACT.Copy)\
                                .then_inc(fo["bcol"], 1)
                    if n == 4:
                        act.dma_start(f_F, wp_in.rearrange("(k p) n -> p k n", p=P)).then_inc(fo["right"], 16)
                    for dest in dests:
                        done += 1
                        act.wait_ge(fo["done"], done)
                        act.activation(dest[:, :], ps_m[:, :], ACT.Copy).then_inc(fo["out"], 1)

            roots(1)
            S = L["tm"]
            act.wait_ge(ln_ready, 2)

            def rows_h(i):
                for u in range(UN):
                    T_, s = i * UN + u, u % 2
                    w(act, S[f"sent{s}"], slot_uses(i, u) * 16)
                    apart(act)
                    act.activation(stage[:, s, 0:D], x[:, T_, :], ACT.Relu, bias=nmr[:, bass.ds(T_, 1)],
                                   scale=rstd[:, bass.ds(T_, 1)]).then_inc(S["out"], 1)
                    act.activation(H[:, T_, 0:D], x[:, T_, :], ACT.Relu, bias=nmr[:, bass.ds(T_, 1)],
                                   scale=rstd[:, bass.ds(T_, 1)]).then_inc(S["kept"], 1)
            loop(act, TI, rows_h)

            S = L["thp"]
            act.wait_ge(passed, 2)

            def pool_tiles(i):
                for u in range(UN):
                    T_, s = i * UN + u, u % 2
                    w(act, S["turned"], T_ + 1 - lag(u))
                    apart(act)
                    act.activation(tile_in[:, s, :], H[:, T_, :], ACT.Copy).then_inc(S["in"], 1)
            loop(act, TI, pool_tiles)

            S = L["ty"]
            act.wait_ge(L["thp"]["mm"], T)

            def y_tiles(i):
                for u in range(UN):
                    T_, s = i * UN + u, u % 2
                    w(act, S["turned"], T_ + 1 - lag(u))
                    apart(act)
                    act.activation(tile_in[:, s, :], H[:, T_, :], ACT.Copy).then_inc(S["in"], 1)
                    w(act, S["mm"], T_ + 1 - lag(u))
                    tile_turned(S, T_, s)
                    act.wait_ge(S["mm"], T_ + 1)
                    apart(act)
                    act.activation(H[:, T_, :], ps_o[u][:, :], ACT.Copy).then_inc(S["out"], 1)
            loop(act, TI, y_tiles)

            S = L["tv"]
            act.wait_ge(passed, 3)

            def max_tiles(i):
                for u in range(UN):
                    T_, s = i * UN + u, u % 2
                    w(act, S["turned"], T_ + 1 - lag(u))
                    apart(act)
                    act.activation(tile_in[:, s, :], acc512[:, T_, :], ACT.Copy).then_inc(S["in"], 1)
                    w(act, S[f"sent{s}"], slot_uses(i, u) * 16)
                    act.wait_ge(S["kept"], T_ + 1)
                    apart(act)
                    act.activation(stage[:, s, 0:HID], H[:, T_, :], ACT.Copy).then_inc(S["out"], 1)
            loop(act, TI, max_tiles)

            roots(2)
            S = L["t2"]
            act.wait_ge(ln_ready, 3)

            def table2_tiles(i):
                for u in range(UN):
                    T_, s = i * UN + u, u % 2
                    w(act, S["turned"], T_ + 1 - lag(u))
                    apart(act)
                    act.activation(tile_in[:, s, 0:D], x[:, T_, :], ACT.Relu, bias=nmr[:, bass.ds(T_, 1)],
                                   scale=rstd[:, bass.ds(T_, 1)]).then_inc(S["in"], 1)
                    w(act, S[f"sent{s}"], slot_uses(i, u) * 16)
                    act.wait_ge(S["mm"], T_ + 1)
                    act.activation(stage[:, s, 0:D], ps_o[u][:, 0:D], ACT.Copy).then_inc(S["out"], 1)
            loop(act, TI, table2_tiles)

            roots(3)
            S = L["t3"]
            act.wait_ge(ln_ready, 4)

            def rows3(i):
                for u in range(UN):
                    T_, s = i * UN + u, u % 2
                    w(act, S[f"sent{s}"], slot_uses(i, u) * 16)
                    apart(act)
                    act.activation(stage[:, s, 0:D], x[:, T_, :], ACT.Relu, bias=nmr[:, bass.ds(T_, 1)],
                                   scale=rstd[:, bass.ds(T_, 1)]).then_inc(S["out"], 1)
            loop(act, TI, rows3)

            S = L["ro"]
            act.wait_ge(passed, 7)

            def last_tiles(i):
                for u in range(UN):
                    T_, s = i * UN + u, u % 2
                    w(act, S["turned"], T_ + 1 - lag(u))
                    apart(act)
                    act.activation(tile_in[:, s, 0:D], acc256[:, T_, :], ACT.Copy).then_inc(S["in"], 1)
                    act.activation(tile_in[:, s, D:D + DE], attr_sum[:, T_, :], ACT.Copy).then_inc(S["in"], 1)
            loop(act, TI, last_tiles)

        @block.tensor
        def _(pe):
            pe.wait_ge(pr["const"], 8)

            def histogram(a):
                def body(i):
                    for s in range(2):
                        pe.wait_ge(pr["hot"], HOT0 + a * 2 * HS + i * 4 + s * 2 + 2)
                        for c in range(HC):
                            first = isinstance(i, int) and s == 0 and c == 0
                            mm = pe.matmul(ps_o[a][0:T, 0:P], hi_hot[:, s, c, :], lo_hot[:, s, c, :],
                                           start=first, stop=c == HC - 1, skip_group_check=True)
                        mm.then_inc(pr["hist"], 1)
                loop(pe, HS // 2, body)
            histogram(0)
            histogram(1)
            pe.wait_ge(pr["sums"], 1)
            pe.matmul(ps_m[0:T, 0:2], upper, tot, start=True, stop=True).then_inc(pr["carry"], 1)
            pe.wait_ge(pr["key"], 1)
            for a, row in enumerate((0, 1, 3, 4)):
                mm = pe.transpose(ps_o[2][:, a * 32:a * 32 + T], hist[:, row, :], ident[0:T, 0:T])
            mm.then_inc(pr["turned"], 1)

            def turn(S, T_, s, widths, lhs_per, n_in=1):
                pe.wait_ge(S["in"], (T_ + 1) * n_in)
                for k, width in enumerate(widths):
                    mm = pe.transpose(ps_T[s][0:width, k * P:(k + 1) * P], tile_in[:, s, k * P:k * P + width], ident[:, :])
                mm.then_inc(S["turned"], 1)
                pe.wait_ge(S["lhs"], (T_ + 1) * lhs_per)

            S = L["t0"]
            pe.wait_ge(ld["w0"], 16 * (R + 2))

            def table0_tiles(i):
                for u in range(UN):
                    T_, s = i * UN + u, u % 2
                    w(pe, S["lhs"], T_ + 1 - lag(u))
                    turn(S, T_, s, [P] * KD, 1)
                    for c in range(5):
                        if c < 4:
                            w(pe, S["out"], (T_ - 1) * 4 + c + 1)
                        else:
                            w(pe, S["kept"], T_)
                        wide = HID if c < 4 else D
                        for k in range(KD):
                            right = w0[:, k, c * HID:(c + 1) * HID] if c < 4 else loopw[:, k, :]
                            mm = pe.matmul(ps_o[c][:, 0:wide], tile_T[:, s, k * P:(k + 1) * P], right,
                                           start=k == 0, stop=k == KD - 1)
                        mm.then_inc(S["mm"], 1)
            loop(pe, TI, table0_tiles)
            pe.wait_ge(S["out"], 4 * T)
            pe.wait_ge(S["kept"], T)

            turned, out_n, bcol = 0, 0, 0
            pe.wait_ge(fo["right"], 16)
            for n, (v, outs) in enumerate(FOLD):
                rows = v.shape[0]
                pe.wait_ge(fo["left"], 16 * (n + 1))
                for k in range(KH):
                    if turned >= 2:
                        pe.wait_ge(fo["lhs"], turned - 1)
                    for m in range(rows // P):
                        mm = pe.transpose(ps_T[k % 2][:, m * P:(m + 1) * P], f_left[:, m, k * P:(k + 1) * P], ident[:, :])
                    mm.then_inc(fo["turned"], 1)
                    turned += 1
                pe.wait_ge(fo["lhs"], turned)
                for (right, _, _, width) in outs:
                    if out_n:
                        pe.wait_ge(fo["out"], out_n)
                    if right is f_F and n >= 5:
                        pe.wait_ge(fo["right"], 32)
                    for m in range(rows // P):
                        for k in range(KH):
                            mm = pe.matmul(ps_o[m][:, 0:width], f_leftT[:, k, m * P:(m + 1) * P], right[:, k, 0:width],
                                           start=k == 0, stop=k == KH - 1)
                        mm.then_inc(fo["done"], 1)
                        out_n += 1
                if n in FOLD_BIAS:
                    bcol += 2 * KH
                    pe.wait_ge(fo["bcol"], bcol)
                    pe.wait_ge(fo["out"], out_n)

                    def add(a, right, width, first, last=False):
                        for k in range(KH):
                            mm = pe.matmul(ps_m[:, 0:width], f_bias[:, a, k, :], right[:, k, 0:width],
                                           start=first and k == 0, stop=last and k == KH - 1, skip_group_check=True)
                        return mm

                    def add_row(r, width):
                        return pe.matmul(ps_m[:, 0:width], ones_row[:, :], f_row[0:1, r, 0:width],
                                         start=False, stop=True, skip_group_check=True)
                    if n == 1:
                        add(0, f_F, HID, True)
                        add(1, f_wfc, D, False)
                        add_row(0, D).then_inc(fo["done"], 1)
                        out_n += 1
                    else:
                        add(0, f_S, HID, True)
                        add(1, f_M, HID, False, True).then_inc(fo["done"], 1)
                        out_n += 1
                        pe.wait_ge(fo["out"], out_n)
                        pe.wait_ge(fo["right"], 32)
                        add(0, f_F, HID, True)
                        add_row(1, HID).then_inc(fo["done"], 1)
                        out_n += 1

            def product(ph, widths, weights, wide, lhs_per=1, n_in=1, row=None, free="out"):
                S = L[ph]

                def body(i):
                    for u in range(UN):
                        T_, s = i * UN + u, u % 2
                        w(pe, S["lhs"], (T_ + 1 - lag(u)) * lhs_per)
                        turn(S, T_, s, widths, lhs_per, n_in)
                        w(pe, S[free], T_ + 1 - UN)
                        for k, width in enumerate(widths):
                            mm = pe.matmul(ps_o[u][:, 0:wide], tile_T[0:width, s, k * P:(k + 1) * P], weights[0:width, k, :],
                                           start=k == 0, stop=row is None and k == len(widths) - 1)
                        if row is not None:
                            mm = pe.matmul(ps_o[u][:, 0:wide], ones_row[:, :], row, start=False, stop=True)
                        mm.then_inc(S["mm"], 1)
                loop(pe, TI, body)
                pe.wait_ge(S[free], T)

            pe.wait_ge(fo["out"], out_n)
            product("thp", [P] * KH, w_hp, HID)
            product("ty", [P] * KH, w_y, HID, row=biasC[0:1, :])
            product("tv", [P] * KH, w_v, HID, free="kept")
            pe.wait_ge(ld["l2"], 16)
            product("t2", [P] * KD, wl2, D)
            pe.wait_ge(ld["l3"], 48)
            product("ro", [P] * KD + [DE], wl3, D, lhs_per=2, n_in=2)

        @block.vector
        def _(ve):
            ch = Chain(ve, dve_chain)
            marks = (mark[:, k:k + 1] for k in range(MARKS))
            bc = lambda a, n: a.unsqueeze(2).to_broadcast([a.shape[0], a.shape[1], n])
            ve.wait_ge(pr["const"], 8)
            ch(ve.tensor_copy(iota_f[:, :], iota_i[:, :]))
            ch(ve.tensor_copy(part_f[:, :], part_i[:, :]))
            ch(ve.tensor_copy(iota_b, iota_i[:, :]))
            ch(ve.memset(idx[:, 0, :], ZROW))
            ch(ve.memset(idx[:, 1, :], ZROW * R))
            ch(ve.memset(wt[:, :], 0.0))
            ch(ve.memset(round_tile[:, :], T - 1))
            ch(ve.memset(attr_sum[:, :, :], 0.0))
            ve.wait_ge(ld["edges"], 64)
            for a in range(2):
                ch(ve.tensor_scalar(edge_i[:, 4 + 2 * a, :], edge_i[:, a, :], P - 1, None, ALU.bitwise_and))
                ch(ve.tensor_scalar(edge_i[:, 5 + 2 * a, :], edge_i[:, a, :], 7, None, ALU.logical_shift_right))
            ch.sync()
            ch.link(ve.tensor_copy(edge_b, edge_i[:, 4:8, :]))
            e3 = edge3.rearrange("p (c r) -> p c r", r=3)
            e3i = edge3.bitcast(I32).rearrange("p (c r) -> p c r", r=3)
            ve.tensor_copy(e3i[:, :, 0], edge_i[:, 1, :]).then_inc(pr["hot"], 1)
            ve.scalar_tensor_tensor(out=e3i[:, :, 1], in0=edge_i[:, 1, :], scalar=float(R), in1=edge_i[:, 2, :],
                                    op0=ALU.mult, op1=ALU.add).then_inc(pr["hot"], 1)
            ve.tensor_copy(e3[:, :, 2], edge_i[:, 3, :].bitcast(F32)).then_inc(pr["hot"], 1)
            for a in range(2):
                def hot(i):
                    for s in range(2):
                        w(ve, pr["hist"], a * HS + i * 2 + s - 1 if a else (i * 2 + s - 1))
                        at = bass.ds((i * 2 + s) * HC, HC)
                        ve.tensor_tensor(lo_hot[:, s, :, :], bc(edge_b[:, 2 * a, at], P),
                                         iota_b[0:EP, :].unsqueeze(1).to_broadcast([EP, HC, P]), ALU.is_equal)\
                            .then_inc(pr["hot"], 1)
                        ve.tensor_tensor(hi_hot[:, s, :, :], bc(edge_b[:, 2 * a + 1, at], T),
                                         iota_b[0:EP, 0:T].unsqueeze(1).to_broadcast([EP, HC, T]), ALU.is_equal)\
                            .then_inc(pr["hot"], 1)
                loop(ve, HS // 2, hot)
            ve.wait_ge(pr["hist"], 2 * HS)
            ch(ve.tensor_copy(hist[:, 0, :], ps_o[0][0:T, 0:P]))
            ch.link(ve.tensor_copy(hist[:, 1, :], ps_o[1][0:T, 0:P]))
            ch(ve.memset(hist[:, 6, :], 1.0))
            ch(ve.memset(tot, 0.0))
            ch.link(ve.tensor_scalar(hist[:, 5, :], hist[:, 0, :], 4095.0, 4096.0, ALU.min, ALU.mult))
            ch.link(ve.tensor_tensor_scan(hist[:, 2, :], hist[:, 6, :], hist[:, 0, :], 0.0, ALU.mult, ALU.add))
            ve.tensor_copy(tot[:, 0:1], hist[:, 2, P - 1:P]).then_inc(pr["sums"], 1)
            ch(ve.tensor_scalar(sp_f[0:T, 0:1], part_f[0:T, :], -float(P), 4095.0, ALU.mult, ALU.add))
            ch.link(ve.tensor_tensor(hist[:, 3, :], hist[:, 2, :], hist[:, 0, :], ALU.subtract))
            ch.link(ve.scalar_tensor_tensor(out=hist[:, 7, :], in0=hist[:, 5, :], scalar=sp_f[0:T, 0:1],
                                            in1=iota_f[0:T, :], op0=ALU.add, op1=ALU.subtract))
            ve.wait_ge(pr["carry"], 1)
            ch.link(ve.tensor_scalar(hist[:, 3, :], hist[:, 3, :], ps_m[0:T, 0:1], None, ALU.add))
            ve.tensor_copy(hist[:, 4, :], hist[:, 7, :]).then_inc(pr["key"], 1)
            ve.wait_ge(pr["turned"], 1)
            for a in range(4):
                ch(ve.tensor_copy(cols[:, a, :], ps_o[2][:, a * 32:a * 32 + T]))
            ch.sync()
            ve.wait_ge(ld["keys"], 32)
            for t in range(T):
                ch.link(ve.tensor_scalar(cmp_out, key_row, cols[:, 3, t:t + 1], None, ALU.is_gt, ALU.add,
                                         accum_out=pos_f[:, t:t + 1]))
            ch(ve.tensor_copy(node_rec_s[:, :, 1], cols[:, 0, :]))
            ch(ve.tensor_copy(node_rec_s[:, :, 2], cols[:, 2, :]))
            ch(ve.tensor_copy(node_rec_s[:, :, 3], cols[:, 1, :]))
            ch(ve.tensor_scalar(node_rec_s[:, :, 0], iota_f[:, 0:T], float(P), part_f[:, :], ALU.mult, ALU.add))
            ch.sync()
            ve.tensor_copy(pos_i, pos_f).then_inc(pr["pos"], 1)

            ve.wait_ge(ld["nodes"], 16)
            ch(ve.tensor_copy(node_of[:, :], recs[:, :, 0]))
            ch(ve.tensor_copy(degf[:, :], recs[:, :, 1]))
            ch(ve.tensor_copy(startf[:, :], recs[:, :, 2]))
            ch(ve.tensor_copy(outdeg[:, :], recs[:, :, 3]))
            ch(ve.tensor_scalar(win_at[:, :], recs[:, :, 2], 3.0, None, ALU.mult))
            ch.link(ve.tensor_scalar(attr_atf[:, :], recs[:, :, 2], float(E - CAP), None, ALU.min))
            ch(ve.tensor_scalar(attr_at[:, :], attr_atf[:, :], float(DE), None, ALU.mult))
            ch(ve.tensor_tensor(attr_lo[:, :], startf[:, :], attr_atf[:, :], ALU.subtract))
            ch.sync()
            ve.tensor_scalar(xrow[:, :], recs[:, :, 0], float(N - 1), None, ALU.min).then_inc(pr["nodes"], 1)
            ch(ve.scalar_tensor_tensor(out=attr_hi[:, :], in0=degf[:, :], scalar=float(CAP), in1=attr_lo[:, :],
                                       op0=ALU.min, op1=ALU.add))
            ch(ve.tensor_scalar(normtmp[:, 0, :], degf[:, :], 1.0, None, ALU.max))
            ch(ve.tensor_scalar(normtmp[:, 1, :], outdeg[:, :], 1.0, None, ALU.max))
            ch(ve.tensor_scalar(rdeg1[:, :], degf[:, :], 1.0, None, ALU.add))
            ch.sync()
            ch(ve.reciprocal(rdeg1[:, :], rdeg1[:, :]))
            ch.link(ve.reciprocal(rdeg[:, :], normtmp[:, 0, :]))
            deg0 = degf[0:1, :]
            ch(ve.memset(small[:, 0, :], 1.0))
            ch(ve.tensor_scalar(small[:, 1, :], deg0, float(CAP), None, ALU.min))
            ch.link(ve.tensor_scalar(small[:, 3, :], deg0, -float(CAP), 0.0, ALU.add, ALU.max))
            ch(ve.tensor_tensor_scan(small[:, 2, :], small[:, 0, :], small[:, 1, :], 0.0, ALU.mult, ALU.add))
            ch.link(ve.tensor_scalar(small_i[:, 3, 0:T], small[:, 3, :], float(SPW - 1), None, ALU.add))
            ch(ve.tensor_tensor(small_i[:, 0, 0:T], small[:, 2, :], small[:, 1, :], ALU.subtract))
            ch.link(ve.tensor_scalar(small_i[:, 1, 0:T], small_i[:, 3, 0:T], 5, None, ALU.logical_shift_right))
            ch.link(ve.tensor_copy(small[:, 4, :], small_i[:, 1, 0:T]))
            ch.link(ve.tensor_tensor_scan(small[:, 5, :], small[:, 0, :], small[:, 4, :], 0.0, ALU.mult, ALU.add))
            ch(ve.tensor_tensor(small_i[:, 2, 0:T], small[:, 5, :], small[:, 4, :], ALU.subtract))
            ch.link(ve.tensor_copy(small_i[:, 3, 0:1], small[:, 5, T - 1:T]))
            ve.tensor_copy(sp_tile[:, :], iota_f[:, 0:T]).then_inc(pr["norm"], 1)
            ve.wait_ge(pr["norm"], 2)
            ch(ve.reciprocal(norm_in[:, :], normtmp[:, 0, :]))
            ch.link(ve.reciprocal(norm_out[:, :], normtmp[:, 1, :]))

            def flatten(i):
                for u in range(UN):
                    t = i * UN + u
                    apart(ve)
                    off = ve.value_load(small_i[0:1, 0, bass.ds(t, 1)], min_val=0, max_val=ROUNDS)
                    at = bass.ds(off, CAP)
                    ve.wait_ge(win_in[u], (i + 1) * 16)
                    rec = win[:, u, :].rearrange("p (j c) -> p j c", c=3)
                    recf = win[:, u, :].bitcast(F32).rearrange("p (j c) -> p j c", c=3)
                    ch.link(ve.tensor_scalar(mask[:, 0, :], iota_f[:, 0:CAP], degf[:, bass.ds(t, 1)], None, ALU.is_lt))
                    ch(ve.scalar_tensor_tensor(out=tmpw[:, 0, :], in0=rec[:, :, 0], scalar=-float(ZROW),
                                               in1=mask[:, 0, :], op0=ALU.add, op1=ALU.mult))
                    ch(ve.scalar_tensor_tensor(out=tmpw[:, 1, :], in0=rec[:, :, 1], scalar=-float(ZROW * R),
                                               in1=mask[:, 0, :], op0=ALU.add, op1=ALU.mult))
                    ch(ve.tensor_tensor(wt[:, at], recf[:, :, 2], mask[:, 0, :], ALU.mult))
                    ch.sync()
                    ch(ve.tensor_scalar(idx[:, 0, at], tmpw[:, 0, :], float(ZROW), None, ALU.add))
                    ch(ve.tensor_scalar(idx[:, 1, at], tmpw[:, 1, :], float(ZROW * R), None, ALU.add))
                    ch(ve.tensor_copy(round_tile[0:1, at], sp_tile[0:1, bass.ds(t, 1)].to_broadcast([1, CAP])))
                    ch.sync()
                ve.memset(mask[:, 1, :], 0.0).then_inc(pr["flat"], 1)
            loop(ve, TI, flatten, ch)

            ve.memset(next(marks), 0.0).then_inc(spb["dve"], 1)
            t_start = ch.n
            with ve.Fori(0, T) as t:
                ch.base, ch.n = t * 2 + t_start, 0
                ch(ve.tensor_scalar(sp_run[:, 0:1], startf[:, bass.ds(t, 1)], float(CAP), None, ALU.add))
                ch.link(ve.tensor_scalar(sp_run[:, 1:2], degf[:, bass.ds(t, 1)], -float(CAP), None, ALU.add))
                n = ve.value_load(small_i[0:1, 1, bass.ds(t, 1)], min_val=0, max_val=SPILLS)
                first = ve.value_load(small_i[0:1, 2, bass.ds(t, 1)], min_val=0, max_val=SPILLS)
                with ve.If(n):
                    with ve.Fori(0, n) as j:
                        q = nc.s_assert_within(ve.snap(first + j), 0, SPILLS - 1, skip_runtime_bounds_check_because="the windows counted by this program are below their bound")
                        sc = Chain(ve, spb["dve"])
                        sc.base = q * SPB_PER + 1
                        sc.link(ve.tensor_scalar(sp_f[:, 2:3], sp_run[:, 0:1], float(E), None, ALU.min))
                        sc(ve.tensor_scalar(sp_at[:, :], sp_f[:, 2:3], 3.0, None, ALU.mult))
                        assert sc.n == SPB_AT
                        sc.link(ve.tensor_scalar(sp_m[:, 0, :], iota_f[:, 0:SPW], sp_run[:, 1:2], None, ALU.is_lt))
                        ve.wait_ge(spb["window"], q * 16 + 16)
                        rec = sp_win[:, :].rearrange("p (j c) -> p j c", c=3)
                        recf = sp_win[:, :].bitcast(F32).rearrange("p (j c) -> p j c", c=3)
                        for c, z in ((0, ZROW), (1, ZROW * R)):
                            sc.link(ve.scalar_tensor_tensor(out=sp_m[:, 1, :], in0=rec[:, :, c], scalar=-float(z),
                                                            in1=sp_m[:, 0, :], op0=ALU.add, op1=ALU.mult))
                            sc.link(ve.tensor_scalar(sp_rec[:, c * SPW:(c + 1) * SPW], sp_m[:, 1, :], float(z), None,
                                                     ALU.add))
                        sc(ve.tensor_tensor(sp_rec[:, 2 * SPW:3 * SPW].bitcast(F32), recf[:, :, 2], sp_m[:, 0, :], ALU.mult))
                        sc(ve.tensor_copy(sp_rec[:, 3 * SPW:3 * SPW + 1], sp_tile[:, bass.ds(t, 1)]))
                        sc(ve.tensor_copy(sp_rec[:, 3 * SPW + 1:3 * SPW + 2], sp_f[:, 2:3]))
                        sc.link(ve.tensor_copy(sp_rec[:, 3 * SPW + 2:3 * SPW + 3], sp_run[:, 1:2]))
                        sc(ve.tensor_scalar(sp_run[:, 0:1], sp_run[:, 0:1], float(SPW), None, ALU.add))
                        sc.link(ve.tensor_scalar(sp_run[:, 1:2], sp_run[:, 1:2], -float(SPW), None, ALU.add))
                        assert sc.n == SPB_PER
            ch.base, ch.n = 0, t_start + 2 * T
            q_total = ve.value_load(small_i[0:1, 3, 0:1], min_val=0, max_val=SPILLS)

            def layer_norm(n):
                def sums(i):
                    for u in range(UN):
                        ch(ve.bn_stats(stats[:, i * UN + u, :], x[:, i * UN + u, :]))
                loop(ve, TI, sums, ch)
                ch.sync()

                for t in range(T):
                    ch(ve.bn_aggr(mv[:, t, :], stats[:, t, :]))
                ch.sync()
                ve.tensor_scalar(std[:, :], mv[:, :, 1], EPS, None, ALU.add).then_inc(ln_var, 1)
                ve.wait_ge(ln_std, n + 1)
                ch.link(ve.reciprocal(rstd[:, :], std[:, :]))
                if n == 3:
                    ch.link(ve.tensor_tensor(rstd[:, :], rstd[:, :], norm_out[:, :], ALU.mult))
                ve.scalar_tensor_tensor(out=nmr[:, :], in0=mv[:, :, 0], scalar=-1.0, in1=rstd[:, :],
                                        op0=ALU.mult, op1=ALU.mult).then_inc(ln_ready, 1)

            def tile_turned(S, T_, s, wide, last=None, mm_lag=None):
                w(ve, S["mm"], mm_lag)
                ve.wait_ge(S["turned"], T_ + 1)
                ve.tensor_copy(tile_T[:, s, 0:wide], ps_T[s][:, 0:wide]).then_inc(S["lhs"], 1)
                if last:
                    ve.tensor_copy(tile_T[0:last, s, wide:wide + P], ps_T[s][0:last, wide:wide + P]).then_inc(S["lhs"], 1)

            def rounds(n, wide, kind):
                view = acc256 if wide == D else acc512
                piece = T * wide // GB
                for k in range(GB):
                    ve.memset(acc[:, k * piece:(k + 1) * piece], 0.0).then_inc(acc_done, 1)

                def fold_in(t, row, weight):
                    if kind == "weighted":
                        return ve.scalar_tensor_tensor(out=view[:, t, :], in0=row, scalar=weight, in1=view[:, t, :],
                                                       op0=ALU.mult, op1=ALU.add)
                    return ve.tensor_tensor(view[:, t, :], view[:, t, :], row, ALU.max if kind == "max" else ALU.add)

                def body(i):
                    for h in range(2):
                        first = i * 2 * GB + h * GB
                        _, tiles = nc.values_load_multi_w_load_instructions(
                            round_tile[0:1, bass.ds(first, GB)], engines=[ve.engine], min_val=0, max_val=T - 1,
                            skip_runtime_bounds_check_because="the numbers of tiles, written by this program")
                        for u in range(GB):
                            ve.wait_ge(gather_in[u], (n * 2 * RI + i * 2 + h + 1) * 16)
                            ve.wait_ge(acc_done, n * PER_PASS + GB + first + u)
                            fold_in(tiles[u], G[:, u, 0:wide], wt[:, bass.ds(first + u, 1)]).then_inc(acc_done, 1)
                loop(ve, RI, body)
                ve.wait_ge(acc_done, (n + 1) * PER_PASS)
                S = SPL[n]
                ve.memset(next(marks), 0.0).then_inc(S["dve"], 1)
                with ve.If(q_total):
                    with ve.Fori(0, q_total) as q:
                        ve.wait_ge(S["load"], q * 16 + 16)
                        apart(ve)
                        t = ve.value_load(sp_rec[0:1, 3 * SPW:3 * SPW + 1], min_val=0, max_val=T - 1)
                        at = SPW if n == 0 else 0
                        with ve.Fori(0, SPW) as j:
                            m = q * SPW + j
                            ve.wait_ge(S["dve"], m * 2 + 1)
                            ve.tensor_copy(sp_idx[:, :], sp_rec[:, bass.ds(j + at, 1)]).then_inc(S["dve"], 1)
                            ve.wait_ge(S["row"], m * 16 + 16)
                            fold_in(t, G[:, 0, 0:wide], sp_rec[:, bass.ds(j + 2 * SPW, 1)].bitcast(F32))\
                                .then_inc(S["dve"], 1)
                            ve.wait_ge(S["dve"], m * 2 + 3)

            ve.wait_ge(pr["x"], 16 * T)
            layer_norm(0)
            S = L["t0"]

            def attributes(i):
                for u in range(UN):
                    T_, s = i * UN + u, u % 2
                    at = bass.ds(T_, 1)
                    ch.link(ve.tensor_scalar(mask[:, 0, :], iota_f[:, 0:CAP], attr_lo[:, at], None, ALU.is_ge))
                    ch.link(ve.scalar_tensor_tensor(out=mask[:, 1, :], in0=iota_f[:, 0:CAP], scalar=attr_hi[:, at],
                                                    in1=mask[:, 0, :], op0=ALU.is_lt, op1=ALU.mult))
                    ve.wait_ge(ea[f"in{s}"], (slot_uses(i, u) + 1) * 16)
                    av = attr_win[s].rearrange("p (j f) -> p j f", f=DE)
                    ch.link(ve.tensor_tensor(av, av, bc(mask[:, 1:2, :].rearrange("p a j -> p (a j)"), DE), ALU.mult))
                    ve.tensor_reduce(attr_sum[:, T_, :], attr_win[s].rearrange("p (j f) -> p f j", f=DE),
                                     mybir.AxisListType.X, ALU.add).then_inc(ea["sum"], 1)
                    ve.wait_ge(S["mm"], T_ * 5 + 5)
                    ve.scalar_tensor_tensor(out=x[:, T_, :], in0=ps_o[4][:, 0:D], scalar=HALF, in1=x[:, T_, :],
                                            op0=ALU.mult, op1=ALU.add).then_inc(S["kept"], 1)
            loop(ve, TI, attributes, ch)
            ve.wait_ge(S["kept"], T)
            ch(ve.tensor_tensor(x[:, :, :], x[:, :, :], biasA[:, 0:D].unsqueeze(1).to_broadcast([P, T, D]), ALU.add))
            ve.wait_ge(ea["sum"], T)
            ve.memset(next(marks), 0.0).then_inc(ea["dve"], 1)
            with ve.If(q_total):
                with ve.Fori(0, q_total) as q:
                    sc = Chain(ve, ea["dve"])
                    sc.base = q * EA_PER + 1
                    ve.wait_ge(ea["load"], q * 16 + 16)
                    apart(ve)
                    t = ve.value_load(sp_rec[0:1, 3 * SPW:3 * SPW + 1], min_val=0, max_val=T - 1)
                    sc.link(ve.tensor_scalar(sp_f[:, 2:3], sp_rec[:, 3 * SPW + 1:3 * SPW + 2], float(E - SPW), None, ALU.min))
                    sc(ve.tensor_scalar(sp_at[:, :], sp_f[:, 2:3], float(DE), None, ALU.mult))
                    assert sc.n == EA_AT
                    sc.link(ve.tensor_tensor(sp_f[:, 3:4], sp_rec[:, 3 * SPW + 1:3 * SPW + 2], sp_f[:, 2:3], ALU.subtract))
                    sc(ve.tensor_tensor(sp_f[:, 0:1], sp_f[:, 3:4], sp_rec[:, 3 * SPW + 2:3 * SPW + 3], ALU.add))
                    sc.link(ve.tensor_scalar(sp_m[:, 0, :], iota_f[:, 0:SPW], sp_f[:, 3:4], None, ALU.is_ge))
                    sc.link(ve.scalar_tensor_tensor(out=sp_m[:, 1, :], in0=iota_f[:, 0:SPW], scalar=sp_f[:, 0:1],
                                                    in1=sp_m[:, 0, :], op0=ALU.is_lt, op1=ALU.mult))
                    ve.wait_ge(ea["window"], q * 16 + 16)
                    av = sp_attr.rearrange("p (j f) -> p j f", f=DE)
                    sc.link(ve.tensor_tensor(av, av, bc(sp_m[:, 1:2, :].rearrange("p a j -> p (a j)"), DE), ALU.mult))
                    sc.link(ve.tensor_reduce(sp_sum[:, :], sp_attr.rearrange("p (j f) -> p f j", f=DE),
                                             mybir.AxisListType.X, ALU.add))
                    sc.link(ve.tensor_tensor(attr_sum[:, t, :], attr_sum[:, t, :], sp_sum[:, :], ALU.add))
                    assert sc.n == EA_PER
            ch.sync()
            ve.memset(next(marks), 0.0).then_inc(ea["done"], 1)
            rounds(0, D, "sum")
            x2 = x[:, :, :].rearrange("p t f -> p (t f)")
            acc2 = acc[:, 0:T * D]
            ch(ve.scalar_tensor_tensor(out=x2, in0=acc2, scalar=HALF, in1=x2, op0=ALU.mult, op1=ALU.add))
            ch.sync()
            ve.memset(next(marks), 0.0).then_inc(passed, 1)

            ve.wait_ge(fo["out"], FOLDED)
            layer_norm(1)
            rounds(1, D, "sum")
            ve.wait_ge(L["tm"]["kept"], T)
            ve.tensor_tensor(H[:, :, D:2 * D], acc256, bc(rdeg[:, :], D), ALU.mult).then_inc(passed, 1)
            S = L["thp"]

            def pool_rows(i):
                for u in range(UN):
                    T_, s = i * UN + u, u % 2
                    tile_turned(S, T_, s, HID, mm_lag=T_ + 1 - lag(u))
                    w(ve, S[f"sent{s}"], slot_uses(i, u) * 16)
                    ve.wait_ge(S["mm"], T_ + 1)
                    ch.link(ve.tensor_tensor(stage[:, s, 0:HID], ps_o[u][:, :], biasB[:, :], ALU.add))
                    ve.tensor_scalar(stage[:, s, 0:HID], stage[:, s, 0:HID], 0.0, None, ALU.max).then_inc(S["out"], 1)
            ve.wait_ge(passed, 2)
            loop(ve, TI, pool_rows, ch)
            rounds(2, HID, "max")
            ve.memset(next(marks), 0.0).then_inc(passed, 1)
            S = L["tv"]
            ve.wait_ge(L["ty"]["out"], T)

            def y_rows(i):
                for u in range(UN):
                    T_, s = i * UN + u, u % 2
                    tile_turned(S, T_, s, HID, mm_lag=T_ + 1 - lag(u))
                    ve.wait_ge(S["mm"], T_ + 1)
                    ve.tensor_tensor(H[:, T_, :], ps_o[u][:, :], H[:, T_, :], ALU.add).then_inc(S["kept"], 1)
            loop(ve, TI, y_rows, ch)
            ve.wait_ge(S["in"], T)
            rounds(3, HID, "sum")
            ve.wait_ge(S["out"], T)
            ch.link(ve.tensor_tensor(Hflat, Hflat, acc[:, :], ALU.add))
            S = L["tg"]

            def g_rows(i):
                for u in range(UN):
                    T_, s = i * UN + u, u % 2
                    w(ve, S[f"sent{s}"], slot_uses(i, u) * 16)
                    ve.scalar_tensor_tensor(out=stage[:, s, 0:D], in0=H[:, T_, D:2 * D], scalar=rdeg1[:, bass.ds(T_, 1)],
                                            in1=biasA[:, D:2 * D], op0=ALU.mult, op1=ALU.add).then_inc(S["out"], 1)
            loop(ve, TI, g_rows, ch)
            ch.link(ve.tensor_tensor(H[:, :, 0:D], H[:, :, 0:D], bc(rdeg1[:, :], D), ALU.mult))
            ch.link(ve.tensor_tensor(x[:, :, :], x[:, :, :], H[:, :, 0:D], ALU.add))
            ch.link(ve.tensor_tensor(x[:, :, :], x[:, :, :], biasA[:, 0:D].unsqueeze(1).to_broadcast([P, T, D]), ALU.add))
            ve.memset(next(marks), 0.0).then_inc(passed, 1)
            rounds(4, D, "sum")
            ch.link(ve.tensor_tensor(acc256, acc256, bc(rdeg[:, :], D), ALU.mult))
            ch.link(ve.tensor_tensor(x2, x2, acc2, ALU.add))
            ve.memset(next(marks), 0.0).then_inc(passed, 1)

            layer_norm(2)
            S = L["t2"]

            def turned2(i):
                for u in range(UN):
                    T_, s = i * UN + u, u % 2
                    tile_turned(S, T_, s, D, mm_lag=T_ + 1 - lag(u))
            loop(ve, TI, turned2, ch)
            rounds(5, D, "weighted")
            ch.link(ve.scalar_tensor_tensor(out=x2, in0=acc2, scalar=0.0, in1=x2, op0=ALU.max, op1=ALU.add))
            ve.memset(next(marks), 0.0).then_inc(passed, 1)

            layer_norm(3)
            rounds(6, D, "sum")
            ve.memset(next(marks), 0.0).then_inc(passed, 1)
            S = L["ro"]
            ve.wait_ge(ld["l3"], 48)

            def last_rows(i):
                for u in range(UN):
                    T_, s = i * UN + u, u % 2
                    tile_turned(S, T_, s, D, last=DE, mm_lag=T_ + 1 - lag(u))
                    w(ve, S[f"sent{s}"], slot_uses(i, u) * 16)
                    ve.wait_ge(S["mm"], T_ + 1)
                    ch.link(ve.scalar_tensor_tensor(out=stage[:, s, 0:D], in0=ps_o[u][:, 0:D], scalar=norm_in[:, bass.ds(T_, 1)],
                                                    in1=biasC[:, 0:D], op0=ALU.mult, op1=ALU.add))
                    ve.scalar_tensor_tensor(out=stage[:, s, 0:D], in0=stage[:, s, 0:D], scalar=0.0, in1=x[:, T_, :],
                                            op0=ALU.max, op1=ALU.add).then_inc(S["out"], 1)
            loop(ve, TI, last_rows, ch)


_INS = ['x', 'src', 'dst', 'edge_attr_64', 'edge_type_8', 'edge_weight',
        'L0_gnn_weight', 'L0_gnn_h_bias', 'L0_gnn_loop_weight',
        'L1_gnn_W1_self', 'L1_gnn_W1_neigh', 'L1_gnn_b1', 'L1_gnn_W2_pool', 'L1_gnn_b2_pool',
        'L1_gnn_W2_self', 'L1_gnn_W2_neigh', 'L1_gnn_b2', 'L1_gnn_W3_neigh', 'L1_gnn_b3',
        'L1_gnn_W4_self', 'L1_gnn_W4_neigh', 'L1_gnn_b4', 'L1_gnn_W_fc', 'L1_gnn_b_fc',
        'L2_gnn_weight', 'L3_gnn_weight', 'L3_gnn_bias']


def kernel(**inputs):
    import concourse.bacc as _bacc
    from concourse import mybir as _mybir
    from concourse.bass_utils import run_bass_kernel_spmd as _run

    nc = _bacc.Bacc("TRN2", target_bir_lowering=False, num_devices=1)
    arrays, args = {}, []
    for name in _INS:
        a = np.ascontiguousarray(inputs[name])
        arrays[f"in_{name}_dram"] = a
        args.append(nc.dram_tensor(f"in_{name}_dram", a.shape, _mybir.dt.from_np(a.dtype), kind="ExternalInput").ap())
    args.append(nc.dram_tensor("out_0_dram", arrays["in_x_dram"].shape, F32, kind="ExternalOutput").ap())
    build_gnn(nc, *args)
    r = _run(nc, [arrays], core_ids=[0])
    return r.results[0]["out_0_dram"]
```

```python
from contextlib import ExitStack

import numpy as np

import concourse.bass as bass
from concourse import mybir

F32 = mybir.dt.float32
BF16 = mybir.dt.bfloat16
I32 = mybir.dt.int32
ALU = mybir.AluOpType
ACT = mybir.ActivationFunctionType

P = 128
UN = 5


def build_gnn(nc, x_in, src_in, dst_in, attr_in, type_in, weight_in,
              w0_in, b0_in, loop_in,
              w1s_in, w1n_in, b1_in, wp_in, bp_in, w2s_in, w2n_in, b2_in, w3_in, b3_in,
              w4s_in, w4n_in, b4_in, wfc_in, bfc_in, wl2_in, wl3_in, bl3_in, out):
    N, D = x_in.shape
    (E,) = src_in.shape
    R = w0_in.shape[0]
    HID = w1s_in.shape[1]
    DE = attr_in.shape[1]
    T = 5 * (-(-N // (P * 5)))
    NP = T * P
    TI = T // UN
    CAP = 41
    SPW = 32
    GB = 8
    ROUNDS = 2 * GB * (-(-(CAP + E // P) // (2 * GB)))
    RI = ROUNDS // (2 * GB)
    RC = ROUNDS + CAP
    EP = max(p for p in range(1, P + 1) if E % p == 0)
    EC = E // EP
    HC = 40
    HS = EC // HC
    assert EC % HC == 0 and HS % 2 == 0
    ZROW = NP
    REC = 3 * SPW + 3
    SPILLS = T + -(-E // SPW)
    KD, KH = D // P, HID // P
    EPS = 1e-5
    HALF = float(np.float32(0.5) ** np.float32(0.5))
    SLOTS2 = [u % 2 for u in range(UN)]
    USES = [3, 2]

    with ExitStack() as ctx:
        def sb(name, shape, dt=F32):
            return ctx.enter_context(nc.sbuf_tensor(name, shape, dt))

        def sem(name):
            return ctx.enter_context(nc.semaphore(name))

        def sems(prefix, names):
            return {n: sem(f"{prefix}_{n}") for n in names.split()}

        def dram(name, shape, dt=F32):
            return nc.dram_tensor(name, shape, dt)

        edge_rec = dram("edge_rec", [(E + CAP) * 3], I32)
        key_dram = dram("key_dram", [NP])
        node_rec = dram("node_rec", [NP, 3], I32)
        out_dram = dram("out_dram", [NP])
        table_x = dram("table_x", [NP, D])
        table0 = dram("table0", [NP + 1, R * D])
        table_h = dram("table_h", [NP + 1, D])
        table_hp = dram("table_hp", [NP + 1, HID])
        table_y = dram("table_y", [NP + 1, HID])
        table_g = dram("table_g", [NP + 1, D])
        table_2 = dram("table_2", [NP + 1, D])
        table_3 = dram("table_3", [NP + 1, D])
        spill = dram("spill", [SPILLS, P, REC], I32)

        x = sb("x", [P, T, D])
        acc = sb("acc", [P, T * HID])
        H = sb("H", [P, T, HID])
        G = sb("G", [P, GB, HID])
        attr_sum = sb("attr_sum", [P, T, DE])
        idx = sb("idx", [P, 2, RC], I32)
        wt = sb("wt", [P, RC])
        round_tile = sb("round_tile", [1, RC], I32)
        wreg = sb("wreg", [P, 3 * KH * HID])
        tile_in = sb("tile_in", [P, 2, HID])
        tile_T = sb("tile_T", [P, 2, HID])
        stats = sb("stats", [P, T, 6])
        mv = sb("mv", [P, T, 2])
        std = sb("std", [P, T])
        rstd = sb("rstd", [P, T])
        nmr = sb("nmr", [P, T])
        recs = sb("recs", [P, T, 3], I32)
        node_of = sb("node_of", [P, T], I32)
        degf = sb("degf", [P, T])
        startf = sb("startf", [P, T])
        outdeg = sb("outdeg", [P, T])
        win_at = sb("win_at", [P, T], I32)
        attr_at = sb("attr_at", [P, T], I32)
        attr_lo = sb("attr_lo", [P, T])
        attr_hi = sb("attr_hi", [P, T])
        attr_atf = sb("attr_atf", [P, T])
        pool_at2 = sb("pool_at2", [P, 1], I32)
        ones_row = sb("ones_row", [1, P])
        rdeg = sb("rdeg", [P, T])
        rdeg1 = sb("rdeg1", [P, T])
        norm_in = sb("norm_in", [P, T])
        norm_out = sb("norm_out", [P, T])
        normtmp = sb("normtmp", [P, 2, T])
        slot_idx = sb("slot_idx", [P, 2, GB], I32)
        iota_i = sb("iota_i", [P, P], I32)
        iota_f = sb("iota_f", [P, P])
        part_i = sb("part_i", [P, 1], I32)
        part_f = sb("part_f", [P, 1])
        ident = sb("ident", [P, P])
        small = sb("small", [1, 8, T])
        small_i = sb("small_i", [1, 4, T + 1], I32)
        biasA = sb("biasA", [P, HID])
        biasB = sb("biasB", [P, HID])
        biasC = sb("biasC", [P, HID])
        mask = sb("mask", [P, 2, CAP])
        tmpw = sb("tmpw", [P, 2, CAP])
        sp_win = sb("sp_win", [P, 3 * SPW], I32)
        sp_rec = sb("sp_rec", [P, REC], I32)
        sp_run = sb("sp_run", [P, 2])
        sp_at = sb("sp_at", [P, 1], I32)
        sp_idx = sb("sp_idx", [P, 1], I32)
        sp_m = sb("sp_m", [P, 2, SPW])
        sp_f = sb("sp_f", [P, 4])
        sp_tile = sb("sp_tile", [P, T])
        sp_sum = sb("sp_sum", [P, DE])

        ps_T = [ctx.enter_context(nc.psum_tensor(f"ps_T{i}", [P, HID], F32)) for i in range(2)]
        ps_o = [ctx.enter_context(nc.psum_tensor(f"ps_o{i}", [P, HID], F32)) for i in range(5)]
        ps_m = ctx.enter_context(nc.psum_tensor("ps_m", [P, HID], F32))

        acc512 = acc[:, :].rearrange("p (t f) -> p t f", t=T)
        acc256 = acc[:, 0:T * D].rearrange("p (t f) -> p t f", t=T)
        Hflat = H[:, :, :].rearrange("p t f -> p (t f)")
        stage = G[:, :, :].rearrange("p b f -> p (b f)").rearrange("p (s f) -> p s f", s=2)
        w0 = wreg[:, 0:KD * R * D].rearrange("p (k n) -> p k n", k=KD)
        loopw = wreg[:, KD * R * D:KD * (R + 1) * D].rearrange("p (k n) -> p k n", k=KD)
        fold = [wreg[:, i * KH * HID:(i + 1) * KH * HID].rearrange("p (k n) -> p k n", k=KH) for i in range(3)]
        w_hp, w_y, w_v = fold
        wl2 = wreg[:, 0:KD * D].rearrange("p (k n) -> p k n", k=KD)
        wl3 = wreg[:, KD * D:KD * D + 3 * D].rearrange("p (k n) -> p k n", k=3)
        edge_i = acc[0:EP, 0:8 * EC].bitcast(I32).rearrange("p (a c) -> p a c", a=8)
        edge3 = acc[0:EP, 8 * EC:11 * EC]
        UPPER = T * D
        lo_hot = Hflat[0:EP, 0:HC * P].bitcast(BF16).rearrange("p (s c n) -> p s c n", s=2, n=P)
        hi_hot = Hflat[0:EP, HC * P:HC * P + HC * T].bitcast(BF16).rearrange("p (s c n) -> p s c n", s=2, n=T)
        iota_b = Hflat[:, 6400:6464].bitcast(BF16)
        hist = Hflat[0:T, 6528:7552].rearrange("p (a c) -> p a c", c=P)
        upper = Hflat[0:T, 7552:7552 + T]
        tot = Hflat[0:T, 7600:7602]
        node_rec_s = Hflat[:, 7700:7700 + 3 * T].bitcast(I32).rearrange("p (t c) -> p t c", c=3)
        cols = Hflat[:, 7850:7850 + 3 * T].rearrange("p (a t) -> p a t", a=3)
        i_tmp = Hflat[:, 8100:8100 + T].bitcast(I32)
        pos_f = Hflat[:, 8000:8000 + T]
        pos_i = Hflat[:, 8050:8050 + T].bitcast(I32)
        zeros = Hflat[:, 8192:8192 + R * D]
        key_row = acc[:, 11 * EC:11 * EC + NP]
        cmp_out = acc[:, 11 * EC + NP:11 * EC + 2 * NP]
        after_keys = 11 * EC + 2 * NP
        edge_b = acc[0:EP, after_keys:after_keys + 2 * EC].bitcast(BF16).rearrange("p (a c) -> p a c", a=4)
        src_counts = acc[0:T, after_keys + 2 * EC:after_keys + 2 * EC + P]
        assert after_keys > UPPER
        win = acc[:, 11 * EC:11 * EC + T * 3 * CAP].bitcast(I32).rearrange("p (t c) -> p t c", t=T)
        flat_in, flat_row, flat_row0 = [acc[:, 11 * EC + NP + k * UN * CAP:11 * EC + NP + (k + 1) * UN * CAP]
                                        .rearrange("p (t j) -> p t j", t=UN) for k in range(3)]
        attr_win = acc[:, UPPER:UPPER + CAP * DE]
        sp_attr = acc[:, UPPER:UPPER + SPW * DE]
        f_wfc = Hflat[:, 0:KH * D].rearrange("p (k n) -> p k n", k=KH)

        def fold_buf(i):
            a = KH * D + i * KH * HID
            return Hflat[:, a:a + KH * HID].rearrange("p (k n) -> p k n", k=KH)

        f_left, f_leftT, f_F, f_M, f_S = [fold_buf(i) for i in range(5)]
        f_row = Hflat[0:1, KH * D + 5 * KH * HID:KH * D + 5 * KH * HID + 2 * HID].rearrange("p (a n) -> p a n", a=2)
        f_bias = tile_in[:, :, :].rearrange("p s f -> p (s f)").rearrange("p (a k n) -> p a k n", a=2, k=KH)
        f_bcol = stats[:, 0:4, 0:4]

        ld = sems("ld", "edges x zero_x w0 loopw zero tail rec keys nodes x2 l2 l3")
        pr = sems("pr", "const hot hist sums carry key turned pos placed nodes norm x flat out_counts out_stored out_in")
        win_in = [sem(f"win_in{i}") for i in range(TI)]
        spb = sems("spb", "run dve window stored")
        ea = sems("ea", "at in step sum dve load window")
        fo = sems("fo", "turned lhs done out left right bias bcol")
        made = "in turned lhs mm"
        L = {"t0": sems("t0", f"{made} out kept sent0 sent1"), "tm": sems("tm", "out kept"),
             "thp": sems("thp", f"{made} out"), "ty": sems("ty", f"{made} out"),
             "tv": sems("tv", f"{made} out kept"), "tg": sems("tg", "out"),
             "t2": sems("t2", f"{made} out"), "t3": sems("t3", "out"), "ro": sems("ro", f"{made} out")}
        SENDERS = "tm thp tv tg t2 t3 ro".split()
        sent = [sem(f"sent{u}") for u in range(UN)]
        gather_in = [sem(f"gather_in{u}") for u in range(GB)]
        rows_in = [sem(f"rows_in{h}") for h in range(2)]
        acc_done = sem("acc_done")
        SPL = [sems(f"spl{n}", "dve load row") for n in range(7)]
        dve_chain = sem("dve_chain")
        act_chain = sem("act_chain")
        ln_var = sem("ln_var")
        ln_std = sem("ln_std")
        ln_ready = sem("ln_ready")
        passed = sem("passed")
        PER_PASS = GB + ROUNDS
        MARKS = 20
        mark = sb("mark", [1, MARKS])
        HOT0 = 3
        SPB_AT, SPB_PER = 2, 13
        EA_AT, EA_PER = 2, 9
        FOLD = [(w4s_in, [(f_wfc, f_F, 0, D)]),
                (w4n_in, [(f_wfc, f_F, D, D)]),
                (w3_in, [(f_F, f_M, 0, HID)]),
                (w2n_in, [(f_M, w_v, 0, HID)]),
                (w2s_in, [(f_M, f_S, 0, HID)]),
                (w1s_in, [(f_S, w_y, 0, HID), (f_F, w_hp, 0, HID)]),
                (w1n_in, [(f_S, w_y[:, KD:KH, :], 0, HID), (f_F, w_hp[:, KD:KH, :], 0, HID)])]
        FOLD_BIAS = {1: ((2, 3), [biasA]), 4: ((0, 1), [biasC, biasB])}
        FOLDED = sum(v.shape[0] // P * len(outs) for v, outs in FOLD) + 3

        class Chain:

            def __init__(self, eng, s):
                self.eng, self.sem, self.base, self.n = eng, s, 0, 0

            def __call__(self, ins):
                ins.then_inc(self.sem, 1)
                self.n += 1

            def sync(self):
                self.eng.wait_ge(self.sem, self.base + self.n)

            def link(self, ins):
                self(ins)
                self.sync()

        def w(eng, s, v):
            if not isinstance(v, int) or v > 0:
                eng.wait_ge(s, v)

        def apart(eng):
            eng.nop(nofuse=True)

        def loop(eng, n, body, chain=None, first=0, head=1, tail=0):
            start = chain.n if chain else 0
            for i in range(first, first + head):
                body(i)
            done = chain.n if chain else 0
            per = (done - start) // head if chain else 0
            at = first + head
            if n - tail > at:
                with eng.Fori(at, n - tail) as i:
                    if chain:
                        chain.base, chain.n = (i - at) * per + done, 0
                    body(i)
                    if chain:
                        assert chain.n == per
                if chain:
                    chain.base, chain.n = 0, done + (n - tail - at) * per
            for i in range(n - tail, n):
                body(i)

        def is_last(i, u):
            return isinstance(i, int) and i == TI - 1 and u == UN - 1

        def following(i, u):
            return (i, u + 1) if u + 1 < UN else (i + 1, 0)

        def with_next(now, ahead=None, before=None):
            def body(i):
                for u in range(UN):
                    more = not is_last(i, u)
                    j, v = following(i, u)
                    if before and more:
                        before(j, v)
                    if ahead and more and v:
                        ahead(j, v)
                    now(i, u)
                    if ahead and more and not v:
                        ahead(j, v)
            return body

        def slot_sent(eng, ph, i, u):
            if not (isinstance(i, int) and i == 0):
                eng.wait_ge(sent[u], 16 * (SENDERS.index(ph) * TI + i))

        def lag(u):
            return 1 if u == 0 else 2

        def slot_uses(i, u):
            if isinstance(i, int) and i == 0:
                return u
            return (i - 1) * USES[u % 2] + u // 2 + (UN if u % 2 == 0 else 0)

        block = ctx.enter_context(nc.Block())

        @block.sync
        def _(sp):
            for a, v in enumerate((dst_in, src_in, type_in)):
                sp.dma_start(edge_i[:, a, :], v.rearrange("(p c) -> p c", p=EP)).then_inc(ld["edges"], 16)
            sp.dma_start(edge_i[:, 3, :].bitcast(F32), weight_in.rearrange("(p c) -> p c", p=EP))\
                .then_inc(ld["edges"], 16)
            FT = N // P
            sp.dma_start(x[:, 0:FT, :], x_in[0:FT * P, :].rearrange("(t p) f -> p t f", p=P)).then_inc(ld["x"], 16)
            sp.wait_ge(ld["zero_x"], 1)
            sp.dma_start(x[0:N - FT * P, FT, :], x_in[FT * P:N, :]).then_inc(ld["x"], 16)
            for r in range(R):
                sp.dma_start(w0[:, :, r * D:(r + 1) * D], w0_in[r].rearrange("(k p) n -> p k n", p=P))\
                    .then_inc(ld["w0"], 16)
            sp.dma_start(loopw, loop_in.rearrange("(k p) n -> p k n", p=P)).then_inc(ld["w0"], 16)
            sp.dma_start(biasA[:, 0:D], b0_in.rearrange("(a n) -> a n", a=1).to_broadcast([P, D]))\
                .then_inc(ld["w0"], 16)
            sp.wait_ge(pr["const"], 8)
            for table, width in ((table0, R * D), (table_h, D), (table_hp, HID), (table_y, HID),
                                 (table_g, D), (table_2, D), (table_3, D)):
                sp.dma_start(table[NP:NP + 1, :], zeros[0:1, 0:width]).then_inc(ld["zero"], 16)
            sp.dma_start(edge_rec[3 * E:3 * (E + CAP)].rearrange("(a n) -> a n", a=1),
                         zeros[0:1, 0:3 * CAP].bitcast(I32)).then_inc(ld["tail"], 16)
            sp.wait_ge(pr["hot"], 3)
            sp.dma_start(edge_rec[0:3 * E].rearrange("(p c) -> p c", p=EP), edge3.bitcast(I32)).then_inc(ld["rec"], 16)
            sp.wait_ge(pr["key"], 1)
            sp.dma_start(key_dram[:].rearrange("(h l) -> h l", l=P), hist[:, 4, :]).then_inc(ld["keys"], 16)
            sp.wait_ge(ld["keys"], 16)
            sp.dma_start(key_row, key_dram[:].rearrange("(a n) -> a n", a=1).to_broadcast([P, NP]))\
                .then_inc(ld["keys"], 16)
            sp.wait_ge(pr["placed"], 16 * T)
            sp.dma_start(recs[:, :, :], node_rec[:, :].rearrange("(t p) c -> p t c", p=P)).then_inc(ld["nodes"], 16)

            sp.wait_ge(L["t0"]["kept"], T)
            sp.dma_start(table_x[:, :].rearrange("(t p) f -> p t f", p=P), x[:, :, :]).then_inc(ld["x2"], 16)

            def row_numbers(n):
                kind = 1 if n == 0 else 0

                def body(i):
                    for h in range(2):
                        w(sp, acc_done, n * PER_PASS + i * 2 * GB + h * GB)
                        sp.dma_start(slot_idx[:, h, :], idx[:, kind, bass.ds(i * 2 * GB + h * GB, GB)])\
                            .then_inc(rows_in[h], 16)
                loop(sp, RI, body)

            sp.wait_ge(pr["flat"], TI)
            for n in range(7):
                row_numbers(n)
                if n == 0:
                    sp.wait_ge(pr["out_counts"], 1)
                    sp.dma_start(out_dram[:].rearrange("(h l) -> h l", l=P), src_counts).then_inc(pr["out_stored"], 16)
                if n == 2:
                    sp.wait_ge(L["ty"]["mm"], T)
                    sp.dma_start(wl2[:, :, :], wl2_in.rearrange("(k p) n -> p k n", p=P)).then_inc(ld["l2"], 16)
                    sp.dma_start(wl3[:, 0:KD, :], wl3_in[0:D, :].rearrange("(k p) n -> p k n", p=P)).then_inc(ld["l3"], 16)
                    sp.dma_start(wl3[0:DE, KD, :], wl3_in[D:D + DE, :]).then_inc(ld["l3"], 16)
                    sp.dma_start(biasC[:, 0:D], bl3_in.rearrange("(a n) -> a n", a=1).to_broadcast([P, D]))\
                        .then_inc(ld["l3"], 16)

        @block.gpsimd
        def _(po):
            po.memset(x[:, T - 1, :], 0.0).then_inc(ld["zero_x"], 1)
            po.iota(iota_i[:, :], pattern=[[1, P]], base=0, channel_multiplier=0).then_inc(pr["const"], 1)
            po.iota(part_i[:, :], pattern=[[0, 1]], base=0, channel_multiplier=1).then_inc(pr["const"], 1)
            po.memset(ident[:, :], 0.0).then_inc(pr["const"], 1)
            po.memset(zeros, 0.0).then_inc(pr["const"], 1)
            po.memset(ones_row[:, :], 1.0).then_inc(pr["const"], 1)
            po.memset(upper, 1.0).then_inc(pr["const"], 1)
            po.wait_ge(pr["const"], 6)
            po.affine_select(out=ident[:, :], in_=ident[:, :], compare_op=ALU.not_equal, fill=1.0,
                             base=0, pattern=[[-1, P]], channel_multiplier=1).then_inc(pr["const"], 1)
            po.affine_select(out=upper, in_=upper, compare_op=ALU.is_gt, fill=0.0,
                             base=0, pattern=[[1, T]], channel_multiplier=-1).then_inc(pr["const"], 1)
            po.wait_ge(pr["pos"], 1)
            for t in range(T):
                po.indirect_dma_start(out=node_rec[:, :], out_offset=bass.IndirectOffsetOnAxis(ap=pos_i[:, t:t + 1], axis=0),
                                      in_=node_rec_s[:, t, :], in_offset=None).then_inc(pr["placed"], 16)
            po.wait_ge(pr["nodes"], 1)
            po.wait_ge(ld["rec"], 16)
            po.wait_ge(ld["tail"], 16)
            po.wait_ge(ld["zero"], 16 * 7)
            rec_row = edge_rec[:].rearrange("(a n) -> a n", a=1)
            attr_row = attr_in.rearrange("(a n) c -> a (n c)", a=1)

            for t in range(T):
                po.indirect_dma_start(out=win[:, t, :], out_offset=None, in_=rec_row,
                                      in_offset=bass.IndirectOffsetOnAxis(ap=win_at[:, t:t + 1], axis=1))\
                    .then_inc(win_in[t // UN], 16)
            po.wait_ge(pr["flat"], TI)

            q_total = po.value_load(small_i[0:1, 3, 0:1], min_val=0, max_val=SPILLS)
            with po.If(q_total):
                with po.Fori(0, T) as t:
                    n = po.value_load(small_i[0:1, 1, bass.ds(t, 1)], min_val=0, max_val=SPILLS)
                    first = po.value_load(small_i[0:1, 2, bass.ds(t, 1)], min_val=0, max_val=SPILLS)
                    with po.If(n):
                        with po.Fori(0, n) as j:
                            q = nc.s_assert_within(po.snap(first + j), 0, SPILLS - 1, skip_runtime_bounds_check_because="the windows counted by this program are below their bound")
                            po.wait_ge(spb["dve"], 1 + SPB_PER * q + SPB_AT)
                            apart(po)
                            po.indirect_dma_start(out=sp_win[:, :], out_offset=None, in_=rec_row,
                                                  in_offset=bass.IndirectOffsetOnAxis(ap=sp_at[:, :], axis=1))\
                                .then_inc(spb["window"], 16)
                            po.wait_ge(spb["dve"], 1 + SPB_PER * q + SPB_PER)
                            po.dma_start(spill[bass.ds(q, 1), :, :].rearrange("q p c -> p (q c)"), sp_rec[:, :])\
                                .then_inc(spb["stored"], 16)
                            po.wait_ge(spb["stored"], q * 16 + 16)

            def scatter(ph, table, width, **bound):
                for t in range(T):
                    po.wait_ge(L[ph]["out"], t + 1)
                    po.indirect_dma_start(out=table, out_offset=bass.IndirectOffsetOnAxis(ap=node_of[:, t:t + 1], axis=0),
                                          in_=G[:, t % UN, 0:width], in_offset=None, **bound).then_inc(sent[t % UN], 16)
                for u in range(UN):
                    po.wait_ge(sent[u], 16 * TI * (SENDERS.index(ph) + 1))

            def gathers(n, table, width):
                def body(i):
                    for h in range(2):
                        if n == 1 and h and (not isinstance(i, int) or 1 <= i <= T):
                            w(po, ea["sum"], i - 1)
                            po.tensor_copy(pool_at2[:, :], attr_at[:, bass.ds(i - 1, 1)]).then_inc(ea["at"], 1)
                            po.wait_ge(ea["at"], i)
                            apart(po)
                            po.indirect_dma_start(out=attr_win, out_offset=None, in_=attr_row,
                                                  in_offset=bass.IndirectOffsetOnAxis(ap=pool_at2[:, :], axis=1))\
                                .then_inc(ea["in"], 16)
                        po.wait_ge(rows_in[h], (n * RI + i + 1) * 16)
                        for u in range(GB):
                            po.wait_ge(acc_done, n * PER_PASS + i * 2 * GB + h * GB + u + 1)
                            apart(po)
                            po.indirect_dma_start(out=G[:, u, 0:width], out_offset=None, in_=table,
                                                  in_offset=bass.IndirectOffsetOnAxis(ap=slot_idx[:, h, u:u + 1], axis=0))\
                                .then_inc(gather_in[u], 16)
                loop(po, RI, body, head=2, tail=RI - 1 - T)
                S = SPL[n]
                with po.If(q_total):
                    with po.Fori(0, q_total) as q:
                        po.wait_ge(S["dve"], q * (2 * SPW) + 1)
                        po.dma_start(sp_rec[:, :], spill[bass.ds(q, 1), :, :].rearrange("q p c -> p (q c)"))\
                            .then_inc(S["load"], 16)
                        with po.Fori(0, SPW) as j:
                            po.wait_ge(S["dve"], (q * SPW + j) * 2 + 2)
                            apart(po)
                            po.indirect_dma_start(out=G[:, 0, 0:width], out_offset=None, in_=table,
                                                  in_offset=bass.IndirectOffsetOnAxis(ap=sp_idx[:, :], axis=0))\
                                .then_inc(S["row"], 16)

            def spill_attributes():
                with po.If(q_total):
                    with po.Fori(0, q_total) as q:
                        po.wait_ge(ea["dve"], q * EA_PER + 1)
                        po.dma_start(sp_rec[:, :], spill[bass.ds(q, 1), :, :].rearrange("q p c -> p (q c)"))\
                            .then_inc(ea["load"], 16)
                        po.wait_ge(ea["dve"], q * EA_PER + 1 + EA_AT)
                        apart(po)
                        po.indirect_dma_start(out=sp_attr, out_offset=None, in_=attr_row,
                                              in_offset=bass.IndirectOffsetOnAxis(ap=sp_at[:, :], axis=1))\
                            .then_inc(ea["window"], 16)

            po.wait_ge(ld["x2"], 16)
            for t in range(T):
                po.indirect_dma_start(out=x[:, t, :], out_offset=None, in_=table_x[:, :],
                                      in_offset=bass.IndirectOffsetOnAxis(ap=node_of[:, t:t + 1], axis=0))\
                    .then_inc(pr["x"], 16)
            po.wait_ge(L["t0"]["sent0"], 16 * (UN + (TI - 1) * USES[0]))
            po.wait_ge(L["t0"]["sent1"], 16 * (TI - 1) * USES[1])
            gathers(0, table0[:, :].rearrange("n (r f) -> (n r) f", r=R), D)
            for ph, n, table, width in (("tm", 1, table_h, D), ("thp", 2, table_hp, HID), ("tv", 3, table_y, HID),
                                        ("tg", 4, table_g, D), ("t2", 5, table_2, D), ("t3", 6, table_3, D)):
                if n == 2:
                    po.wait_ge(pr["out_stored"], 16)
                    for t in range(T):
                        po.indirect_dma_start(out=outdeg[:, t:t + 1], out_offset=None, in_=out_dram[:].rearrange("(n a) -> n a", a=1),
                                              in_offset=bass.IndirectOffsetOnAxis(ap=node_of[:, t:t + 1], axis=0))\
                            .then_inc(pr["out_in"], 16)
                scatter(ph, table[:, :], width)
                gathers(n, table[:, :], width)
                if n == 1:
                    spill_attributes()
            scatter("ro", out, D, bounds_check=N - 1, oob_is_err=False)

        @block.scalar
        def _(act):
            ch = Chain(act, act_chain)

            def roots(n):
                act.wait_ge(ln_var, n + 1)
                act.activation(std[:, :], std[:, :], ACT.Sqrt).then_inc(ln_std, 1)

            def tile_turned(S, T_, s):
                act.wait_ge(S["turned"], T_ + 1)
                act.activation(tile_T[:, s, :], ps_T[s][:, :], ACT.Copy).then_inc(S["lhs"], 1)

            roots(0)
            S = L["t0"]
            act.wait_ge(ln_ready, 1)

            def go_in(i, u, tile=None, ago=None):
                T_ = i * UN + u if tile is None else tile
                w(act, S["turned"], T_ + 1 - (ago or lag(u)))
                apart(act)
                act.activation(tile_in[:, u % 2, 0:D], x[:, T_, :], ACT.Relu, bias=nmr[:, bass.ds(T_, 1)],
                               scale=rstd[:, bass.ds(T_, 1)]).then_inc(S["in"], 1)

            def turned0(i, u, tile=None, ago=None):
                T_ = i * UN + u if tile is None else tile
                w(act, S["mm"], (T_ + 1 - (ago or lag(u))) * 5)
                act.wait_ge(S["turned"], T_ + 1)
                act.activation(tile_T[:, u % 2, 0:D], ps_T[u % 2][:, 0:D], ACT.Copy).then_inc(S["lhs"], 1)

            def rows_out(i, u, tile=None):
                T_ = i * UN + u if tile is None else tile
                s = u % 2
                w(act, S[f"sent{s}"], (slot_uses(i, u) if tile is None else tile) * 16)
                for c in range(4):
                    act.wait_ge(S["mm"], T_ * 5 + c + 1)
                    act.activation(stage[:, s, c * HID:(c + 1) * HID], ps_o[c][:, :], ACT.Copy).then_inc(S["out"], 1)
                act.wait_ge(S["mm"], T_ * 5 + 5)
                apart(act)
                act.activation(x[:, T_, :], ps_o[4][:, 0:D], ACT.Copy).then_inc(S["kept"], 1)
                act.wait_ge(S["out"], T_ * 4 + 4)
                apart(act)
                act.dma_start(table0[bass.ds(T_ * P, P), :], stage[:, s, :]).then_inc(S[f"sent{s}"], 16)

            def first_tiles(t):
                go_in(0, 0, t, 1)
                turned0(0, 0, t, 1)
                rows_out(0, 0, t)
            loop(act, UN, first_tiles)
            go_in(1, 0)
            turned0(1, 0)
            loop(act, TI, with_next(rows_out, turned0, go_in), first=1, tail=1)

            act.wait_ge(pr["out_counts"], 1)
            act.wait_ge(ld["zero"], 16 * 7)
            act.dma_start(f_wfc, wfc_in.rearrange("(k p) n -> p k n", p=P)).then_inc(fo["right"], 16)
            for a, v in enumerate((b1_in, b2_in, b3_in, b4_in)):
                act.dma_start(f_bcol[:, a, :], v.rearrange("(k p) -> p k", p=P), allow_slow_non_contiguous=True).then_inc(fo["bias"], 16)
            act.dma_start(f_row[0:1, 0, 0:D], bfc_in.rearrange("(a n) -> a n", a=1)).then_inc(fo["bias"], 16)
            act.dma_start(f_row[0:1, 1, :], bp_in.rearrange("(a n) -> a n", a=1)).then_inc(fo["bias"], 16)
            turned, done = 0, 0
            for n, (v, outs) in enumerate(FOLD):
                rows = v.shape[0]
                if n:
                    act.wait_ge(fo["turned"], turned)
                act.dma_start(f_left[:, 0:rows // P, :], v.rearrange("(m p) k -> p m k", p=P)).then_inc(fo["left"], 16)
                for k in range(KH):
                    act.wait_ge(fo["turned"], turned + 1)
                    if n and k == 0:
                        act.wait_ge(fo["done"], done)
                    act.activation(f_leftT[:, k, 0:rows], ps_T[k % 2][:, 0:rows], ACT.Copy).then_inc(fo["lhs"], 1)
                    turned += 1
                for (_, dest, lo, width) in outs:
                    for m in range(rows // P):
                        done += 1
                        act.wait_ge(fo["done"], done)
                        act.activation(dest[:, m, lo:lo + width], ps_o[m][:, 0:width], ACT.Copy).then_inc(fo["out"], 1)
                if n in FOLD_BIAS:
                    pair, dests = FOLD_BIAS[n]
                    if n == 4:
                        act.wait_ge(fo["turned"], turned)
                    act.wait_ge(fo["bias"], 16 * 6)
                    for a, b in enumerate(pair):
                        for k in range(KH):
                            act.activation(f_bias[:, a, k, :], f_bcol[:, b, k:k + 1].to_broadcast([P, P]), ACT.Copy)\
                                .then_inc(fo["bcol"], 1)
                    if n == 4:
                        act.dma_start(f_F, wp_in.rearrange("(k p) n -> p k n", p=P)).then_inc(fo["right"], 16)
                    for dest in dests:
                        done += 1
                        act.wait_ge(fo["done"], done)
                        act.activation(dest[:, :], ps_m[:, :], ACT.Copy).then_inc(fo["out"], 1)

            roots(1)
            S = L["tm"]
            act.wait_ge(ln_ready, 2)

            def rows_h(i):
                for u in range(UN):
                    T_ = i * UN + u
                    slot_sent(act, "tm", i, u)
                    apart(act)
                    act.activation(G[:, u, 0:D], x[:, T_, :], ACT.Relu, bias=nmr[:, bass.ds(T_, 1)],
                                   scale=rstd[:, bass.ds(T_, 1)]).then_inc(S["out"], 1)
                    act.activation(H[:, T_, 0:D], x[:, T_, :], ACT.Relu, bias=nmr[:, bass.ds(T_, 1)],
                                   scale=rstd[:, bass.ds(T_, 1)]).then_inc(S["kept"], 1)
            loop(act, TI, rows_h)

            S = L["thp"]
            act.wait_ge(passed, 2)

            def pool_tiles(i):
                for u in range(UN):
                    T_, s = i * UN + u, u % 2
                    w(act, S["turned"], T_ + 1 - lag(u))
                    apart(act)
                    act.activation(tile_in[:, s, :], H[:, T_, :], ACT.Copy).then_inc(S["in"], 1)
            loop(act, TI, pool_tiles)

            S = L["ty"]
            act.wait_ge(L["thp"]["mm"], T)

            def y_in(i, u):
                w(act, S["turned"], i * UN + u + 1 - lag(u))
                apart(act)
                act.activation(tile_in[:, u % 2, :], H[:, i * UN + u, :], ACT.Copy).then_inc(S["in"], 1)

            def y_turned(i, u):
                w(act, S["mm"], i * UN + u + 1 - lag(u))
                tile_turned(S, i * UN + u, u % 2)

            def y_out(i, u):
                act.wait_ge(S["mm"], i * UN + u + 1)
                apart(act)
                act.activation(H[:, i * UN + u, :], ps_o[u][:, :], ACT.Copy).then_inc(S["out"], 1)
            y_in(0, 0)
            y_turned(0, 0)
            loop(act, TI, with_next(y_out, y_turned, y_in), tail=1)

            S = L["tv"]
            act.wait_ge(passed, 3)

            def max_in(i, u):
                w(act, S["turned"], i * UN + u + 1 - lag(u))
                apart(act)
                act.activation(tile_in[:, u % 2, :], acc512[:, i * UN + u, :], ACT.Copy).then_inc(S["in"], 1)

            def y_rows_out(i, u):
                slot_sent(act, "tv", i, u)
                act.wait_ge(S["kept"], i * UN + u + 1)
                apart(act)
                act.activation(G[:, u, :], H[:, i * UN + u, :], ACT.Copy).then_inc(S["out"], 1)
            max_in(0, 0)
            loop(act, TI, with_next(y_rows_out, before=max_in), tail=1)

            act.wait_ge(pr["norm"], 1)
            act.activation(normtmp[:, :, :], normtmp[:, :, :], ACT.Sqrt).then_inc(pr["norm"], 1)
            roots(2)
            S = L["t2"]
            act.wait_ge(ln_ready, 3)

            def in2(i, u):
                T_ = i * UN + u
                w(act, S["turned"], T_ + 1 - lag(u))
                apart(act)
                act.activation(tile_in[:, u % 2, 0:D], x[:, T_, :], ACT.Relu, bias=nmr[:, bass.ds(T_, 1)],
                               scale=rstd[:, bass.ds(T_, 1)]).then_inc(S["in"], 1)

            def out2(i, u):
                slot_sent(act, "t2", i, u)
                act.wait_ge(S["mm"], i * UN + u + 1)
                act.activation(G[:, u, 0:D], ps_o[u][:, 0:D], ACT.Copy).then_inc(S["out"], 1)
            in2(0, 0)
            loop(act, TI, with_next(out2, before=in2), tail=1)

            roots(3)
            S = L["t3"]
            act.wait_ge(ln_ready, 4)

            def rows3(i):
                for u in range(UN):
                    T_ = i * UN + u
                    slot_sent(act, "t3", i, u)
                    apart(act)
                    act.activation(G[:, u, 0:D], x[:, T_, :], ACT.Relu, bias=nmr[:, bass.ds(T_, 1)],
                                   scale=rstd[:, bass.ds(T_, 1)]).then_inc(S["out"], 1)
            loop(act, TI, rows3)

            S = L["ro"]
            act.wait_ge(passed, 7)

            def last_tiles(i):
                for u in range(UN):
                    T_, s = i * UN + u, u % 2
                    w(act, S["turned"], T_ + 1 - lag(u))
                    apart(act)
                    act.activation(tile_in[:, s, 0:D], acc256[:, T_, :], ACT.Copy).then_inc(S["in"], 1)
                    act.activation(tile_in[:, s, D:D + DE], attr_sum[:, T_, :], ACT.Copy).then_inc(S["in"], 1)
            loop(act, TI, last_tiles)

        @block.tensor
        def _(pe):
            pe.wait_ge(pr["const"], 8)

            def turn(S, T_, s, widths, n_in=1):
                pe.wait_ge(S["in"], (T_ + 1) * n_in)
                for k, width in enumerate(widths):
                    mm = pe.transpose(ps_T[s][0:width, k * P:(k + 1) * P], tile_in[:, s, k * P:k * P + width], ident[:, :])
                mm.then_inc(S["turned"], 1)

            def count(step, s, first):
                pe.wait_ge(pr["hot"], HOT0 + step * 2 + 2)
                for c in range(HC):
                    mm = pe.matmul(ps_m[0:T, 0:P], hi_hot[:, s, c, :], lo_hot[:, s, c, :],
                                   start=first and c == 0, stop=c == HC - 1, skip_group_check=True)
                mm.then_inc(pr["hist"], 1)

            S = L["t0"]

            def turn0(i, u, tile=None, ago=None):
                T_ = i * UN + u if tile is None else tile
                w(pe, S["lhs"], T_ + 1 - (ago or lag(u)))
                turn(S, T_, u % 2, [P] * KD)

            def multiply0(i, u, tile=None):
                T_ = i * UN + u if tile is None else tile
                s = u % 2
                pe.wait_ge(S["lhs"], T_ + 1)
                for c in range(4):
                    w(pe, S["out"], (T_ - 1) * 4 + c + 1)
                    for k in range(KD):
                        mm = pe.matmul(ps_o[c][:, :], tile_T[:, s, k * P:(k + 1) * P], w0[:, k, c * HID:(c + 1) * HID],
                                       start=k == 0, stop=k == KD - 1)
                    mm.then_inc(S["mm"], 1)
                w(pe, S["kept"], T_)
                for k in range(KD):
                    pe.matmul(ps_o[4][:, 0:D], tile_T[:, s, k * P:(k + 1) * P], loopw[:, k, :], start=k == 0, stop=False)
                pe.matmul(ps_o[4][:, 0:D], ident[:, :], x[:, T_, :], start=False, stop=True).then_inc(S["mm"], 1)

            def first_tiles(t):
                turn0(0, 0, t, 1)
                for s in range(2):
                    count(t * 2 + s, s, isinstance(t, int) and s == 0)
                if isinstance(t, int):
                    pe.wait_ge(ld["loopw"], 1)
                multiply0(0, 0, t)
            loop(pe, UN, first_tiles)
            pe.wait_ge(pr["sums"], 1)
            pe.matmul(ps_m[0:T, 0:2], upper, tot, start=True, stop=True).then_inc(pr["carry"], 1)
            pe.wait_ge(pr["key"], 1)
            for a, row in enumerate((0, 3, 4)):
                mm = pe.transpose(ps_m[:, P + a * 32:P + a * 32 + T], hist[:, row, :], ident[0:T, 0:T])
            mm.then_inc(pr["turned"], 1)
            turn0(1, 0)
            loop(pe, TI, with_next(multiply0, before=turn0), first=1, tail=1)
            pe.wait_ge(S["out"], 4 * T)
            pe.wait_ge(S["kept"], T)

            def count_src(i):
                count(HS + i, 0, isinstance(i, int))
            loop(pe, HS, count_src)
            pe.wait_ge(pr["out_counts"], 1)

            turned, out_n, bcol = 0, 0, 0
            pe.wait_ge(fo["right"], 16)
            for n, (v, outs) in enumerate(FOLD):
                rows = v.shape[0]
                pe.wait_ge(fo["left"], 16 * (n + 1))
                for k in range(KH):
                    if turned >= 2:
                        pe.wait_ge(fo["lhs"], turned - 1)
                    for m in range(rows // P):
                        mm = pe.transpose(ps_T[k % 2][:, m * P:(m + 1) * P], f_left[:, m, k * P:(k + 1) * P], ident[:, :])
                    mm.then_inc(fo["turned"], 1)
                    turned += 1
                pe.wait_ge(fo["lhs"], turned)
                for (right, _, _, width) in outs:
                    if out_n:
                        pe.wait_ge(fo["out"], out_n)
                    if right is f_F and n >= 5:
                        pe.wait_ge(fo["right"], 32)
                    for m in range(rows // P):
                        for k in range(KH):
                            mm = pe.matmul(ps_o[m][:, 0:width], f_leftT[:, k, m * P:(m + 1) * P], right[:, k, 0:width],
                                           start=k == 0, stop=k == KH - 1)
                        mm.then_inc(fo["done"], 1)
                        out_n += 1
                if n in FOLD_BIAS:
                    bcol += 2 * KH
                    pe.wait_ge(fo["bcol"], bcol)
                    pe.wait_ge(fo["out"], out_n)

                    def add(a, right, width, first, last=False):
                        for k in range(KH):
                            mm = pe.matmul(ps_m[:, 0:width], f_bias[:, a, k, :], right[:, k, 0:width],
                                           start=first and k == 0, stop=last and k == KH - 1, skip_group_check=True)
                        return mm

                    def add_row(r, width):
                        return pe.matmul(ps_m[:, 0:width], ones_row[:, :], f_row[0:1, r, 0:width],
                                         start=False, stop=True, skip_group_check=True)
                    if n == 1:
                        add(0, f_F, HID, True)
                        add(1, f_wfc, D, False)
                        add_row(0, D).then_inc(fo["done"], 1)
                        out_n += 1
                    else:
                        add(0, f_S, HID, True)
                        add(1, f_M, HID, False, True).then_inc(fo["done"], 1)
                        out_n += 1
                        pe.wait_ge(fo["out"], out_n)
                        pe.wait_ge(fo["right"], 32)
                        add(0, f_F, HID, True)
                        add_row(1, HID).then_inc(fo["done"], 1)
                        out_n += 1

            def product(ph, widths, weights, wide, lhs_per=1, n_in=1, row=None, free="out"):
                S = L[ph]

                def turn_next(i, u):
                    w(pe, S["lhs"], (i * UN + u + 1 - lag(u)) * lhs_per)
                    turn(S, i * UN + u, u % 2, widths, n_in)

                def multiply(i, u):
                    T_, s = i * UN + u, u % 2
                    pe.wait_ge(S["lhs"], (T_ + 1) * lhs_per)
                    w(pe, S[free], T_ + 1 - UN)
                    for k, width in enumerate(widths):
                        mm = pe.matmul(ps_o[u][:, 0:wide], tile_T[0:width, s, k * P:(k + 1) * P], weights[0:width, k, :],
                                       start=k == 0, stop=row is None and k == len(widths) - 1)
                    if row is not None:
                        mm = pe.matmul(ps_o[u][:, 0:wide], ones_row[:, :], row, start=False, stop=True)
                    mm.then_inc(S["mm"], 1)
                turn_next(0, 0)
                loop(pe, TI, with_next(multiply, before=turn_next), tail=1)
                pe.wait_ge(S[free], T)

            pe.wait_ge(fo["out"], out_n)
            product("thp", [P] * KH, w_hp, HID)
            product("ty", [P] * KH, w_y, HID, row=biasC[0:1, :])
            product("tv", [P] * KH, w_v, HID, free="kept")
            pe.wait_ge(ld["l2"], 16)
            product("t2", [P] * KD, wl2, D)
            pe.wait_ge(ld["l3"], 48)
            product("ro", [P] * KD + [DE], wl3, D, lhs_per=2, n_in=2)

        @block.vector
        def _(ve):
            ch = Chain(ve, dve_chain)
            marks = (mark[:, k:k + 1] for k in range(MARKS))
            bc = lambda a, n: a.unsqueeze(2).to_broadcast([a.shape[0], a.shape[1], n])
            ve.wait_ge(pr["const"], 8)
            ch(ve.tensor_copy(iota_f[:, :], iota_i[:, :]))
            ch(ve.tensor_copy(part_f[:, :], part_i[:, :]))
            ch(ve.tensor_copy(iota_b, iota_i[:, :]))
            ch(ve.memset(idx[:, 0, :], ZROW))
            ch(ve.memset(idx[:, 1, :], ZROW * R))
            ch(ve.memset(wt[:, :], 0.0))
            ch(ve.memset(round_tile[:, :], T - 1))
            ch(ve.memset(attr_sum[:, :, :], 0.0))
            ve.wait_ge(ld["edges"], 64)
            for a in range(2):
                ch(ve.tensor_scalar(edge_i[:, 4 + 2 * a, :], edge_i[:, a, :], P - 1, None, ALU.bitwise_and))
                ch(ve.tensor_scalar(edge_i[:, 5 + 2 * a, :], edge_i[:, a, :], 7, None, ALU.logical_shift_right))
            ch.sync()
            ch.link(ve.tensor_copy(edge_b, edge_i[:, 4:8, :]))
            e3 = edge3.rearrange("p (c r) -> p c r", r=3)
            e3i = edge3.bitcast(I32).rearrange("p (c r) -> p c r", r=3)
            ve.tensor_copy(e3i[:, :, 0], edge_i[:, 1, :]).then_inc(pr["hot"], 1)
            ve.scalar_tensor_tensor(out=e3i[:, :, 1], in0=edge_i[:, 1, :], scalar=float(R), in1=edge_i[:, 2, :],
                                    op0=ALU.mult, op1=ALU.add).then_inc(pr["hot"], 1)
            ve.tensor_copy(e3[:, :, 2], edge_i[:, 3, :].bitcast(F32)).then_inc(pr["hot"], 1)
            def layer_norm(n):
                def sums(i):
                    for u in range(UN):
                        ch(ve.bn_stats(stats[:, i * UN + u, :], x[:, i * UN + u, :]))
                loop(ve, TI, sums, ch)
                ch.sync()

                for t in range(T):
                    ch(ve.bn_aggr(mv[:, t, :], stats[:, t, :]))
                ch.sync()
                ve.tensor_scalar(std[:, :], mv[:, :, 1], EPS, None, ALU.add).then_inc(ln_var, 1)
                ve.wait_ge(ln_std, n + 1)
                ch.link(ve.reciprocal(rstd[:, :], std[:, :]))
                if n == 3:
                    ch.link(ve.tensor_tensor(rstd[:, :], rstd[:, :], norm_out[:, :], ALU.mult))
                ve.scalar_tensor_tensor(out=nmr[:, :], in0=mv[:, :, 0], scalar=-1.0, in1=rstd[:, :],
                                        op0=ALU.mult, op1=ALU.mult).then_inc(ln_ready, 1)

            ve.wait_ge(ld["x"], 32)
            layer_norm(0)
            ve.wait_ge(ld["w0"], 16 * (R + 2))
            ve.tensor_scalar(loopw, loopw, HALF, None, ALU.mult).then_inc(ld["loopw"], 1)
            def hot(a, step, s):
                at = bass.ds(step * HC, HC)
                ve.tensor_tensor(lo_hot[:, s, :, :], bc(edge_b[:, 2 * a, at], P),
                                 iota_b[0:EP, :].unsqueeze(1).to_broadcast([EP, HC, P]), ALU.is_equal)\
                    .then_inc(pr["hot"], 1)
                ve.tensor_tensor(hi_hot[:, s, :, :], bc(edge_b[:, 2 * a + 1, at], T),
                                 iota_b[0:EP, 0:T].unsqueeze(1).to_broadcast([EP, HC, T]), ALU.is_equal)\
                    .then_inc(pr["hot"], 1)

            def hot_dst(i):
                for s in range(2):
                    w(ve, pr["hist"], i * 2 + s - 1)
                    hot(0, i * 2 + s, s)
            loop(ve, HS // 2, hot_dst)
            ve.wait_ge(pr["hist"], HS)
            ch.link(ve.tensor_copy(hist[:, 0, :], ps_m[0:T, 0:P]))
            ch(ve.memset(hist[:, 6, :], 1.0))
            ch(ve.memset(tot, 0.0))
            ch.link(ve.tensor_scalar(hist[:, 5, :], hist[:, 0, :], 4095.0, 4096.0, ALU.min, ALU.mult))
            ch.link(ve.tensor_tensor_scan(hist[:, 2, :], hist[:, 6, :], hist[:, 0, :], 0.0, ALU.mult, ALU.add))
            ve.tensor_copy(tot[:, 0:1], hist[:, 2, P - 1:P]).then_inc(pr["sums"], 1)
            ch(ve.tensor_scalar(sp_f[0:T, 0:1], part_f[0:T, :], -float(P), 4095.0, ALU.mult, ALU.add))
            ch.link(ve.tensor_tensor(hist[:, 3, :], hist[:, 2, :], hist[:, 0, :], ALU.subtract))
            ch.link(ve.scalar_tensor_tensor(out=hist[:, 7, :], in0=hist[:, 5, :], scalar=sp_f[0:T, 0:1],
                                            in1=iota_f[0:T, :], op0=ALU.add, op1=ALU.subtract))
            ve.wait_ge(pr["carry"], 1)
            ch.link(ve.tensor_scalar(hist[:, 3, :], hist[:, 3, :], ps_m[0:T, 0:1], None, ALU.add))
            ve.tensor_copy(hist[:, 4, :], hist[:, 7, :]).then_inc(pr["key"], 1)
            ve.wait_ge(pr["turned"], 1)
            for a in range(3):
                ch(ve.tensor_copy(cols[:, a, :], ps_m[:, P + a * 32:P + a * 32 + T]))
            ch.sync()
            ve.wait_ge(ld["keys"], 32)
            for t in range(T):
                ch.link(ve.tensor_scalar(cmp_out, key_row, cols[:, 2, t:t + 1], None, ALU.is_gt, ALU.add,
                                         accum_out=pos_f[:, t:t + 1]))
            ch(ve.tensor_copy(node_rec_s[:, :, 1], cols[:, 0, :]))
            ch(ve.tensor_copy(node_rec_s[:, :, 2], cols[:, 1, :]))
            ch(ve.tensor_scalar(node_rec_s[:, :, 0], iota_f[:, 0:T], float(P), part_f[:, :], ALU.mult, ALU.add))
            ch.sync()
            ve.tensor_copy(pos_i, pos_f).then_inc(pr["pos"], 1)

            ve.wait_ge(ld["nodes"], 16)
            ch(ve.tensor_copy(node_of[:, :], recs[:, :, 0]))
            ch(ve.tensor_copy(degf[:, :], recs[:, :, 1]))
            ch(ve.tensor_copy(startf[:, :], recs[:, :, 2]))
            ch.link(ve.tensor_scalar(win_at[:, :], recs[:, :, 2], 3.0, None, ALU.mult))
            ve.tensor_scalar(attr_atf[:, :], recs[:, :, 2], float(E - CAP), None, ALU.min).then_inc(pr["nodes"], 1)
            deg0 = degf[0:1, :]
            ch(ve.memset(small[:, 0, :], 1.0))
            ch(ve.tensor_scalar(small[:, 1, :], deg0, float(CAP), None, ALU.min))
            ch.link(ve.tensor_scalar(small[:, 3, :], deg0, -float(CAP), 0.0, ALU.add, ALU.max))
            ch(ve.tensor_tensor_scan(small[:, 2, :], small[:, 0, :], small[:, 1, :], 0.0, ALU.mult, ALU.add))
            ch.link(ve.tensor_scalar(small_i[:, 3, 0:T], small[:, 3, :], float(SPW - 1), None, ALU.add))
            ch(ve.tensor_tensor(small_i[:, 0, 0:T], small[:, 2, :], small[:, 1, :], ALU.subtract))
            ch.link(ve.tensor_scalar(small_i[:, 1, 0:T], small_i[:, 3, 0:T], 5, None, ALU.logical_shift_right))
            ch.link(ve.tensor_copy(small[:, 4, :], small_i[:, 1, 0:T]))
            ch.link(ve.tensor_tensor_scan(small[:, 5, :], small[:, 0, :], small[:, 4, :], 0.0, ALU.mult, ALU.add))
            ch(ve.tensor_tensor(small_i[:, 2, 0:T], small[:, 5, :], small[:, 4, :], ALU.subtract))
            ch.link(ve.tensor_copy(small_i[:, 3, 0:1], small[:, 5, T - 1:T]))
            ch.link(ve.tensor_copy(sp_tile[:, :], iota_f[:, 0:T]))

            def flatten(i):
                ve.wait_ge(win_in[i], 16 * UN)
                some = bass.ds(i * UN, UN)
                rec = win[:, some, :].rearrange("p t (j c) -> p t j c", c=3)
                ch.link(ve.tensor_tensor(flat_in, iota_f[:, 0:CAP].unsqueeze(1).to_broadcast([P, UN, CAP]),
                                         bc(degf[:, some], CAP), ALU.is_lt))
                ch(ve.scalar_tensor_tensor(out=flat_row, in0=rec[:, :, :, 0], scalar=-float(ZROW),
                                           in1=flat_in, op0=ALU.add, op1=ALU.mult))
                ch(ve.scalar_tensor_tensor(out=flat_row0, in0=rec[:, :, :, 1], scalar=-float(ZROW * R),
                                           in1=flat_in, op0=ALU.add, op1=ALU.mult))
                ch.sync()
                apart(ve)
                for u in range(UN):
                    t = i * UN + u
                    off = ve.value_load(small_i[0:1, 0, bass.ds(t, 1)], min_val=0, max_val=ROUNDS)
                    at = bass.ds(off, CAP)
                    weight = win[:, t, :].bitcast(F32).rearrange("p (j c) -> p j c", c=3)[:, :, 2]
                    ch(ve.tensor_tensor(wt[:, at], weight, flat_in[:, u, :], ALU.mult))
                    ch(ve.tensor_scalar(idx[:, 0, at], flat_row[:, u, :], float(ZROW), None, ALU.add))
                    ch(ve.tensor_scalar(idx[:, 1, at], flat_row0[:, u, :], float(ZROW * R), None, ALU.add))
                    ch(ve.tensor_copy(round_tile[0:1, at], sp_tile[0:1, bass.ds(t, 1)].to_broadcast([1, CAP])))
                    ch.sync()
                    apart(ve)
                ve.memset(mask[:, 1, :], 0.0).then_inc(pr["flat"], 1)
            for i in range(TI):
                flatten(i)

            ve.memset(next(marks), 0.0).then_inc(spb["dve"], 1)
            q_total = ve.value_load(small_i[0:1, 3, 0:1], min_val=0, max_val=SPILLS)
            with ve.If(q_total):
                with ve.Fori(0, T) as t:
                    run = Chain(ve, spb["run"])
                    run.base = t * 2
                    run(ve.tensor_scalar(sp_run[:, 0:1], startf[:, bass.ds(t, 1)], float(CAP), None, ALU.add))
                    run.link(ve.tensor_scalar(sp_run[:, 1:2], degf[:, bass.ds(t, 1)], -float(CAP), None, ALU.add))
                    apart(ve)
                    n = ve.value_load(small_i[0:1, 1, bass.ds(t, 1)], min_val=0, max_val=SPILLS)
                    first = ve.value_load(small_i[0:1, 2, bass.ds(t, 1)], min_val=0, max_val=SPILLS)
                    with ve.If(n):
                        with ve.Fori(0, n) as j:
                            q = nc.s_assert_within(ve.snap(first + j), 0, SPILLS - 1, skip_runtime_bounds_check_because="the windows counted by this program are below their bound")
                            sc = Chain(ve, spb["dve"])
                            sc.base = q * SPB_PER + 1
                            sc.link(ve.tensor_scalar(sp_f[:, 2:3], sp_run[:, 0:1], float(E), None, ALU.min))
                            sc(ve.tensor_scalar(sp_at[:, :], sp_f[:, 2:3], 3.0, None, ALU.mult))
                            assert sc.n == SPB_AT
                            sc.link(ve.tensor_scalar(sp_m[:, 0, :], iota_f[:, 0:SPW], sp_run[:, 1:2], None, ALU.is_lt))
                            ve.wait_ge(spb["window"], q * 16 + 16)
                            rec = sp_win[:, :].rearrange("p (j c) -> p j c", c=3)
                            recf = sp_win[:, :].bitcast(F32).rearrange("p (j c) -> p j c", c=3)
                            for c, z in ((0, ZROW), (1, ZROW * R)):
                                sc.link(ve.scalar_tensor_tensor(out=sp_m[:, 1, :], in0=rec[:, :, c], scalar=-float(z),
                                                                in1=sp_m[:, 0, :], op0=ALU.add, op1=ALU.mult))
                                sc.link(ve.tensor_scalar(sp_rec[:, c * SPW:(c + 1) * SPW], sp_m[:, 1, :], float(z), None,
                                                         ALU.add))
                            sc(ve.tensor_tensor(sp_rec[:, 2 * SPW:3 * SPW].bitcast(F32), recf[:, :, 2], sp_m[:, 0, :], ALU.mult))
                            sc(ve.tensor_copy(sp_rec[:, 3 * SPW:3 * SPW + 1], sp_tile[:, bass.ds(t, 1)]))
                            sc(ve.tensor_copy(sp_rec[:, 3 * SPW + 1:3 * SPW + 2], sp_f[:, 2:3]))
                            sc.link(ve.tensor_copy(sp_rec[:, 3 * SPW + 2:3 * SPW + 3], sp_run[:, 1:2]))
                            sc(ve.tensor_scalar(sp_run[:, 0:1], sp_run[:, 0:1], float(SPW), None, ALU.add))
                            sc.link(ve.tensor_scalar(sp_run[:, 1:2], sp_run[:, 1:2], -float(SPW), None, ALU.add))
                            assert sc.n == SPB_PER

            ch(ve.tensor_scalar(attr_at[:, :], attr_atf[:, :], float(DE), None, ALU.mult))
            ch.link(ve.tensor_tensor(attr_lo[:, :], startf[:, :], attr_atf[:, :], ALU.subtract))
            ch(ve.scalar_tensor_tensor(out=attr_hi[:, :], in0=degf[:, :], scalar=float(CAP), in1=attr_lo[:, :],
                                       op0=ALU.min, op1=ALU.add))
            ch(ve.tensor_scalar(normtmp[:, 0, :], degf[:, :], 1.0, None, ALU.max))
            ch(ve.tensor_scalar(rdeg1[:, :], degf[:, :], 1.0, None, ALU.add))
            ch.sync()
            ch(ve.reciprocal(rdeg1[:, :], rdeg1[:, :]))
            ch.link(ve.reciprocal(rdeg[:, :], normtmp[:, 0, :]))

            def tile_turned(S, wide, last=None):
                def step(i, u):
                    T_, s = i * UN + u, u % 2
                    w(ve, S["mm"], T_ + 1 - lag(u))
                    ve.wait_ge(S["turned"], T_ + 1)
                    ve.tensor_copy(tile_T[:, s, 0:wide], ps_T[s][:, 0:wide]).then_inc(S["lhs"], 1)
                    if last:
                        ve.tensor_copy(tile_T[0:last, s, wide:wide + P], ps_T[s][0:last, wide:wide + P]).then_inc(S["lhs"], 1)
                return step

            def rounds(n, wide, kind, beside=None, head=1, turns=RI, between=None):
                view = acc256 if wide == D else acc512
                piece = T * wide // GB
                for k in range(GB):
                    ve.memset(acc[:, k * piece:(k + 1) * piece], 0.0).then_inc(acc_done, 1)

                def fold_in(t, row, weight):
                    if kind == "weighted":
                        return ve.scalar_tensor_tensor(out=view[:, t, :], in0=row, scalar=weight, in1=view[:, t, :],
                                                       op0=ALU.mult, op1=ALU.add)
                    return ve.tensor_tensor(view[:, t, :], view[:, t, :], row, ALU.max if kind == "max" else ALU.add)

                def body(i):
                    for h in range(2):
                        first = i * 2 * GB + h * GB
                        _, tiles = nc.values_load_multi_w_load_instructions(
                            round_tile[0:1, bass.ds(first, GB)], engines=[ve.engine], min_val=0, max_val=T - 1,
                            skip_runtime_bounds_check_because="the numbers of tiles, written by this program")
                        for u in range(GB):
                            ve.wait_ge(gather_in[u], (n * 2 * RI + i * 2 + h + 1) * 16)
                            ve.wait_ge(acc_done, n * PER_PASS + GB + first + u)
                            fold_in(tiles[u], G[:, u, 0:wide], wt[:, bass.ds(first + u, 1)]).then_inc(acc_done, 1)

                def body_beside(i):
                    if beside:
                        beside(i)
                    body(i)
                loop(ve, turns, body_beside, head=head)
                if between:
                    between()
                    loop(ve, RI, body, first=turns, head=0)
                ve.wait_ge(acc_done, (n + 1) * PER_PASS)
                S = SPL[n]
                ve.memset(next(marks), 0.0).then_inc(S["dve"], 1)
                with ve.If(q_total):
                    with ve.Fori(0, q_total) as q:
                        ve.wait_ge(S["load"], q * 16 + 16)
                        apart(ve)
                        t = ve.value_load(sp_rec[0:1, 3 * SPW:3 * SPW + 1], min_val=0, max_val=T - 1)
                        at = SPW if n == 0 else 0
                        with ve.Fori(0, SPW) as j:
                            m = q * SPW + j
                            ve.wait_ge(S["dve"], m * 2 + 1)
                            ve.tensor_copy(sp_idx[:, :], sp_rec[:, bass.ds(j + at, 1)]).then_inc(S["dve"], 1)
                            ve.wait_ge(S["row"], m * 16 + 16)
                            fold_in(t, G[:, 0, 0:wide], sp_rec[:, bass.ds(j + 2 * SPW, 1)].bitcast(F32))\
                                .then_inc(S["dve"], 1)
                            ve.wait_ge(S["dve"], m * 2 + 3)

            def hot_src(i):
                ve.wait_ge(pr["hist"], HS + i)
                hot(1, i, 0)

            def bias_and_counts():
                ve.wait_ge(pr["x"], 16 * T)
                ch.link(ve.tensor_tensor(x[:, :, :], x[:, :, :], biasA[:, 0:D].unsqueeze(1).to_broadcast([P, T, D]), ALU.add))
                ve.wait_ge(pr["hist"], 2 * HS)
                ve.tensor_copy(src_counts, ps_m[0:T, 0:P]).then_inc(pr["out_counts"], 1)
            rounds(0, D, "sum", hot_src, turns=HS, between=bias_and_counts)
            x2 = x[:, :, :].rearrange("p t f -> p (t f)")
            acc2 = acc[:, 0:T * D]
            ch(ve.scalar_tensor_tensor(out=x2, in0=acc2, scalar=HALF, in1=x2, op0=ALU.mult, op1=ALU.add))
            ch.sync()
            ve.memset(next(marks), 0.0).then_inc(passed, 1)

            def attributes(i):
                if isinstance(i, int) and i < 2:
                    return
                st = Chain(ve, ea["step"])
                st.base = (i - 2) * 3
                at = bass.ds(i - 2, 1)
                st.link(ve.tensor_scalar(mask[:, 0, :], iota_f[:, 0:CAP], attr_lo[:, at], None, ALU.is_ge))
                st.link(ve.scalar_tensor_tensor(out=mask[:, 1, :], in0=iota_f[:, 0:CAP], scalar=attr_hi[:, at],
                                                in1=mask[:, 0, :], op0=ALU.is_lt, op1=ALU.mult))
                ve.wait_ge(ea["in"], (i - 1) * 16)
                av = attr_win.rearrange("p (j f) -> p j f", f=DE)
                st.link(ve.tensor_tensor(av, av, bc(mask[:, 1:2, :].rearrange("p a j -> p (a j)"), DE), ALU.mult))
                ve.tensor_reduce(attr_sum[:, i - 2, :], attr_win.rearrange("p (j f) -> p f j", f=DE),
                                 mybir.AxisListType.X, ALU.add).then_inc(ea["sum"], 1)

            def spill_attributes():
                ve.wait_ge(ea["sum"], T)
                ve.memset(next(marks), 0.0).then_inc(ea["dve"], 1)
                with ve.If(q_total):
                    with ve.Fori(0, q_total) as q:
                        sc = Chain(ve, ea["dve"])
                        sc.base = q * EA_PER + 1
                        ve.wait_ge(ea["load"], q * 16 + 16)
                        apart(ve)
                        t = ve.value_load(sp_rec[0:1, 3 * SPW:3 * SPW + 1], min_val=0, max_val=T - 1)
                        sc.link(ve.tensor_scalar(sp_f[:, 2:3], sp_rec[:, 3 * SPW + 1:3 * SPW + 2], float(E - SPW), None, ALU.min))
                        sc(ve.tensor_scalar(sp_at[:, :], sp_f[:, 2:3], float(DE), None, ALU.mult))
                        assert sc.n == EA_AT
                        sc.link(ve.tensor_tensor(sp_f[:, 3:4], sp_rec[:, 3 * SPW + 1:3 * SPW + 2], sp_f[:, 2:3], ALU.subtract))
                        sc(ve.tensor_tensor(sp_f[:, 0:1], sp_f[:, 3:4], sp_rec[:, 3 * SPW + 2:3 * SPW + 3], ALU.add))
                        sc.link(ve.tensor_scalar(sp_m[:, 0, :], iota_f[:, 0:SPW], sp_f[:, 3:4], None, ALU.is_ge))
                        sc.link(ve.scalar_tensor_tensor(out=sp_m[:, 1, :], in0=iota_f[:, 0:SPW], scalar=sp_f[:, 0:1],
                                                        in1=sp_m[:, 0, :], op0=ALU.is_lt, op1=ALU.mult))
                        ve.wait_ge(ea["window"], q * 16 + 16)
                        av = sp_attr.rearrange("p (j f) -> p j f", f=DE)
                        sc.link(ve.tensor_tensor(av, av, bc(sp_m[:, 1:2, :].rearrange("p a j -> p (a j)"), DE), ALU.mult))
                        sc.link(ve.tensor_reduce(sp_sum[:, :], sp_attr.rearrange("p (j f) -> p f j", f=DE),
                                                 mybir.AxisListType.X, ALU.add))
                        sc.link(ve.tensor_tensor(attr_sum[:, t, :], attr_sum[:, t, :], sp_sum[:, :], ALU.add))
                        assert sc.n == EA_PER

            ve.wait_ge(fo["out"], FOLDED)
            layer_norm(1)
            rounds(1, D, "sum", attributes, head=2)
            spill_attributes()
            ve.wait_ge(L["tm"]["kept"], T)
            ve.tensor_tensor(H[:, :, D:2 * D], acc256, bc(rdeg[:, :], D), ALU.mult).then_inc(passed, 1)
            S = L["thp"]

            def pool_rows(i, u):
                slot_sent(ve, "thp", i, u)
                ve.wait_ge(S["mm"], i * UN + u + 1)
                ch.link(ve.tensor_tensor(G[:, u, :], ps_o[u][:, :], biasB[:, :], ALU.add))
                ve.tensor_scalar(G[:, u, :], G[:, u, :], 0.0, None, ALU.max).then_inc(S["out"], 1)
            ve.wait_ge(passed, 2)
            turned = tile_turned(S, HID)
            turned(0, 0)
            loop(ve, TI, with_next(pool_rows, turned), ch, tail=1)
            rounds(2, HID, "max")
            ve.memset(next(marks), 0.0).then_inc(passed, 1)
            S = L["tv"]
            ve.wait_ge(L["ty"]["out"], T)

            def y_rows(i, u):
                T_ = i * UN + u
                ve.wait_ge(S["mm"], T_ + 1)
                ve.tensor_tensor(H[:, T_, :], ps_o[u][:, :], H[:, T_, :], ALU.add).then_inc(S["kept"], 1)
            turned = tile_turned(S, HID)
            turned(0, 0)
            loop(ve, TI, with_next(y_rows, turned), tail=1)
            ve.wait_ge(S["in"], T)
            rounds(3, HID, "sum")
            ve.wait_ge(S["out"], T)
            ch.link(ve.tensor_tensor(Hflat, Hflat, acc[:, :], ALU.add))

            def g_rows(i):
                for u in range(UN):
                    T_ = i * UN + u
                    slot_sent(ve, "tg", i, u)
                    ve.scalar_tensor_tensor(out=G[:, u, 0:D], in0=H[:, T_, D:2 * D], scalar=rdeg1[:, bass.ds(T_, 1)],
                                            in1=biasA[:, D:2 * D], op0=ALU.mult, op1=ALU.add).then_inc(L["tg"]["out"], 1)
            loop(ve, TI, g_rows, ch)
            ch.link(ve.tensor_tensor(H[:, :, 0:D], H[:, :, 0:D], bc(rdeg1[:, :], D), ALU.mult))
            ch.link(ve.tensor_tensor(x[:, :, :], x[:, :, :], H[:, :, 0:D], ALU.add))
            ch.link(ve.tensor_tensor(x[:, :, :], x[:, :, :], biasA[:, 0:D].unsqueeze(1).to_broadcast([P, T, D]), ALU.add))
            ve.memset(next(marks), 0.0).then_inc(passed, 1)
            ve.wait_ge(pr["out_in"], 16 * T)
            ve.tensor_scalar(normtmp[:, 1, :], outdeg[:, :], 1.0, None, ALU.max).then_inc(pr["norm"], 1)
            rounds(4, D, "sum")
            ve.wait_ge(pr["norm"], 2)
            ch(ve.reciprocal(norm_in[:, :], normtmp[:, 0, :]))
            ch(ve.reciprocal(norm_out[:, :], normtmp[:, 1, :]))
            ch.link(ve.tensor_tensor(acc256, acc256, bc(rdeg[:, :], D), ALU.mult))
            ch.link(ve.tensor_tensor(x2, x2, acc2, ALU.add))
            ve.memset(next(marks), 0.0).then_inc(passed, 1)

            layer_norm(2)
            S = L["t2"]
            loop(ve, TI, with_next(tile_turned(S, D)))
            rounds(5, D, "weighted")
            ch.link(ve.scalar_tensor_tensor(out=x2, in0=acc2, scalar=0.0, in1=x2, op0=ALU.max, op1=ALU.add))
            ve.memset(next(marks), 0.0).then_inc(passed, 1)

            layer_norm(3)
            rounds(6, D, "sum")
            ve.memset(next(marks), 0.0).then_inc(passed, 1)
            S = L["ro"]
            ve.wait_ge(ld["l3"], 48)

            def last_rows(i, u):
                T_ = i * UN + u
                slot_sent(ve, "ro", i, u)
                ve.wait_ge(S["mm"], T_ + 1)
                ch.link(ve.scalar_tensor_tensor(out=G[:, u, 0:D], in0=ps_o[u][:, 0:D], scalar=norm_in[:, bass.ds(T_, 1)],
                                                in1=biasC[:, 0:D], op0=ALU.mult, op1=ALU.add))
                ve.scalar_tensor_tensor(out=G[:, u, 0:D], in0=G[:, u, 0:D], scalar=0.0, in1=x[:, T_, :],
                                        op0=ALU.max, op1=ALU.add).then_inc(S["out"], 1)
            turned = tile_turned(S, D, last=DE)
            turned(0, 0)
            loop(ve, TI, with_next(last_rows, turned), ch, tail=1)


_INS = ['x', 'src', 'dst', 'edge_attr_64', 'edge_type_8', 'edge_weight',
        'L0_gnn_weight', 'L0_gnn_h_bias', 'L0_gnn_loop_weight',
        'L1_gnn_W1_self', 'L1_gnn_W1_neigh', 'L1_gnn_b1', 'L1_gnn_W2_pool', 'L1_gnn_b2_pool',
        'L1_gnn_W2_self', 'L1_gnn_W2_neigh', 'L1_gnn_b2', 'L1_gnn_W3_neigh', 'L1_gnn_b3',
        'L1_gnn_W4_self', 'L1_gnn_W4_neigh', 'L1_gnn_b4', 'L1_gnn_W_fc', 'L1_gnn_b_fc',
        'L2_gnn_weight', 'L3_gnn_weight', 'L3_gnn_bias']


def kernel(**inputs):
    import concourse.bacc as _bacc
    from concourse import mybir as _mybir
    from concourse.bass_utils import run_bass_kernel_spmd as _run

    nc = _bacc.Bacc("TRN2", target_bir_lowering=False, num_devices=1)
    arrays, args = {}, []
    for name in _INS:
        a = np.ascontiguousarray(inputs[name])
        arrays[f"in_{name}_dram"] = a
        args.append(nc.dram_tensor(f"in_{name}_dram", a.shape, _mybir.dt.from_np(a.dtype), kind="ExternalInput").ap())
    args.append(nc.dram_tensor("out_0_dram", arrays["in_x_dram"].shape, F32, kind="ExternalOutput").ap())
    build_gnn(nc, *args)
    r = _run(nc, [arrays], core_ids=[0])
    return r.results[0]["out_0_dram"]
```

```python
from contextlib import ExitStack

import numpy as np

import concourse.bass as bass
from concourse import mybir

F32 = mybir.dt.float32
BF16 = mybir.dt.bfloat16
I32 = mybir.dt.int32
ALU = mybir.AluOpType
ACT = mybir.ActivationFunctionType

P = 128
UN = 5


def build_gnn(nc, x_in, src_in, dst_in, attr_in, type_in, weight_in,
              w0_in, b0_in, loop_in,
              w1s_in, w1n_in, b1_in, wp_in, bp_in, w2s_in, w2n_in, b2_in, w3_in, b3_in,
              w4s_in, w4n_in, b4_in, wfc_in, bfc_in, wl2_in, wl3_in, bl3_in, out):
    N, D = x_in.shape
    (E,) = src_in.shape
    R = w0_in.shape[0]
    HID = w1s_in.shape[1]
    DE = attr_in.shape[1]
    T = 5 * (-(-N // (P * 5)))
    NP = T * P
    TI = T // UN
    CAP = 41
    TOP_DEG = 4095
    TOPS = E // TOP_DEG + 1
    SPW = 32
    GB = 8
    ROUNDS = 2 * GB * (-(-(E // P + T) // (2 * GB)))
    RI = ROUNDS // (2 * GB)
    assert (T - UN) % 2 == 0
    assert NP <= TOP_DEG and TOPS <= P
    assert RI == T + 1 and RI % 2 == 0
    RC = ROUNDS + CAP
    EP = max(p for p in range(1, P + 1) if E % p == 0)
    EC = E // EP
    HC = 40
    HS = EC // HC
    assert EC % HC == 0 and HS % 2 == 0
    ZROW = NP
    REC = 3 * SPW + 3
    SPILLS = T + -(-E // SPW)
    KD, KH = D // P, HID // P
    EPS = 1e-5
    HALF = float(np.float32(0.5) ** np.float32(0.5))

    with ExitStack() as ctx:
        def sb(name, shape, dt=F32):
            return ctx.enter_context(nc.sbuf_tensor(name, shape, dt))

        def sem(name):
            return ctx.enter_context(nc.semaphore(name))

        def sems(prefix, names):
            return {n: sem(f"{prefix}_{n}") for n in names.split()}

        def dram(name, shape, dt=F32):
            return nc.dram_tensor(name, shape, dt)

        edge_rec = dram("edge_rec", [(E + CAP) * 3], I32)
        key_dram = dram("key_dram", [NP])
        node_rec = dram("node_rec", [NP, 3], I32)
        out_dram = dram("out_dram", [NP])
        table_x = dram("table_x", [NP, D])
        table0 = dram("table0", [NP + 1, R * D])
        table_h = dram("table_h", [NP + 1, D])
        table_hp = dram("table_hp", [NP + 1, HID])
        table_y = dram("table_y", [NP + 1, HID])
        table_g = dram("table_g", [NP + 1, D])
        table_2 = dram("table_2", [NP + 1, D])
        table_3 = dram("table_3", [NP + 1, D])
        spill = dram("spill", [SPILLS, P, REC], I32)

        x = sb("x", [P, T, D])
        acc = sb("acc", [P, T * HID])
        H = sb("H", [P, T, HID])
        G = sb("G", [P, GB, HID])
        attr_sum = sb("attr_sum", [P, T, DE])
        idx = sb("idx", [P, 2, RC], I32)
        wt = sb("wt", [P, RC])
        round_tile = sb("round_tile", [1, RC], I32)
        wreg = sb("wreg", [P, 3 * KH * HID])
        tile_in = sb("tile_in", [P, 2, HID])
        tile_T = sb("tile_T", [P, 2, HID])
        stats = sb("stats", [P, T, 6])
        mv = sb("mv", [P, T, 2])
        std = sb("std", [P, T])
        rstd = sb("rstd", [P, T])
        nmr = sb("nmr", [P, T])
        row_sum = sb("row_sum", [P, T])
        neg_mean = sb("neg_mean", [P, T])
        squares = sb("squares", [P, T])
        recs = sb("recs", [P, T, 3], I32)
        node_of = sb("node_of", [P, T], I32)
        degf = sb("degf", [P, T])
        startf = sb("startf", [P, T])
        outdeg = sb("outdeg", [P, T])
        win_at = sb("win_at", [P, T], I32)
        attr_at = sb("attr_at", [P, T], I32)
        attr_lo = sb("attr_lo", [P, T])
        attr_hi = sb("attr_hi", [P, T])
        attr_atf = sb("attr_atf", [P, T])
        attr_start = sb("attr_start", [P, 2], I32)
        ones_row = sb("ones_row", [1, P])
        rdeg = sb("rdeg", [P, T])
        rdeg1 = sb("rdeg1", [P, T])
        norm_in = sb("norm_in", [P, T])
        norm_out = sb("norm_out", [P, T])
        normtmp = sb("normtmp", [P, 2, T])
        slot_idx = sb("slot_idx", [P, 2, GB], I32)
        iota_i = sb("iota_i", [P, P], I32)
        iota_f = sb("iota_f", [P, P])
        part_i = sb("part_i", [P, 1], I32)
        part_f = sb("part_f", [P, 1])
        ident = sb("ident", [P, P])
        small = sb("small", [P, 8, T])
        ends = sb("ends", [1, T], I32)
        small_i = sb("small_i", [P, 4, T + 1], I32)
        first_recs = sb("first_recs", [P, T, 3], I32)
        caps = sb("caps", [P, T])
        top_recs = sb("top_recs", [P, TOPS, 3], I32)
        top_deg = sb("top_deg", [P, TOPS])
        biasA = sb("biasA", [P, HID])
        biasB = sb("biasB", [P, HID])
        biasC = sb("biasC", [P, HID])
        mask = sb("mask", [P, 2, CAP])
        sp_win = sb("sp_win", [P, 3 * SPW], I32)
        sp_rec = sb("sp_rec", [P, REC], I32)
        sp_run = sb("sp_run", [P, 2])
        sp_at = sb("sp_at", [P, 1], I32)
        sp_idx = sb("sp_idx", [P, 1], I32)
        sp_m = sb("sp_m", [P, 2, SPW])
        sp_f = sb("sp_f", [P, 4])
        sp_tile = sb("sp_tile", [P, T])
        sp_sum = sb("sp_sum", [P, DE])

        ps_T = [ctx.enter_context(nc.psum_tensor(f"ps_T{i}", [P, HID], F32)) for i in range(2)]
        ps_o = [ctx.enter_context(nc.psum_tensor(f"ps_o{i}", [P, HID], F32)) for i in range(5)]
        ps_m = ctx.enter_context(nc.psum_tensor("ps_m", [P, HID], F32))

        acc512 = acc[:, :].rearrange("p (t f) -> p t f", t=T)
        acc256 = acc[:, 0:T * D].rearrange("p (t f) -> p t f", t=T)
        POOL_AT = [*range(3 * UN, 5 * UN), *range(2 * UN), 13, 14, 10, 11, 12]
        assert HID == 2 * D and TI == 5
        Hflat = H[:, :, :].rearrange("p t f -> p (t f)")
        stage = G[:, :, :].rearrange("p b f -> p (b f)").rearrange("p (s f) -> p s f", s=2)
        w0 = wreg[:, 0:KD * R * D].rearrange("p (k n) -> p k n", k=KD)
        loopw = wreg[:, KD * R * D:KD * (R + 1) * D].rearrange("p (k n) -> p k n", k=KD)
        fold = [wreg[:, i * KH * HID:(i + 1) * KH * HID].rearrange("p (k n) -> p k n", k=KH) for i in range(3)]
        w_hp, w_y, w_v = fold
        wl2 = wreg[:, 0:KD * D].rearrange("p (k n) -> p k n", k=KD)
        wl3 = wreg[:, KD * D:KD * D + 3 * D].rearrange("p (k n) -> p k n", k=3)
        edge_i = acc[0:EP, 0:8 * EC].bitcast(I32).rearrange("p (a c) -> p a c", a=8)
        edge3 = acc[0:EP, 8 * EC:11 * EC]
        UPPER = T * D
        lo_hot = Hflat[0:EP, 0:HC * P].bitcast(BF16).rearrange("p (s c n) -> p s c n", s=2, n=P)
        hi_hot = Hflat[0:EP, HC * P:HC * P + HC * T].bitcast(BF16).rearrange("p (s c n) -> p s c n", s=2, n=T)
        iota_b = Hflat[:, 6400:6464].bitcast(BF16)
        hist = Hflat[0:T, 6528:7552].rearrange("p (a c) -> p a c", c=P)
        upper = Hflat[0:T, 7552:7552 + T]
        tot = Hflat[0:T, 7600:7602]
        node_rec_s = Hflat[:, 7700:7700 + 3 * T].bitcast(I32).rearrange("p (t c) -> p t c", c=3)
        cols = Hflat[:, 7850:7850 + 3 * T].rearrange("p (a t) -> p a t", a=3)
        pos_f = Hflat[:, 8000:8000 + T]
        pos_i = Hflat[:, 8050:8050 + T].bitcast(I32)
        zeros = Hflat[:, 8192:8192 + R * D]
        key_row = acc[:, 11 * EC:11 * EC + NP]
        cmp_out = acc[:, 11 * EC + NP:11 * EC + 2 * NP]
        after_keys = 11 * EC + 2 * NP
        edge_b = acc[0:EP, after_keys:after_keys + 2 * EC].bitcast(BF16).rearrange("p (a c) -> p a c", a=4)
        src_counts = acc[0:T, after_keys + 2 * EC:after_keys + 2 * EC + P]
        assert after_keys > UPPER
        win = acc[:, 11 * EC:11 * EC + T * 3 * CAP].bitcast(I32).rearrange("p (t c) -> p t c", t=T)
        flat_in, flat_row, flat_row0 = [acc[:, 11 * EC + NP + k * UN * CAP:11 * EC + NP + (k + 1) * UN * CAP]
                                        .rearrange("p (t j) -> p t j", t=UN) for k in range(3)]
        attr_win = [acc[:, UPPER + i * CAP * DE:UPPER + (i + 1) * CAP * DE] for i in range(2)]
        sp_attr = acc[:, UPPER:UPPER + SPW * DE]
        f_wfc = Hflat[:, 0:KH * D].rearrange("p (k n) -> p k n", k=KH)

        def fold_buf(i):
            a = KH * D + i * KH * HID
            return Hflat[:, a:a + KH * HID].rearrange("p (k n) -> p k n", k=KH)

        f_left, f_leftT, f_F, f_M, f_S = [fold_buf(i) for i in range(5)]
        f_row = Hflat[0:1, KH * D + 5 * KH * HID:KH * D + 5 * KH * HID + 2 * HID].rearrange("p (a n) -> p a n", a=2)
        f_bias = tile_in[:, :, :].rearrange("p s f -> p (s f)").rearrange("p (a k n) -> p a k n", a=2, k=KH)
        f_bcol = stats[:, 0:4, 0:4]

        ld = sems("ld", "edges x zero_x w0 loopw zero tail rec keys nodes x2 l2 l3")
        pr = sems("pr", "const hot hist sums carry key turned pos placed nodes norm x flat out_counts out_stored out_in norm_in")
        win_in = [sem(f"win_in{i}") for i in range(TI)]
        spb = sems("spb", "run dve window stored")
        ea = sems("ea", "at in0 in1 step sum dve load window")
        fo = sems("fo", "turned lhs done out left right bias bcol")
        made = "in turned lhs mm"
        L = {"t0": sems("t0", f"{made} out kept sent0 sent1"), "tm": sems("tm", "out kept"),
             "thp": sems("thp", f"{made} out kept"), "tv": sems("tv", f"{made} out"),
             "tg": sems("tg", "out"),
             "t2": sems("t2", f"in added moments centred turned lhs mm kept out"),
             "t3": sems("t3", "in added moments kept out"), "ro": sems("ro", f"{made} kept out")}
        SENDERS = "tm thp tv tg t2 t3 ro".split()
        sent = [sem(f"sent{u}") for u in range(UN)]
        gather_in = [[sem(f"gather_in{h}_{u}") for u in range(GB)] for h in range(2)]
        rows_in = [sem(f"rows_in{h}") for h in range(2)]
        acc_done = sem("acc_done")
        SPL = [sems(f"spl{n}", "dve load row") for n in range(7)]
        dve_chain = sem("dve_chain")
        act_chain = sem("act_chain")
        ln_var = sem("ln_var")
        ln_std = sem("ln_std")
        ln_ready = sem("ln_ready")
        whole = sem("whole")
        PER_PASS = GB + ROUNDS
        MARKS = 24
        mark = sb("mark", [1, MARKS])
        HOT0 = 3
        SPB_AT, SPB_PER = 2, 13
        EA_AT, EA_PER = 2, 9
        FOLD = [(w4s_in, [(f_wfc, f_F, 0, D)]),
                (w4n_in, [(f_wfc, f_F, D, D)]),
                (w3_in, [(f_F, f_M, 0, HID)]),
                (w2n_in, [(f_M, w_v, 0, HID)]),
                (w2s_in, [(f_M, f_S, 0, HID)]),
                (w1s_in, [(f_S, w_y, 0, HID), (f_F, w_hp, 0, HID)]),
                (w1n_in, [(f_S, w_y[:, KD:KH, :], 0, HID), (f_F, w_hp[:, KD:KH, :], 0, HID)])]
        FOLD_BIAS = {1: ((2, 3), [biasA]), 4: ((0, 1), [biasC, biasB])}
        FOLDED = sum(v.shape[0] // P * len(outs) for v, outs in FOLD) + 3

        class Chain:

            def __init__(self, eng, s):
                self.eng, self.sem, self.base, self.n = eng, s, 0, 0

            def __call__(self, ins):
                ins.then_inc(self.sem, 1)
                self.n += 1

            def sync(self):
                self.eng.wait_ge(self.sem, self.base + self.n)

            def link(self, ins):
                self(ins)
                self.sync()

        def w(eng, s, v):
            if not isinstance(v, int) or v > 0:
                eng.wait_ge(s, v)

        def apart(eng):
            eng.nop(nofuse=True)

        def loop(eng, n, body, chain=None, first=0, head=1, tail=0):
            start = chain.n if chain else 0
            for i in range(first, first + head):
                body(i)
            done = chain.n if chain else 0
            per = (done - start) // head if chain else 0
            at = first + head
            if n - tail > at:
                with eng.Fori(at, n - tail) as i:
                    if chain:
                        chain.base, chain.n = (i - at) * per + done, 0
                    body(i)
                    if chain:
                        assert chain.n == per
                if chain:
                    chain.base, chain.n = 0, done + (n - tail - at) * per
            for i in range(n - tail, n):
                body(i)

        def is_last(i, u):
            return isinstance(i, int) and i == TI - 1 and u == UN - 1

        def previous(i, u):
            return (i, u - 1) if u else (i - 1, UN - 1)

        def following(i, u):
            return (i, u + 1) if u + 1 < UN else (i + 1, 0)

        def with_next(now, ahead=None, before=None):
            def body(i):
                for u in range(UN):
                    more = not is_last(i, u)
                    j, v = following(i, u)
                    if before and more:
                        before(j, v)
                    if ahead and more and v:
                        ahead(j, v)
                    now(i, u)
                    if ahead and more and not v:
                        ahead(j, v)
            return body

        def slot_sent(eng, ph, i, u):
            if not (isinstance(i, int) and i == 0):
                eng.wait_ge(sent[u], 16 * (SENDERS.index(ph) * TI + i))

        def lag(u):
            return 1 if u == 0 else 2

        def gathered(wide, h, u):
            return G[:, u, 0:HID] if wide == HID else G[:, u, h * D:(h + 1) * D]

        block = ctx.enter_context(nc.Block())

        @block.sync
        def _(sp):
            for a, v in enumerate((dst_in, src_in, type_in)):
                sp.dma_start(edge_i[:, a, :], v.rearrange("(p c) -> p c", p=EP)).then_inc(ld["edges"], 16)
            sp.dma_start(edge_i[:, 3, :].bitcast(F32), weight_in.rearrange("(p c) -> p c", p=EP))\
                .then_inc(ld["edges"], 16)
            FT = N // P
            sp.dma_start(x[:, 0:FT, :], x_in[0:FT * P, :].rearrange("(t p) f -> p t f", p=P)).then_inc(ld["x"], 16)
            sp.wait_ge(ld["zero_x"], 1)
            sp.dma_start(x[0:N - FT * P, FT, :], x_in[FT * P:N, :]).then_inc(ld["x"], 16)
            for r in range(R):
                sp.dma_start(w0[:, :, r * D:(r + 1) * D], w0_in[r].rearrange("(k p) n -> p k n", p=P))\
                    .then_inc(ld["w0"], 16)
            sp.dma_start(loopw, loop_in.rearrange("(k p) n -> p k n", p=P)).then_inc(ld["w0"], 16)
            sp.dma_start(biasA[:, 0:D], b0_in.rearrange("(a n) -> a n", a=1).to_broadcast([P, D]))\
                .then_inc(ld["w0"], 16)
            sp.wait_ge(pr["const"], 8)
            for table, width in ((table0, R * D), (table_h, D), (table_hp, HID), (table_y, HID),
                                 (table_g, D), (table_2, D), (table_3, D)):
                sp.dma_start(table[NP:NP + 1, :], zeros[0:1, 0:width]).then_inc(ld["zero"], 16)
            sp.dma_start(edge_rec[3 * E:3 * (E + CAP)].rearrange("(a n) -> a n", a=1),
                         zeros[0:1, 0:3 * CAP].bitcast(I32)).then_inc(ld["tail"], 16)
            sp.wait_ge(pr["hot"], 3)
            sp.dma_start(edge_rec[0:3 * E].rearrange("(p c) -> p c", p=EP), edge3.bitcast(I32)).then_inc(ld["rec"], 16)
            sp.wait_ge(pr["key"], 1)
            sp.dma_start(key_dram[:].rearrange("(h l) -> h l", l=P), hist[:, 4, :]).then_inc(ld["keys"], 16)
            sp.wait_ge(ld["keys"], 16)
            sp.dma_start(key_row, key_dram[:].rearrange("(a n) -> a n", a=1).to_broadcast([P, NP]))\
                .then_inc(ld["keys"], 16)
            sp.wait_ge(pr["placed"], 16 * T)
            sp.dma_start(recs[:, :, :], node_rec[:, :].rearrange("(t p) c -> p t c", p=P)).then_inc(ld["nodes"], 16)
            sp.dma_start(first_recs[:, :, :], node_rec[:, :].rearrange("(t p) c -> p t c", p=P)[0:1, :, :].to_broadcast([P, T, 3]))\
                .then_inc(ld["nodes"], 16)
            sp.dma_start(top_recs[:, :, :], node_rec[0:TOPS, :].rearrange("(a t) c -> a t c", a=1).to_broadcast([P, TOPS, 3]))\
                .then_inc(ld["nodes"], 16)

            def row_numbers(n):
                kind = 1 if n == 0 else 0

                def body(i):
                    for h in range(2):
                        for u in range(GB):
                            w(sp, gather_in[h][u], (n * RI + i) * 16)
                        sp.dma_start(slot_idx[:, h, :], idx[:, kind, bass.ds(i * 2 * GB + h * GB, GB)])\
                            .then_inc(rows_in[h], 16)
                loop(sp, RI, body)

            sp.wait_ge(pr["flat"], TI)
            for n in range(7):
                row_numbers(n)
                if n == 0:
                    sp.wait_ge(pr["out_counts"], 1)
                    sp.dma_start(out_dram[:].rearrange("(h l) -> h l", l=P), src_counts).then_inc(pr["out_stored"], 16)
                if n == 2:
                    sp.wait_ge(L["thp"]["mm"], 2 * T)
                    sp.dma_start(wl2[:, :, :], wl2_in.rearrange("(k p) n -> p k n", p=P)).then_inc(ld["l2"], 16)
                    sp.dma_start(wl3[:, 0:KD, :], wl3_in[0:D, :].rearrange("(k p) n -> p k n", p=P)).then_inc(ld["l3"], 16)
                    sp.dma_start(wl3[0:DE, KD, :], wl3_in[D:D + DE, :]).then_inc(ld["l3"], 16)
                    sp.dma_start(biasC[:, 0:D], bl3_in.rearrange("(a n) -> a n", a=1).to_broadcast([P, D]))\
                        .then_inc(ld["l3"], 16)

        @block.gpsimd
        def _(po):
            po.memset(x[:, T - 1, :], 0.0).then_inc(ld["zero_x"], 1)
            po.iota(iota_i[:, :], pattern=[[1, P]], base=0, channel_multiplier=0).then_inc(pr["const"], 1)
            po.iota(part_i[:, :], pattern=[[0, 1]], base=0, channel_multiplier=1).then_inc(pr["const"], 1)
            po.memset(ident[:, :], 0.0).then_inc(pr["const"], 1)
            po.memset(zeros, 0.0).then_inc(pr["const"], 1)
            po.memset(ones_row[:, :], 1.0).then_inc(pr["const"], 1)
            po.memset(upper, 1.0).then_inc(pr["const"], 1)
            po.wait_ge(pr["const"], 6)
            po.affine_select(out=ident[:, :], in_=ident[:, :], compare_op=ALU.not_equal, fill=1.0,
                             base=0, pattern=[[-1, P]], channel_multiplier=1).then_inc(pr["const"], 1)
            po.affine_select(out=upper, in_=upper, compare_op=ALU.is_gt, fill=0.0,
                             base=0, pattern=[[1, T]], channel_multiplier=-1).then_inc(pr["const"], 1)
            po.wait_ge(pr["pos"], 1)
            for t in range(T):
                po.indirect_dma_start(out=node_rec[:, :], out_offset=bass.IndirectOffsetOnAxis(ap=pos_i[:, t:t + 1], axis=0),
                                      in_=node_rec_s[:, t, :], in_offset=None).then_inc(pr["placed"], 16)
            po.wait_ge(pr["nodes"], 1)
            po.wait_ge(ld["rec"], 16)
            po.wait_ge(ld["tail"], 16)
            po.wait_ge(ld["zero"], 16 * 7)
            rec_row = edge_rec[:].rearrange("(a n) -> a n", a=1)
            attr_row = attr_in.rearrange("(a n) c -> a (n c)", a=1)

            for t in range(T):
                po.indirect_dma_start(out=win[:, t, :], out_offset=None, in_=rec_row,
                                      in_offset=bass.IndirectOffsetOnAxis(ap=win_at[:, t:t + 1], axis=1))\
                    .then_inc(win_in[t // UN], 16)
            for t in range(T):
                po.wait_ge(L["t0"]["kept"], t + 1)
                po.indirect_dma_start(out=table_x[:, :], out_offset=bass.IndirectOffsetOnAxis(ap=pos_i[:, t:t + 1], axis=0),
                                      in_=x[:, t, :], in_offset=None).then_inc(pr["x"], 16)
            po.wait_ge(pr["flat"], TI)

            q_total = po.value_load(small_i[0:1, 3, 0:1], min_val=0, max_val=SPILLS)
            with po.If(q_total):
                with po.Fori(0, T) as t:
                    n = po.value_load(small_i[0:1, 1, bass.ds(t, 1)], min_val=0, max_val=SPILLS)
                    first = po.value_load(small_i[0:1, 2, bass.ds(t, 1)], min_val=0, max_val=SPILLS)
                    with po.If(n):
                        with po.Fori(0, n) as j:
                            q = nc.s_assert_within(po.snap(first + j), 0, SPILLS - 1, skip_runtime_bounds_check_because="the windows counted by this program are below their bound")
                            po.wait_ge(spb["dve"], 1 + SPB_PER * q + SPB_AT)
                            apart(po)
                            po.indirect_dma_start(out=sp_win[:, :], out_offset=None, in_=rec_row,
                                                  in_offset=bass.IndirectOffsetOnAxis(ap=sp_at[:, :], axis=1))\
                                .then_inc(spb["window"], 16)
                            po.wait_ge(spb["dve"], 1 + SPB_PER * q + SPB_PER)
                            po.dma_start(spill[bass.ds(q, 1), :, :].rearrange("q p c -> p (q c)"), sp_rec[:, :])\
                                .then_inc(spb["stored"], 16)
                            po.wait_ge(spb["stored"], q * 16 + 16)

            def scatter(ph, table, width, rows=None, **bound):
                for t in range(T):
                    po.wait_ge(L[ph]["out"], t + 1)
                    po.indirect_dma_start(out=table, out_offset=bass.IndirectOffsetOnAxis(ap=node_of[:, t:t + 1], axis=0),
                                          in_=rows(t) if rows else G[:, t % UN, 0:width], in_offset=None, **bound).then_inc(sent[t % UN], 16)
                for u in range(UN):
                    po.wait_ge(sent[u], 16 * TI * (SENDERS.index(ph) + 1))

            def gathers(n, table, width):
                def body(i, slot=0):
                    for h in range(2):
                        if n == 4 and h and (not isinstance(i, int) or 1 <= i <= T):
                            w(po, ea["sum"], i - 2)
                            po.tensor_copy(attr_start[:, slot:slot + 1], attr_at[:, bass.ds(i - 1, 1)]).then_inc(ea["at"], 1)
                            po.wait_ge(ea["at"], i)
                            apart(po)
                            po.indirect_dma_start(out=attr_win[slot], out_offset=None, in_=attr_row,
                                                  in_offset=bass.IndirectOffsetOnAxis(ap=attr_start[:, slot:slot + 1], axis=1))\
                                .then_inc(ea[f"in{slot}"], 16)
                        po.wait_ge(rows_in[h], (n * RI + i + 1) * 16)
                        for u in range(GB):
                            if width == HID or isinstance(i, int) and i == 0:
                                po.wait_ge(acc_done, n * PER_PASS + i * 2 * GB + h * GB + u + 1 if width == HID
                                           else n * PER_PASS + (GB if h else u + 1))
                            else:
                                po.wait_ge(acc_done, n * PER_PASS + (i - 1) * 2 * GB + h * GB + u + 1 + GB)
                            apart(po)
                            po.indirect_dma_start(out=gathered(width, h, u), out_offset=None, in_=table,
                                                  in_offset=bass.IndirectOffsetOnAxis(ap=slot_idx[:, h, u:u + 1], axis=0))\
                                .then_inc(gather_in[h][u], 16)

                def pair(k):
                    body(2 * k, 1)
                    body(2 * k + 1, 0)
                if n == 4:
                    loop(po, RI // 2, pair, head=2)
                else:
                    loop(po, RI, body)
                S = SPL[n]
                with po.If(q_total):
                    with po.Fori(0, q_total) as q:
                        po.wait_ge(S["dve"], q * (2 * SPW) + 1)
                        po.dma_start(sp_rec[:, :], spill[bass.ds(q, 1), :, :].rearrange("q p c -> p (q c)"))\
                            .then_inc(S["load"], 16)
                        with po.Fori(0, SPW) as j:
                            po.wait_ge(S["dve"], (q * SPW + j) * 2 + 2)
                            apart(po)
                            po.indirect_dma_start(out=G[:, 0, 0:width], out_offset=None, in_=table,
                                                  in_offset=bass.IndirectOffsetOnAxis(ap=sp_idx[:, :], axis=0))\
                                .then_inc(S["row"], 16)
                        po.wait_ge(S["dve"], (q + 1) * (2 * SPW) + 1)
                        apart(po)
                        po.inc_swdge_sem([S["row"]], [16 * SPW], mode="sub")

            def spill_attributes():
                with po.If(q_total):
                    with po.Fori(0, q_total) as q:
                        po.wait_ge(ea["dve"], q * EA_PER + 1)
                        po.dma_start(sp_rec[:, :], spill[bass.ds(q, 1), :, :].rearrange("q p c -> p (q c)"))\
                            .then_inc(ea["load"], 16)
                        po.wait_ge(ea["dve"], q * EA_PER + 1 + EA_AT)
                        apart(po)
                        po.indirect_dma_start(out=sp_attr, out_offset=None, in_=attr_row,
                                              in_offset=bass.IndirectOffsetOnAxis(ap=sp_at[:, :], axis=1))\
                            .then_inc(ea["window"], 16)

            po.wait_ge(L["t0"]["sent0"], 16 * (UN + (T - UN) // 2))
            po.wait_ge(L["t0"]["sent1"], 16 * ((T - UN) // 2))
            gathers(0, table0[:, :].rearrange("n (r f) -> (n r) f", r=R), D)
            for ph, n, table, width in (("tm", 1, table_h, D), ("thp", 2, table_hp, HID), ("tv", 3, table_y, HID),
                                        ("tg", 4, table_g, D), ("t2", 5, table_2, D), ("t3", 6, table_3, D)):
                if n == 1:
                    po.wait_ge(pr["out_stored"], 16)
                for t in {1: range(2 * T // 3), 5: range(2 * T // 3, T)}.get(n, ()):
                    po.indirect_dma_start(out=outdeg[:, t:t + 1], out_offset=None, in_=out_dram[:].rearrange("(n a) -> n a", a=1),
                                          in_offset=bass.IndirectOffsetOnAxis(ap=node_of[:, t:t + 1], axis=0))\
                        .then_inc(pr["out_in"], 16)
                scatter(ph, table[:, :], width, rows={"thp": lambda t: acc512[:, POOL_AT[t], :], "tv": lambda t: H[:, t, :]}.get(ph))
                gathers(n, table[:, :], width)
                if n == 4:
                    spill_attributes()
            scatter("ro", out, D, lambda t: acc256[:, t, :], bounds_check=N - 1, oob_is_err=False)

        @block.scalar
        def _(act):
            ch = Chain(act, act_chain)

            def roots(n):
                act.wait_ge(ln_var, n + 1)
                act.activation(std[:, :], std[:, :], ACT.Sqrt).then_inc(ln_std, 1)

            def tile_turned(i, u, per=1):
                T_, s = i * UN + u, u % 2
                w(act, S["mm"], (T_ + 1 - lag(u)) * per)
                act.wait_ge(S["turned"], T_ + 1)
                act.activation(tile_T[:, s, :], ps_T[s][:, :], ACT.Copy).then_inc(S["lhs"], 1)

            def folded_in(n, tile):
                last = act.value_load(ends[0:1, bass.ds(tile, 1)], min_val=1, max_val=ROUNDS)
                act.wait_ge(acc_done, n * PER_PASS + GB + last)
                apart(act)

            def spilled(n):
                with act.If(act_q_total):
                    act.wait_ge(whole, n + 1)

            roots(0)
            S = L["t0"]
            act.wait_ge(ln_ready, 1)

            def go_in(t, s, ago=2):
                w(act, S["turned"], t + 1 - ago)
                apart(act)
                act.activation(tile_in[:, s, 0:D], x[:, t, :], ACT.Relu, bias=nmr[:, bass.ds(t, 1)],
                               scale=rstd[:, bass.ds(t, 1)]).then_inc(S["in"], 1)

            def turned0(t, s, ago=2):
                w(act, S["mm"], (t + 1 - ago) * 5)
                act.wait_ge(S["turned"], t + 1)
                act.activation(tile_T[:, s, 0:D], ps_T[s][:, 0:D], ACT.Copy).then_inc(S["lhs"], 1)

            def rows_out(t, s, used):
                w(act, S[f"sent{s}"], used * 16)
                for c in range(4):
                    act.wait_ge(S["mm"], t * 5 + c + 1)
                    act.activation(stage[:, s, c * HID:(c + 1) * HID], ps_o[c][:, :], ACT.Copy).then_inc(S["out"], 1)
                act.wait_ge(S["mm"], t * 5 + 5)
                apart(act)
                act.activation(x[:, t, :], ps_o[4][:, 0:D], ACT.Copy).then_inc(S["kept"], 1)
                act.wait_ge(S["out"], t * 4 + 4)
                apart(act)
                act.dma_start(table0[bass.ds(t * P, P), :], stage[:, s, :]).then_inc(S[f"sent{s}"], 16)

            def first_tiles(t):
                go_in(t, 0, 1)
                turned0(t, 0, 1)
                rows_out(t, 0, t)
            loop(act, UN, first_tiles)

            def next_in(t, s):
                go_in(t, s)
                turned0(t, s)

            def pair_out(k):
                for u in range(2):
                    t = k * 2 + u + UN
                    if not (isinstance(k, int) and k == (T - UN) // 2 - 1 and u):
                        next_in(t + 1, u)
                    rows_out(t, 1 - u, k + UN * u)
            next_in(UN, 1)
            loop(act, (T - UN) // 2, pair_out, tail=1)

            act.wait_ge(pr["x"], 16 * T)
            act.dma_start(x[:, :, :], table_x[:, :].rearrange("(t p) f -> p t f", p=P)).then_inc(ld["x2"], 16)

            act.wait_ge(pr["out_counts"], 1)
            act.wait_ge(ld["zero"], 16 * 7)
            act.dma_start(f_wfc, wfc_in.rearrange("(k p) n -> p k n", p=P)).then_inc(fo["right"], 16)
            for a, v in enumerate((b1_in, b2_in, b3_in, b4_in)):
                act.dma_start(f_bcol[:, a, :], v.rearrange("(k p) -> p k", p=P), allow_slow_non_contiguous=True).then_inc(fo["bias"], 16)
            act.dma_start(f_row[0:1, 0, 0:D], bfc_in.rearrange("(a n) -> a n", a=1)).then_inc(fo["bias"], 16)
            act.dma_start(f_row[0:1, 1, :], bp_in.rearrange("(a n) -> a n", a=1)).then_inc(fo["bias"], 16)
            turned, done = 0, 0
            for n, (v, outs) in enumerate(FOLD):
                rows = v.shape[0]
                if n:
                    act.wait_ge(fo["turned"], turned)
                act.dma_start(f_left[:, 0:rows // P, :], v.rearrange("(m p) k -> p m k", p=P)).then_inc(fo["left"], 16)
                for k in range(KH):
                    act.wait_ge(fo["turned"], turned + 1)
                    if n and k == 0:
                        act.wait_ge(fo["done"], done)
                    act.activation(f_leftT[:, k, 0:rows], ps_T[k % 2][:, 0:rows], ACT.Copy).then_inc(fo["lhs"], 1)
                    turned += 1
                for (_, dest, lo, width) in outs:
                    for m in range(rows // P):
                        done += 1
                        act.wait_ge(fo["done"], done)
                        act.activation(dest[:, m, lo:lo + width], ps_o[m][:, 0:width], ACT.Copy).then_inc(fo["out"], 1)
                if n in FOLD_BIAS:
                    pair, dests = FOLD_BIAS[n]
                    if n == 4:
                        act.wait_ge(fo["turned"], turned)
                    act.wait_ge(fo["bias"], 16 * 6)
                    for a, b in enumerate(pair):
                        for k in range(KH):
                            act.activation(f_bias[:, a, k, :], f_bcol[:, b, k:k + 1].to_broadcast([P, P]), ACT.Copy)\
                                .then_inc(fo["bcol"], 1)
                    if n == 4:
                        act.dma_start(f_F, wp_in.rearrange("(k p) n -> p k n", p=P)).then_inc(fo["right"], 16)
                    for dest in dests:
                        done += 1
                        act.wait_ge(fo["done"], done)
                        act.activation(dest[:, :], ps_m[:, :], ACT.Copy).then_inc(fo["out"], 1)

            act_q_total = act.value_load(small_i[0:1, 3, 0:1], min_val=0, max_val=SPILLS)
            roots(1)
            S = L["tm"]
            act.wait_ge(ln_ready, 2)

            def rows_h(i):
                for u in range(UN):
                    T_ = i * UN + u
                    slot_sent(act, "tm", i, u)
                    apart(act)
                    act.activation(G[:, u, 0:D], x[:, T_, :], ACT.Relu, bias=nmr[:, bass.ds(T_, 1)],
                                   scale=rstd[:, bass.ds(T_, 1)]).then_inc(S["out"], 1)
                    act.activation(H[:, T_, 0:D], x[:, T_, :], ACT.Relu, bias=nmr[:, bass.ds(T_, 1)],
                                   scale=rstd[:, bass.ds(T_, 1)]).then_inc(S["kept"], 1)
            loop(act, TI, rows_h)

            act.wait_ge(S["kept"], T)
            S = L["thp"]
            spilled(1)

            def pool_in(i, u):
                T_, s = i * UN + u, u % 2
                folded_in(1, T_)
                w(act, S["turned"], T_ + 1 - lag(u))
                apart(act)
                act.activation(tile_in[:, s, 0:D], H[:, T_, 0:D], ACT.Copy).then_inc(S["in"], 1)
                act.activation(tile_in[:, s, D:2 * D], acc256[:, T_, :], ACT.Identity, scale=rdeg[:, bass.ds(T_, 1)])\
                    .then_inc(S["in"], 1)

            def pool_turned(i, u):
                tile_turned(i, u, 2)

            def pool_out(i, u):
                T_, bank = i * UN + u, 2 * (u % 2)
                act.wait_ge(S["mm"], 2 * T_ + 1)
                at = POOL_AT[T_] if isinstance(i, int) else T_ - 2 * UN
                apart(act)
                act.activation(acc512[:, at, :], ps_o[bank][:, :], ACT.Relu).then_inc(S["out"], 1)
                act.wait_ge(S["mm"], 2 * T_ + 2)
                apart(act)
                act.activation(H[:, T_, :], ps_o[bank + 1][:, :], ACT.Copy).then_inc(S["kept"], 1)
            pool_in(0, 0)
            pool_turned(0, 0)
            loop(act, TI, with_next(pool_out, pool_turned, pool_in), head=2, tail=1)

            act.wait_ge(S["kept"], T)
            S = L["tv"]
            spilled(2)

            def max_tile(i, u):
                T_, s = i * UN + u, u % 2
                folded_in(2, T_)
                w(act, S["turned"], T_ + 1 - lag(u))
                apart(act)
                act.activation(tile_in[:, s, :], acc512[:, T_, :], ACT.Copy).then_inc(S["in"], 1)
                tile_turned(i, u)
                act.wait_ge(S["mm"], T_ + 1)
                apart(act)
                act.activation(H[:, T_, :], ps_o[u][:, :], ACT.Copy).then_inc(S["out"], 1)
            loop(act, TI, with_next(max_tile))

            def moments(S, n, i, u, **scaled):
                T_, s = i * UN + u, u % 2
                at = bass.ds(T_, 1)
                folded_in(n, T_)
                act.activation(tile_in[:, s, 0:D], acc256[:, T_, :], **scaled).then_inc(S["in"], 1)
                act.wait_ge(S["added"], T_ + 1)
                apart(act)
                act.activation(x[:, T_, :], ps_o[u][:, 0:D], ACT.Copy, accum_out=row_sum[:, at]).then_inc(S["moments"], 1)
                act.wait_ge(S["moments"], T_ * 3 + 1)
                apart(act)
                act.activation(neg_mean[:, at], row_sum[:, at], ACT.Identity, scale=-1.0 / D).then_inc(S["moments"], 1)
                act.wait_ge(S["moments"], T_ * 3 + 2)
                apart(act)
                act.activation(tile_in[:, s, D:2 * D], x[:, T_, :], ACT.Square, bias=neg_mean[:, at],
                               accum_out=squares[:, at]).then_inc(S["moments"], 1)

            spilled(4)

            def tile2(i, u):
                S = L["t2"]
                T_, s = i * UN + u, u % 2
                moments(S, 4, i, u, func=ACT.Identity, scale=rdeg[:, bass.ds(T_, 1)])
                act.activation(tile_in[:, s, 0:D], x[:, T_, :], ACT.Relu, bias=neg_mean[:, bass.ds(T_, 1)]).then_inc(S["centred"], 1)
                act.wait_ge(S["turned"], T_ + 1)
                act.activation(tile_T[:, s, 0:D], ps_T[s][:, 0:D], ACT.Copy).then_inc(S["lhs"], 1)
                act.wait_ge(S["mm"], T_ + 1)
                apart(act)
                act.activation(acc256[:, T_, :], ps_m[:, 0:D], ACT.Copy).then_inc(S["kept"], 1)
            loop(act, TI, with_next(tile2))
            roots(2)

            act.wait_ge(pr["norm"], 1)
            act.activation(normtmp[:, :, :], normtmp[:, :, :], ACT.Sqrt).then_inc(pr["norm"], 1)
            spilled(5)

            def tile3(i, u):
                S = L["t3"]
                T_ = i * UN + u
                moments(S, 5, i, u, func=ACT.Relu)
                act.activation(acc256[:, T_, :], x[:, T_, :], ACT.Relu, bias=neg_mean[:, bass.ds(T_, 1)]).then_inc(S["kept"], 1)
            loop(act, TI, with_next(tile3))
            roots(3)

            S = L["ro"]
            act.wait_ge(pr["norm_in"], 1)
            spilled(6)

            def last_tile(i, u):
                T_, s = i * UN + u, u % 2
                folded_in(6, T_)
                w(act, S["turned"], T_ + 1 - lag(u))
                apart(act)
                act.activation(tile_in[:, s, 0:D], acc256[:, T_, :], ACT.Identity, scale=norm_in[:, bass.ds(T_, 1)])\
                    .then_inc(S["in"], 1)
                act.activation(tile_in[:, s, D:D + DE], attr_sum[:, T_, :], ACT.Identity, scale=norm_in[:, bass.ds(T_, 1)])\
                    .then_inc(S["in"], 1)
                w(act, S["mm"], T_ + 1 - lag(u))
                act.wait_ge(S["turned"], T_ + 1)
                act.activation(tile_T[:, s, 0:D], ps_T[s][:, 0:D], ACT.Copy).then_inc(S["lhs"], 1)
                act.activation(tile_T[0:DE, s, D:D + P], ps_T[s][0:DE, D:D + P], ACT.Copy).then_inc(S["lhs"], 1)
                act.wait_ge(S["mm"], T_ + 1)
                apart(act)
                act.activation(acc256[:, T_, :], ps_o[u][:, 0:D], ACT.Relu).then_inc(S["kept"], 1)
            loop(act, TI, with_next(last_tile))

        @block.tensor
        def _(pe):
            pe.wait_ge(pr["const"], 8)

            def turn(S, T_, s, widths, n_in=1):
                pe.wait_ge(S["in"], (T_ + 1) * n_in)
                for k, width in enumerate(widths):
                    mm = pe.transpose(ps_T[s][0:width, k * P:(k + 1) * P], tile_in[:, s, k * P:k * P + width], ident[:, :])
                mm.then_inc(S["turned"], 1)

            def count(step, s, first):
                pe.wait_ge(pr["hot"], HOT0 + step * 2 + 2)
                for c in range(HC):
                    mm = pe.matmul(ps_m[0:T, 0:P], hi_hot[:, s, c, :], lo_hot[:, s, c, :],
                                   start=first and c == 0, stop=c == HC - 1, skip_group_check=True)
                mm.then_inc(pr["hist"], 1)

            S = L["t0"]

            def turn0(t, s, ago=2):
                w(pe, S["lhs"], t + 1 - ago)
                turn(S, t, s, [P] * KD)

            def multiply0(t, s):
                pe.wait_ge(S["lhs"], t + 1)
                for c in range(4):
                    w(pe, S["out"], (t - 1) * 4 + c + 1)
                    for k in range(KD):
                        mm = pe.matmul(ps_o[c][:, :], tile_T[:, s, k * P:(k + 1) * P], w0[:, k, c * HID:(c + 1) * HID],
                                       start=k == 0, stop=k == KD - 1)
                    mm.then_inc(S["mm"], 1)
                w(pe, S["kept"], t)
                for k in range(KD):
                    pe.matmul(ps_o[4][:, 0:D], tile_T[:, s, k * P:(k + 1) * P], loopw[:, k, :], start=k == 0, stop=False)
                pe.matmul(ps_o[4][:, 0:D], ident[:, :], x[:, t, :], start=False, stop=True).then_inc(S["mm"], 1)

            def first_tiles(t):
                count(t * 2, 0, isinstance(t, int))
                turn0(t, 0, 1)
                count(t * 2 + 1, 1, False)
                if isinstance(t, int):
                    pe.wait_ge(ld["loopw"], 1)
                multiply0(t, 0)
            loop(pe, UN, first_tiles)
            turn0(UN, 1)
            pe.wait_ge(pr["sums"], 1)
            pe.matmul(ps_m[0:T, 0:2], upper, tot, start=True, stop=True).then_inc(pr["carry"], 1)
            pe.wait_ge(pr["key"], 1)
            for a, row in enumerate((0, 3, 4)):
                mm = pe.transpose(ps_m[:, P + a * 32:P + a * 32 + T], hist[:, row, :], ident[0:T, 0:T])
            mm.then_inc(pr["turned"], 1)
            def pair(k):
                for u in range(2):
                    t = k * 2 + u + UN
                    if not (isinstance(k, int) and k == (T - UN) // 2 - 1 and u):
                        turn0(t + 1, u)
                    multiply0(t, 1 - u)
            loop(pe, (T - UN) // 2, pair, tail=1)
            pe.wait_ge(S["out"], 4 * T)
            pe.wait_ge(S["kept"], T)

            def count_src(i):
                count(HS + i, 0, isinstance(i, int))
            loop(pe, HS, count_src)
            pe.wait_ge(pr["out_counts"], 1)

            turned, out_n, bcol = 0, 0, 0
            pe.wait_ge(fo["right"], 16)
            for n, (v, outs) in enumerate(FOLD):
                rows = v.shape[0]
                pe.wait_ge(fo["left"], 16 * (n + 1))
                for k in range(KH):
                    if turned >= 2:
                        pe.wait_ge(fo["lhs"], turned - 1)
                    for m in range(rows // P):
                        mm = pe.transpose(ps_T[k % 2][:, m * P:(m + 1) * P], f_left[:, m, k * P:(k + 1) * P], ident[:, :])
                    mm.then_inc(fo["turned"], 1)
                    turned += 1
                pe.wait_ge(fo["lhs"], turned)
                for (right, _, _, width) in outs:
                    if out_n:
                        pe.wait_ge(fo["out"], out_n)
                    if right is f_F and n >= 5:
                        pe.wait_ge(fo["right"], 32)
                    for m in range(rows // P):
                        for k in range(KH):
                            mm = pe.matmul(ps_o[m][:, 0:width], f_leftT[:, k, m * P:(m + 1) * P], right[:, k, 0:width],
                                           start=k == 0, stop=k == KH - 1)
                        mm.then_inc(fo["done"], 1)
                        out_n += 1
                if n in FOLD_BIAS:
                    bcol += 2 * KH
                    pe.wait_ge(fo["bcol"], bcol)
                    pe.wait_ge(fo["out"], out_n)

                    def add(a, right, width, first, last=False):
                        for k in range(KH):
                            mm = pe.matmul(ps_m[:, 0:width], f_bias[:, a, k, :], right[:, k, 0:width],
                                           start=first and k == 0, stop=last and k == KH - 1, skip_group_check=True)
                        return mm

                    def add_row(r, width):
                        return pe.matmul(ps_m[:, 0:width], ones_row[:, :], f_row[0:1, r, 0:width],
                                         start=False, stop=True, skip_group_check=True)
                    if n == 1:
                        add(0, f_F, HID, True)
                        add(1, f_wfc, D, False)
                        add_row(0, D).then_inc(fo["done"], 1)
                        out_n += 1
                    else:
                        add(0, f_S, HID, True)
                        add(1, f_M, HID, False, True).then_inc(fo["done"], 1)
                        out_n += 1
                        pe.wait_ge(fo["out"], out_n)
                        pe.wait_ge(fo["right"], 32)
                        add(0, f_F, HID, True)
                        add_row(1, HID).then_inc(fo["done"], 1)
                        out_n += 1

            def pool_and_y():
                S = L["thp"]

                def turn_next(i, u):
                    w(pe, S["lhs"], i * UN + u + 1 - lag(u))
                    turn(S, i * UN + u, u % 2, [P] * KH, 2)

                def multiply(i, u):
                    T_, s = i * UN + u, u % 2
                    pe.wait_ge(S["lhs"], T_ + 1)
                    for bank, weights, row, free in ((2 * s, w_hp, biasB, "out"), (2 * s + 1, w_y, biasC, "kept")):
                        w(pe, S[free], T_ + 1 - lag(u))
                        for k in range(KH):
                            pe.matmul(ps_o[bank][:, :], tile_T[:, s, k * P:(k + 1) * P], weights[:, k, :],
                                      start=k == 0, stop=False)
                        pe.matmul(ps_o[bank][:, :], ones_row[:, :], row[0:1, :], start=False, stop=True).then_inc(S["mm"], 1)
                turn_next(0, 0)
                loop(pe, TI, with_next(multiply, before=turn_next), tail=1)
                pe.wait_ge(S["out"], T)
                pe.wait_ge(S["kept"], T)

            def product(ph, widths, weights, wide, lhs_per=1, n_in=1, row=None, add=None, free="out", ahead=True):
                S = L[ph]

                def turn_next(i, u):
                    w(pe, S["lhs"], (i * UN + u + 1 - lag(u)) * lhs_per)
                    turn(S, i * UN + u, u % 2, widths, n_in)

                def multiply(i, u):
                    T_, s = i * UN + u, u % 2
                    pe.wait_ge(S["lhs"], (T_ + 1) * lhs_per)
                    w(pe, S[free], T_ + 1 - UN)
                    for k, width in enumerate(widths):
                        mm = pe.matmul(ps_o[u][:, 0:wide], tile_T[0:width, s, k * P:(k + 1) * P], weights[0:width, k, :],
                                       start=k == 0, stop=row is None and add is None and k == len(widths) - 1)
                    if row is not None:
                        mm = pe.matmul(ps_o[u][:, 0:wide], ones_row[:, :], row, start=False, stop=True)
                    if add is not None:
                        mm = pe.matmul(ps_o[u][:, 0:wide], ident[:, :], add[:, T_, :], start=False, stop=True)
                    mm.then_inc(S["mm"], 1)

                def own(i, u):
                    turn_next(i, u)
                    multiply(i, u)
                if ahead:
                    turn_next(0, 0)
                    loop(pe, TI, with_next(multiply, before=turn_next), tail=1)
                else:
                    loop(pe, TI, with_next(own))
                pe.wait_ge(S[free], T)

            pe.wait_ge(fo["out"], out_n)
            pool_and_y()
            product("tv", [P] * KH, w_v, HID, add=H, ahead=False)
            pe.wait_ge(ld["l2"], 16)

            def add_to_x(S, i, u):
                T_, s = i * UN + u, u % 2
                pe.wait_ge(S["in"], T_ + 1)
                pe.matmul(ps_o[u][:, 0:D], ident[:, :], tile_in[:, s, 0:D], start=True, stop=False)
                pe.matmul(ps_o[u][:, 0:D], ident[:, :], x[:, T_, :], start=False, stop=True).then_inc(S["added"], 1)

            def tile2(i, u):
                S = L["t2"]
                T_, s = i * UN + u, u % 2
                add_to_x(S, i, u)
                pe.wait_ge(S["centred"], T_ + 1)
                for k in range(KD):
                    mm = pe.transpose(ps_T[s][:, k * P:(k + 1) * P], tile_in[:, s, k * P:(k + 1) * P], ident[:, :])
                mm.then_inc(S["turned"], 1)
                pe.wait_ge(S["lhs"], T_ + 1)
                for k in range(KD):
                    mm = pe.matmul(ps_m[:, 0:D], tile_T[:, s, k * P:(k + 1) * P], wl2[:, k, :], start=k == 0, stop=k == KD - 1)
                mm.then_inc(S["mm"], 1)
            loop(pe, TI, with_next(tile2))
            loop(pe, TI, with_next(lambda i, u: add_to_x(L["t3"], i, u)))
            pe.wait_ge(ld["l3"], 48)
            product("ro", [P] * KD + [DE], wl3, D, lhs_per=2, n_in=2, row=biasC[0:1, 0:D], free="kept", ahead=False)

        @block.vector
        def _(ve):
            ch = Chain(ve, dve_chain)
            marks = (mark[:, k:k + 1] for k in range(MARKS))
            bc = lambda a, n: a.unsqueeze(2).to_broadcast([a.shape[0], a.shape[1], n])
            ve.wait_ge(pr["const"], 8)
            ch(ve.tensor_copy(iota_f[:, :], iota_i[:, :]))
            ch(ve.tensor_copy(part_f[:, :], part_i[:, :]))
            ch(ve.tensor_copy(iota_b, iota_i[:, :]))
            ch(ve.memset(idx[:, 0, :], ZROW))
            ch(ve.memset(idx[:, 1, :], ZROW * R))
            ch(ve.memset(wt[:, :], 0.0))
            ch(ve.memset(round_tile[:, :], T - 1))
            ch(ve.memset(attr_sum[:, :, :], 0.0))
            ve.wait_ge(ld["edges"], 64)
            for a in range(2):
                ch(ve.tensor_scalar(edge_i[:, 4 + 2 * a, :], edge_i[:, a, :], P - 1, None, ALU.bitwise_and))
                ch(ve.tensor_scalar(edge_i[:, 5 + 2 * a, :], edge_i[:, a, :], 7, None, ALU.logical_shift_right))
            ch.sync()
            ch.link(ve.tensor_copy(edge_b, edge_i[:, 4:8, :]))
            e3 = edge3.rearrange("p (c r) -> p c r", r=3)
            e3i = edge3.bitcast(I32).rearrange("p (c r) -> p c r", r=3)
            ve.tensor_copy(e3i[:, :, 0], edge_i[:, 1, :]).then_inc(pr["hot"], 1)
            ve.scalar_tensor_tensor(out=e3i[:, :, 1], in0=edge_i[:, 1, :], scalar=float(R), in1=edge_i[:, 2, :],
                                    op0=ALU.mult, op1=ALU.add).then_inc(pr["hot"], 1)
            ve.tensor_copy(e3[:, :, 2], edge_i[:, 3, :].bitcast(F32)).then_inc(pr["hot"], 1)
            def layer_norm(n):
                def sums(i):
                    for u in range(UN):
                        ch(ve.bn_stats(stats[:, i * UN + u, :], x[:, i * UN + u, :]))
                loop(ve, TI, sums, ch)
                ch.sync()

                for t in range(T):
                    ch(ve.bn_aggr(mv[:, t, :], stats[:, t, :]))
                ch.sync()
                ve.tensor_scalar(std[:, :], mv[:, :, 1], EPS, None, ALU.add).then_inc(ln_var, 1)
                ve.wait_ge(ln_std, n + 1)
                ch.link(ve.reciprocal(rstd[:, :], std[:, :]))
                ve.scalar_tensor_tensor(out=nmr[:, :], in0=mv[:, :, 0], scalar=-1.0, in1=rstd[:, :],
                                        op0=ALU.mult, op1=ALU.mult).then_inc(ln_ready, 1)

            ve.wait_ge(ld["x"], 32)
            layer_norm(0)
            ve.wait_ge(ld["w0"], 16 * (R + 2))
            ve.tensor_scalar(loopw, loopw, HALF, None, ALU.mult).then_inc(ld["loopw"], 1)
            def hot(a, step, s):
                at = bass.ds(step * HC, HC)
                ve.tensor_tensor(lo_hot[:, s, :, :], bc(edge_b[:, 2 * a, at], P),
                                 iota_b[0:EP, :].unsqueeze(1).to_broadcast([EP, HC, P]), ALU.is_equal)\
                    .then_inc(pr["hot"], 1)
                ve.tensor_tensor(hi_hot[:, s, :, :], bc(edge_b[:, 2 * a + 1, at], T),
                                 iota_b[0:EP, 0:T].unsqueeze(1).to_broadcast([EP, HC, T]), ALU.is_equal)\
                    .then_inc(pr["hot"], 1)

            def hot_dst(i):
                for s in range(2):
                    w(ve, pr["hist"], i * 2 + s - 1)
                    hot(0, i * 2 + s, s)
            loop(ve, HS // 2, hot_dst)
            ve.wait_ge(pr["hist"], HS)
            ch.link(ve.tensor_copy(hist[:, 0, :], ps_m[0:T, 0:P]))
            ch(ve.memset(hist[:, 6, :], 1.0))
            ch(ve.memset(tot, 0.0))
            ch.link(ve.tensor_scalar(hist[:, 5, :], hist[:, 0, :], float(TOP_DEG), float(TOP_DEG + 1), ALU.min, ALU.mult))
            ch.link(ve.tensor_tensor_scan(hist[:, 2, :], hist[:, 6, :], hist[:, 0, :], 0.0, ALU.mult, ALU.add))
            ve.tensor_copy(tot[:, 0:1], hist[:, 2, P - 1:P]).then_inc(pr["sums"], 1)
            ch(ve.tensor_scalar(sp_f[0:T, 0:1], part_f[0:T, :], -float(P), float(TOP_DEG), ALU.mult, ALU.add))
            ch.link(ve.tensor_tensor(hist[:, 3, :], hist[:, 2, :], hist[:, 0, :], ALU.subtract))
            ch.link(ve.scalar_tensor_tensor(out=hist[:, 7, :], in0=hist[:, 5, :], scalar=sp_f[0:T, 0:1],
                                            in1=iota_f[0:T, :], op0=ALU.add, op1=ALU.subtract))
            ve.wait_ge(pr["carry"], 1)
            ch.link(ve.tensor_scalar(hist[:, 3, :], hist[:, 3, :], ps_m[0:T, 0:1], None, ALU.add))
            ve.tensor_copy(hist[:, 4, :], hist[:, 7, :]).then_inc(pr["key"], 1)
            ve.wait_ge(pr["turned"], 1)
            for a in range(3):
                ch(ve.tensor_copy(cols[:, a, :], ps_m[:, P + a * 32:P + a * 32 + T]))
            ch.sync()
            ve.wait_ge(ld["keys"], 32)
            for t in range(T):
                ch.link(ve.tensor_scalar(cmp_out, key_row, cols[:, 2, t:t + 1], None, ALU.is_gt, ALU.add,
                                         accum_out=pos_f[:, t:t + 1]))
            ch(ve.tensor_copy(node_rec_s[:, :, 1], cols[:, 0, :]))
            ch(ve.tensor_copy(node_rec_s[:, :, 2], cols[:, 1, :]))
            ch(ve.tensor_scalar(node_rec_s[:, :, 0], iota_f[:, 0:T], float(P), part_f[:, :], ALU.mult, ALU.add))
            ch.sync()
            ve.tensor_copy(pos_i, pos_f).then_inc(pr["pos"], 1)

            ve.wait_ge(ld["nodes"], 48)
            ch(ve.tensor_copy(node_of[:, :], recs[:, :, 0]))
            ch(ve.tensor_copy(degf[:, :], recs[:, :, 1]))
            ch(ve.tensor_copy(startf[:, :], recs[:, :, 2]))
            ch.link(ve.tensor_scalar(win_at[:, :], recs[:, :, 2], 3.0, None, ALU.mult))
            ve.tensor_scalar(attr_atf[:, :], recs[:, :, 2], float(E - CAP), None, ALU.min).then_inc(pr["nodes"], 1)
            ch(ve.memset(small[:, 0, :], 1.0))
            ch(ve.tensor_copy(small[:, 6, :], first_recs[:, :, 1]))
            ch.link(ve.tensor_copy(top_deg[:, :], top_recs[:, :, 1]))
            ch.link(ve.tensor_reduce(small[:, 6, 0:1], top_deg[:, :], mybir.AxisListType.X, ALU.max))
            ch.link(ve.tensor_scalar(small[:, 1, :], small[:, 6, :], float(CAP), None, ALU.min))
            ch.link(ve.tensor_tensor_scan(small[:, 2, :], small[:, 0, :], small[:, 1, :], 0.0, ALU.mult, ALU.add))
            ch.link(ve.tensor_tensor(small[:, 3, :], small[:, 2, :], small[:, 1, :], ALU.subtract))
            ch(ve.tensor_scalar(small_i[:, 0, 0:T], small[:, 3, :], float(ROUNDS), None, ALU.min))
            ch.link(ve.tensor_scalar(caps[:, :], small[:, 3, :], -1.0, float(ROUNDS), ALU.mult, ALU.add))
            ch.link(ve.tensor_scalar(caps[:, :], caps[:, :], 0.0, float(CAP), ALU.max, ALU.min))
            ch.link(ve.tensor_tensor(small[:, 7, :], small[:, 6, :], caps[:, :], ALU.subtract))
            ch.link(ve.tensor_scalar(small_i[:, 3, 0:T], small[:, 7, :], 0.0, float(SPW - 1), ALU.max, ALU.add))
            ch.link(ve.tensor_scalar(small_i[:, 1, 0:T], small_i[:, 3, 0:T], 5, None, ALU.logical_shift_right))
            ch.link(ve.tensor_copy(small[:, 4, :], small_i[:, 1, 0:T]))
            ch.link(ve.tensor_tensor_scan(small[:, 5, :], small[:, 0, :], small[:, 4, :], 0.0, ALU.mult, ALU.add))
            ch(ve.tensor_tensor(small_i[:, 2, 0:T], small[:, 5, :], small[:, 4, :], ALU.subtract))
            ch.link(ve.tensor_copy(small_i[:, 3, 0:1], small[:, 5, T - 1:T]))
            ch(ve.tensor_copy(sp_tile[:, :], iota_f[:, 0:T]))
            ch.link(ve.tensor_scalar(ends[:, :], small[0:1, 2, :], float(ROUNDS), None, ALU.min))
            ch.link(ve.memset(ends[:, T - 1:T], ROUNDS))

            def flatten(i):
                ve.wait_ge(win_in[i], 16 * UN)
                some = bass.ds(i * UN, UN)
                rec = win[:, some, :].rearrange("p t (j c) -> p t j c", c=3)
                ch.link(ve.tensor_tensor(flat_in, iota_f[:, 0:CAP].unsqueeze(1).to_broadcast([P, UN, CAP]),
                                         bc(degf[:, some], CAP), ALU.is_lt))
                ch(ve.scalar_tensor_tensor(out=flat_row, in0=rec[:, :, :, 0], scalar=-float(ZROW),
                                           in1=flat_in, op0=ALU.add, op1=ALU.mult))
                ch(ve.scalar_tensor_tensor(out=flat_row0, in0=rec[:, :, :, 1], scalar=-float(ZROW * R),
                                           in1=flat_in, op0=ALU.add, op1=ALU.mult))
                ch.sync()
                apart(ve)
                for u in range(UN):
                    t = i * UN + u
                    off = ve.value_load(small_i[0:1, 0, bass.ds(t, 1)], min_val=0, max_val=ROUNDS)
                    at = bass.ds(off, CAP)
                    weight = win[:, t, :].bitcast(F32).rearrange("p (j c) -> p j c", c=3)[:, :, 2]
                    ch(ve.tensor_tensor(wt[:, at], weight, flat_in[:, u, :], ALU.mult))
                    ch(ve.tensor_scalar(idx[:, 0, at], flat_row[:, u, :], float(ZROW), None, ALU.add))
                    ch(ve.tensor_scalar(idx[:, 1, at], flat_row0[:, u, :], float(ZROW * R), None, ALU.add))
                    ch(ve.tensor_copy(round_tile[0:1, at], sp_tile[0:1, bass.ds(t, 1)].to_broadcast([1, CAP])))
                    ch.sync()
                    apart(ve)
                ve.memset(mask[:, 1, :], 0.0).then_inc(pr["flat"], 1)
            for i in range(TI):
                flatten(i)

            ve.memset(next(marks), 0.0).then_inc(spb["dve"], 1)
            q_total = ve.value_load(small_i[0:1, 3, 0:1], min_val=0, max_val=SPILLS)
            with ve.If(q_total):
                with ve.Fori(0, T) as t:
                    run = Chain(ve, spb["run"])
                    run.base = t * 2
                    run(ve.tensor_scalar(sp_run[:, 0:1], startf[:, bass.ds(t, 1)], caps[:, bass.ds(t, 1)], None, ALU.add))
                    run.link(ve.tensor_scalar(sp_run[:, 1:2], degf[:, bass.ds(t, 1)], caps[:, bass.ds(t, 1)], None, ALU.subtract))
                    apart(ve)
                    n = ve.value_load(small_i[0:1, 1, bass.ds(t, 1)], min_val=0, max_val=SPILLS)
                    first = ve.value_load(small_i[0:1, 2, bass.ds(t, 1)], min_val=0, max_val=SPILLS)
                    with ve.If(n):
                        with ve.Fori(0, n) as j:
                            q = nc.s_assert_within(ve.snap(first + j), 0, SPILLS - 1, skip_runtime_bounds_check_because="the windows counted by this program are below their bound")
                            sc = Chain(ve, spb["dve"])
                            sc.base = q * SPB_PER + 1
                            sc.link(ve.tensor_scalar(sp_f[:, 2:3], sp_run[:, 0:1], float(E), None, ALU.min))
                            sc(ve.tensor_scalar(sp_at[:, :], sp_f[:, 2:3], 3.0, None, ALU.mult))
                            assert sc.n == SPB_AT
                            sc.link(ve.tensor_scalar(sp_m[:, 0, :], iota_f[:, 0:SPW], sp_run[:, 1:2], None, ALU.is_lt))
                            ve.wait_ge(spb["window"], q * 16 + 16)
                            rec = sp_win[:, :].rearrange("p (j c) -> p j c", c=3)
                            recf = sp_win[:, :].bitcast(F32).rearrange("p (j c) -> p j c", c=3)
                            for c, z in ((0, ZROW), (1, ZROW * R)):
                                sc.link(ve.scalar_tensor_tensor(out=sp_m[:, 1, :], in0=rec[:, :, c], scalar=-float(z),
                                                                in1=sp_m[:, 0, :], op0=ALU.add, op1=ALU.mult))
                                sc.link(ve.tensor_scalar(sp_rec[:, c * SPW:(c + 1) * SPW], sp_m[:, 1, :], float(z), None,
                                                         ALU.add))
                            sc(ve.tensor_tensor(sp_rec[:, 2 * SPW:3 * SPW].bitcast(F32), recf[:, :, 2], sp_m[:, 0, :], ALU.mult))
                            sc(ve.tensor_copy(sp_rec[:, 3 * SPW:3 * SPW + 1], sp_tile[:, bass.ds(t, 1)]))
                            sc(ve.tensor_copy(sp_rec[:, 3 * SPW + 1:3 * SPW + 2], sp_f[:, 2:3]))
                            sc.link(ve.tensor_copy(sp_rec[:, 3 * SPW + 2:3 * SPW + 3], sp_run[:, 1:2]))
                            sc(ve.tensor_scalar(sp_run[:, 0:1], sp_run[:, 0:1], float(SPW), None, ALU.add))
                            sc.link(ve.tensor_scalar(sp_run[:, 1:2], sp_run[:, 1:2], -float(SPW), None, ALU.add))
                            assert sc.n == SPB_PER

            ch(ve.tensor_scalar(attr_at[:, :], attr_atf[:, :], float(DE), None, ALU.mult))
            ch.link(ve.tensor_tensor(attr_lo[:, :], startf[:, :], attr_atf[:, :], ALU.subtract))
            ch.link(ve.tensor_tensor(attr_hi[:, :], degf[:, :], caps[:, :], ALU.min))
            ch(ve.tensor_tensor(attr_hi[:, :], attr_hi[:, :], attr_lo[:, :], ALU.add))
            ch(ve.tensor_scalar(normtmp[:, 0, :], degf[:, :], 1.0, None, ALU.max))
            ch(ve.tensor_scalar(rdeg1[:, :], degf[:, :], 1.0, None, ALU.add))
            ch.sync()
            ch(ve.reciprocal(rdeg1[:, :], rdeg1[:, :]))
            ch.link(ve.reciprocal(rdeg[:, :], normtmp[:, 0, :]))

            def tile_turned(S, wide, last=None):
                def step(i, u):
                    T_, s = i * UN + u, u % 2
                    w(ve, S["mm"], T_ + 1 - lag(u))
                    ve.wait_ge(S["turned"], T_ + 1)
                    ve.tensor_copy(tile_T[:, s, 0:wide], ps_T[s][:, 0:wide]).then_inc(S["lhs"], 1)
                    if last:
                        ve.tensor_copy(tile_T[0:last, s, wide:wide + P], ps_T[s][0:last, wide:wide + P]).then_inc(S["lhs"], 1)
                return step

            def rounds(n, wide, kind, beside=None, pairs=False, turns=RI, between=None):
                view = acc256 if wide == D else acc512
                piece = T * wide // GB
                for k in range(GB):
                    ve.memset(acc[:, k * piece:(k + 1) * piece], 0.0).then_inc(acc_done, 1)

                def fold_in(t, row, weight):
                    if kind == "weighted":
                        return ve.scalar_tensor_tensor(out=view[:, t, :], in0=row, scalar=weight, in1=view[:, t, :],
                                                       op0=ALU.mult, op1=ALU.add)
                    return ve.tensor_tensor(view[:, t, :], view[:, t, :], row, ALU.max if kind == "max" else ALU.add)

                def body(i):
                    for h in range(2):
                        first = i * 2 * GB + h * GB
                        _, tiles = nc.values_load_multi_w_load_instructions(
                            round_tile[0:1, bass.ds(first, GB)], engines=[ve.engine], min_val=0, max_val=T - 1,
                            skip_runtime_bounds_check_because="the numbers of tiles, written by this program")
                        for u in range(GB):
                            ve.wait_ge(gather_in[h][u], (n * RI + i + 1) * 16)
                            ve.wait_ge(acc_done, n * PER_PASS + GB + first + u)
                            fold_in(tiles[u], gathered(wide, h, u), wt[:, bass.ds(first + u, 1)]).then_inc(acc_done, 1)

                def body_beside(i):
                    if beside:
                        beside(i)
                    body(i)

                def pair(k):
                    for r in range(2):
                        beside(2 * k + r, k, r)
                        body(2 * k + r)
                if pairs:
                    loop(ve, RI // 2, pair)
                else:
                    loop(ve, turns, body_beside)
                if between:
                    between()
                    loop(ve, RI, body, first=turns, head=0)
                ve.wait_ge(acc_done, (n + 1) * PER_PASS)
                S = SPL[n]
                ve.memset(next(marks), 0.0).then_inc(S["dve"], 1)
                with ve.If(q_total):
                    with ve.Fori(0, q_total) as q:
                        ve.wait_ge(S["load"], q * 16 + 16)
                        apart(ve)
                        t = ve.value_load(sp_rec[0:1, 3 * SPW:3 * SPW + 1], min_val=0, max_val=T - 1)
                        at = SPW if n == 0 else 0
                        with ve.Fori(0, SPW) as j:
                            m = q * SPW + j
                            ve.wait_ge(S["dve"], m * 2 + 1)
                            ve.tensor_copy(sp_idx[:, :], sp_rec[:, bass.ds(j + at, 1)]).then_inc(S["dve"], 1)
                            ve.wait_ge(S["row"], j * 16 + 16)
                            fold_in(t, G[:, 0, 0:wide], sp_rec[:, bass.ds(j + 2 * SPW, 1)].bitcast(F32))\
                                .then_inc(S["dve"], 1)
                            ve.wait_ge(S["dve"], m * 2 + 3)
                ve.memset(next(marks), 0.0).then_inc(whole, 1)

            def hot_src(i):
                ve.wait_ge(pr["hist"], HS + i)
                hot(1, i, 0)

            def bias_and_counts():
                ve.wait_ge(ld["x2"], 16)
                ch.link(ve.tensor_tensor(x[:, :, :], x[:, :, :], biasA[:, 0:D].unsqueeze(1).to_broadcast([P, T, D]), ALU.add))
                ve.wait_ge(pr["hist"], 2 * HS)
                ve.tensor_copy(src_counts, ps_m[0:T, 0:P]).then_inc(pr["out_counts"], 1)
            rounds(0, D, "sum", hot_src, turns=HS, between=bias_and_counts)
            x2 = x[:, :, :].rearrange("p t f -> p (t f)")
            acc2 = acc[:, 0:T * D]
            ch(ve.scalar_tensor_tensor(out=x2, in0=acc2, scalar=HALF, in1=x2, op0=ALU.mult, op1=ALU.add))
            ch.sync()

            def attributes(i, k, slot):
                if isinstance(i, int) and i < 2:
                    return
                st = Chain(ve, ea["step"])
                st.base = (i - 2) * 3
                at = bass.ds(i - 2, 1)
                st.link(ve.tensor_scalar(mask[:, 0, :], iota_f[:, 0:CAP], attr_lo[:, at], None, ALU.is_ge))
                st.link(ve.scalar_tensor_tensor(out=mask[:, 1, :], in0=iota_f[:, 0:CAP], scalar=attr_hi[:, at],
                                                in1=mask[:, 0, :], op0=ALU.is_lt, op1=ALU.mult))
                ve.wait_ge(ea[f"in{slot}"], k * 16)
                av = attr_win[slot].rearrange("p (j f) -> p j f", f=DE)
                st.link(ve.tensor_tensor(av, av, bc(mask[:, 1:2, :].rearrange("p a j -> p (a j)"), DE), ALU.mult))
                ve.tensor_reduce(attr_sum[:, i - 2, :], attr_win[slot].rearrange("p (j f) -> p f j", f=DE),
                                 mybir.AxisListType.X, ALU.add).then_inc(ea["sum"], 1)

            def spill_attributes():
                ve.wait_ge(ea["sum"], T)
                ve.memset(next(marks), 0.0).then_inc(ea["dve"], 1)
                with ve.If(q_total):
                    with ve.Fori(0, q_total) as q:
                        sc = Chain(ve, ea["dve"])
                        sc.base = q * EA_PER + 1
                        ve.wait_ge(ea["load"], q * 16 + 16)
                        apart(ve)
                        t = ve.value_load(sp_rec[0:1, 3 * SPW:3 * SPW + 1], min_val=0, max_val=T - 1)
                        sc.link(ve.tensor_scalar(sp_f[:, 2:3], sp_rec[:, 3 * SPW + 1:3 * SPW + 2], float(E - SPW), None, ALU.min))
                        sc(ve.tensor_scalar(sp_at[:, :], sp_f[:, 2:3], float(DE), None, ALU.mult))
                        assert sc.n == EA_AT
                        sc.link(ve.tensor_tensor(sp_f[:, 3:4], sp_rec[:, 3 * SPW + 1:3 * SPW + 2], sp_f[:, 2:3], ALU.subtract))
                        sc(ve.tensor_tensor(sp_f[:, 0:1], sp_f[:, 3:4], sp_rec[:, 3 * SPW + 2:3 * SPW + 3], ALU.add))
                        sc.link(ve.tensor_scalar(sp_m[:, 0, :], iota_f[:, 0:SPW], sp_f[:, 3:4], None, ALU.is_ge))
                        sc.link(ve.scalar_tensor_tensor(out=sp_m[:, 1, :], in0=iota_f[:, 0:SPW], scalar=sp_f[:, 0:1],
                                                        in1=sp_m[:, 0, :], op0=ALU.is_lt, op1=ALU.mult))
                        ve.wait_ge(ea["window"], q * 16 + 16)
                        av = sp_attr.rearrange("p (j f) -> p j f", f=DE)
                        sc.link(ve.tensor_tensor(av, av, bc(sp_m[:, 1:2, :].rearrange("p a j -> p (a j)"), DE), ALU.mult))
                        sc.link(ve.tensor_reduce(sp_sum[:, :], sp_attr.rearrange("p (j f) -> p f j", f=DE),
                                                 mybir.AxisListType.X, ALU.add))
                        sc.link(ve.tensor_tensor(attr_sum[:, t, :], attr_sum[:, t, :], sp_sum[:, :], ALU.add))
                        assert sc.n == EA_PER

            ve.wait_ge(fo["out"], FOLDED)
            layer_norm(1)
            rounds(1, D, "sum")
            for u in range(UN):
                ve.wait_ge(sent[u], 16 * TI * (SENDERS.index("thp") + 1))
            rounds(2, HID, "max")
            ve.wait_ge(L["tv"]["in"], T)
            ch.link(ve.tensor_tensor(x[:, :, :], x[:, :, :], biasA[:, 0:D].unsqueeze(1).to_broadcast([P, T, D]), ALU.add))
            rounds(3, HID, "sum")
            ve.wait_ge(L["tv"]["out"], T)

            def g_rows(i):
                for u in range(UN):
                    T_ = i * UN + u
                    ch.link(ve.tensor_tensor(H[:, T_, D:2 * D], H[:, T_, D:2 * D], acc512[:, T_, D:2 * D], ALU.add))
                    slot_sent(ve, "tg", i, u)
                    ve.scalar_tensor_tensor(out=G[:, u, 0:D], in0=H[:, T_, D:2 * D], scalar=rdeg1[:, bass.ds(T_, 1)],
                                            in1=biasA[:, D:2 * D], op0=ALU.mult, op1=ALU.add).then_inc(L["tg"]["out"], 1)
            loop(ve, TI, g_rows, ch)
            ch.link(ve.tensor_tensor(H[:, :, 0:D], H[:, :, 0:D], acc512[:, :, 0:D], ALU.add))
            ch.link(ve.tensor_tensor(H[:, :, 0:D], H[:, :, 0:D], bc(rdeg1[:, :], D), ALU.mult))
            ch.link(ve.tensor_tensor(x[:, :, :], x[:, :, :], H[:, :, 0:D], ALU.add))
            rounds(4, D, "sum", attributes, pairs=True)
            attributes(T + 1, (T + 1) // 2, (T + 1) % 2)
            spill_attributes()

            def centred_rows(ph, n):
                S = L[ph]
                ve.wait_ge(S["kept"], T)
                ve.tensor_scalar(std[:, :], squares[:, :], 1.0 / D, EPS, ALU.mult, ALU.add).then_inc(ln_var, 1)
                ve.wait_ge(ln_std, n + 1)
                ch.link(ve.reciprocal(rstd[:, :], std[:, :]))
                if n == 3:
                    ch.link(ve.tensor_tensor(rstd[:, :], rstd[:, :], norm_out[:, :], ALU.mult))

                def rows(i):
                    for u in range(UN):
                        T_ = i * UN + u
                        slot_sent(ve, ph, i, u)
                        ve.tensor_scalar(G[:, u, 0:D], acc256[:, T_, :], rstd[:, bass.ds(T_, 1)], None, ALU.mult).then_inc(S["out"], 1)
                loop(ve, TI, rows)
                ve.wait_ge(S["out"], T)

            centred_rows("t2", 2)
            ve.wait_ge(pr["out_in"], 16 * T)
            ve.tensor_scalar(normtmp[:, 1, :], outdeg[:, :], 1.0, None, ALU.max).then_inc(pr["norm"], 1)
            rounds(5, D, "weighted")
            ve.wait_ge(pr["norm"], 2)
            ve.reciprocal(norm_in[:, :], normtmp[:, 0, :]).then_inc(pr["norm_in"], 1)
            ch(ve.reciprocal(norm_out[:, :], normtmp[:, 1, :]))

            centred_rows("t3", 3)
            rounds(6, D, "sum")
            for t in range(T):
                ve.wait_ge(L["ro"]["kept"], t + 1)
                ve.tensor_tensor(acc256[:, t, :], acc256[:, t, :], x[:, t, :], ALU.add).then_inc(L["ro"]["out"], 1)


_INS = ['x', 'src', 'dst', 'edge_attr_64', 'edge_type_8', 'edge_weight',
        'L0_gnn_weight', 'L0_gnn_h_bias', 'L0_gnn_loop_weight',
        'L1_gnn_W1_self', 'L1_gnn_W1_neigh', 'L1_gnn_b1', 'L1_gnn_W2_pool', 'L1_gnn_b2_pool',
        'L1_gnn_W2_self', 'L1_gnn_W2_neigh', 'L1_gnn_b2', 'L1_gnn_W3_neigh', 'L1_gnn_b3',
        'L1_gnn_W4_self', 'L1_gnn_W4_neigh', 'L1_gnn_b4', 'L1_gnn_W_fc', 'L1_gnn_b_fc',
        'L2_gnn_weight', 'L3_gnn_weight', 'L3_gnn_bias']


def kernel(**inputs):
    import concourse.bacc as _bacc
    from concourse import mybir as _mybir
    from concourse.bass_utils import run_bass_kernel_spmd as _run

    nc = _bacc.Bacc("TRN2", target_bir_lowering=False, num_devices=1)
    arrays, args = {}, []
    for name in _INS:
        a = np.ascontiguousarray(inputs[name])
        arrays[f"in_{name}_dram"] = a
        args.append(nc.dram_tensor(f"in_{name}_dram", a.shape, _mybir.dt.from_np(a.dtype), kind="ExternalInput").ap())
    args.append(nc.dram_tensor("out_0_dram", arrays["in_x_dram"].shape, F32, kind="ExternalOutput").ap())
    build_gnn(nc, *args)
    r = _run(nc, [arrays], core_ids=[0])
    return r.results[0]["out_0_dram"]
```
